# Optimizing a Trainium2 kernel written in Bass

```python
import numpy as np
import jax
import jax.numpy as jnp

def _softmax(x, axis=-1):
    return jax.nn.softmax(x, axis=axis)

def _gelu(x):
    return jax.nn.gelu(x, approximate=True)

def _silu(x):
    return jax.nn.silu(x)

def _sigmoid(x):
    return jax.nn.sigmoid(x)

def _layernorm(x, axis=-1, eps=1e-05):
    m = jnp.mean(x, axis=axis, keepdims=True)
    v = jnp.var(x, axis=axis, keepdims=True)
    return (x - m) / jnp.sqrt(v + eps)

def _scatter_add(tgt, idx, src, axis=0):
    return tgt.at[idx].add(src)

def _segment_sum(src, seg, n):
    return jax.ops.segment_sum(src, seg, n)
kernel_name = 'mk_decoder_preln_d4_seqx_r4_caf836'

def setup_inputs(seed: int=0):
    np.random.seed(seed)
    _w = jnp.asarray

    def _rec_inputs():
        import jax
        import jax.numpy as jnp
        _rk = jax.random.key(seed)
        x = -0.0002928 + 1 * jax.random.normal(jax.random.fold_in(_rk, 1), (8, 256, 256), jnp.float32)
        _lenS = 256 - jax.random.randint(jax.random.fold_in(_rk, 7), (8,), 0, max(1, 256 // 4) + 1, jnp.int32)
        _lenS2 = 77 - jax.random.randint(jax.random.fold_in(_rk, 8), (8,), 0, max(1, 77 // 4) + 1, jnp.int32)
        _ctx_1024P = jax.random.normal(jax.random.fold_in(_rk, 11), (8, 16, 256), jnp.float32)
        _ctx_1024c = jax.random.dirichlet(jax.random.fold_in(_rk, 511), 0.3 * jnp.ones((16,), jnp.float32), (8, 77))
        _ctx_1024t = jnp.einsum('bsk,bkd->bsd', _ctx_1024c, _ctx_1024P)
        _ctx_1024t = _ctx_1024t * jax.lax.rsqrt(jnp.mean(jnp.square(_ctx_1024t)) + 1e-12) * 0.953939
        ctx_1024 = 2.81802e-05 + 1.00001 * (_ctx_1024t + 0.3 * jax.random.normal(jax.random.fold_in(_rk, 611), (8, 77, 256), jnp.float32))
        _validS = jnp.arange(256)[None, :] < _lenS[:, None]
        _validS2 = jnp.arange(77)[None, :] < _lenS2[:, None]
        _causal = jnp.tril(jnp.ones((256, 256), dtype=bool))
        mask_1x1xSxS2_if1 = jnp.where(jnp.ones((1, 1, 256, 77), dtype=bool), 1, 0).astype(jnp.int32)
        return (x, ctx_1024, mask_1x1xSxS2_if1)
    x, ctx_1024, mask_1x1xSxS2_if1 = _rec_inputs()

    def _L0_attn_setup():
        import jax, jax.numpy as jnp
        import numpy as np
        N_HEAD = 16
        key = jax.random.key(seed)
        ks = jax.random.split(key, 5)
        B, T, C = (4, 256, 256)
        d = C // N_HEAD
        x = jax.random.normal(ks[0], (B, T, C), dtype=jnp.float32)
        w_attn = jax.random.normal(ks[1], (C, 3 * C), dtype=jnp.float32) * 0.02
        w_proj = jax.random.normal(ks[2], (C, C), dtype=jnp.float32) * 0.02
        embk = 0.02 * jax.random.normal(ks[3], (T, d), dtype=jnp.float32)
        embv = 0.02 * jax.random.normal(ks[4], (T, d), dtype=jnp.float32)
        return {'x': x, 'w_attn': w_attn, 'w_proj': w_proj, 'embk': embk, 'embv': embv}
    _L0_attn_all = _L0_attn_setup()
    _L0_attn_in = {k: v for k, v in _L0_attn_all.items() if k in ('w_attn', 'w_proj', 'embk', 'embv')}
    del _L0_attn_all

    def _L0_xattn_setup():
        import jax, jax.numpy as jnp
        import numpy as np
        D_MODEL = 256
        N_HEADS = 16
        HEAD_DIM = D_MODEL // N_HEADS
        key = jax.random.key(seed)
        k1, k2, k3, k4, k5, k6 = jax.random.split(key, 6)
        B, T_q, T_kv = (4, 256, 1024)
        s = 1.0 / np.sqrt(D_MODEL)
        return {'query': jax.random.normal(k1, (B, T_q, D_MODEL), dtype=jnp.float32), 'kv_source': jax.random.normal(k2, (B, T_kv, D_MODEL), dtype=jnp.float32), 'w_q': jax.random.normal(k3, (D_MODEL, D_MODEL), dtype=jnp.float32) * s, 'w_k': jax.random.normal(k4, (D_MODEL, D_MODEL), dtype=jnp.float32) * s, 'w_v': jax.random.normal(k5, (D_MODEL, D_MODEL), dtype=jnp.float32) * s, 'w_o': jax.random.normal(k6, (D_MODEL, D_MODEL), dtype=jnp.float32) * s}
    _L0_xattn_all = _L0_xattn_setup()
    _L0_xattn_in = {k: v for k, v in _L0_xattn_all.items() if k in ('w_q', 'w_k', 'w_v', 'w_o')}
    del _L0_xattn_all

    def _L0_ffn_setup():
        import jax, jax.numpy as jnp
        import numpy as np
        THRESHOLD = 0.1
        key = jax.random.key(seed)
        k1, k2, k3 = jax.random.split(key, 3)
        B, S, D, E = (4, 1024, 256, 8)
        inputs = jax.random.normal(k1, (B, S, D), dtype=jnp.float32)
        gate_w = jax.random.normal(k2, (D, E), dtype=jnp.float32) * 0.02
        gate_b = jnp.zeros((E,), dtype=jnp.float32)
        expert_w = jax.random.normal(k3, (E, D, D), dtype=jnp.float32) * 0.02
        expert_b = jnp.zeros((E, D), dtype=jnp.float32)
        return {'inputs': inputs, 'gate_w': gate_w, 'gate_b': gate_b, 'expert_w': expert_w, 'expert_b': expert_b}
    _L0_ffn_all = _L0_ffn_setup()
    _L0_ffn_in = {k: v for k, v in _L0_ffn_all.items() if k in ('gate_w', 'gate_b', 'expert_w', 'expert_b')}
    del _L0_ffn_all

    def _L1_attn_setup():
        import jax, jax.numpy as jnp
        import numpy as np
        B, L, E, H = (8, 512, 256, 16)
        D = E // H
        EPS = 1e-06
        key = jax.random.key(seed)
        ks = jax.random.split(key, 9)
        s = 1.0 / np.sqrt(E)

        def lin_w(k):
            return jax.random.uniform(k, (E, E), jnp.float32, -s, s)

        def lin_b(k):
            return jax.random.uniform(k, (E,), jnp.float32, -s, s)
        return {'query': jax.random.normal(ks[0], (B, L, E), jnp.float32), 'Wq': lin_w(ks[1]), 'bq': lin_b(ks[2]), 'Wk': lin_w(ks[3]), 'bk': lin_b(ks[4]), 'Wv': lin_w(ks[5]), 'bv': lin_b(ks[6]), 'Wo': lin_w(ks[7]), 'bo': lin_b(ks[8])}
    _L1_attn_all = _L1_attn_setup()
    _L1_attn_in = {k: v for k, v in _L1_attn_all.items() if k in ('Wq', 'bq', 'Wk', 'bk', 'Wv', 'bv', 'Wo', 'bo')}
    del _L1_attn_all

    def _L1_xattn_setup():
        import jax, jax.numpy as jnp
        import numpy as np
        D_MODEL = 256
        HEADS = 16
        D_K = D_MODEL // HEADS
        B, S = (2, 512)
        NEG = -1000000000.0
        key = jax.random.key(seed)
        ks = jax.random.split(key, 7)
        Query = jax.random.normal(ks[0], (B, S, D_MODEL), dtype=jnp.float32)
        Key = jax.random.normal(ks[1], (B, S, D_MODEL), dtype=jnp.float32)
        Value = jax.random.normal(ks[2], (B, S, D_MODEL), dtype=jnp.float32)
        mask = jnp.ones((1, 1, S, S), dtype=jnp.int32)
        sc = 1.0 / np.sqrt(D_MODEL)
        W_q = jax.random.normal(ks[3], (D_MODEL, D_MODEL), dtype=jnp.float32) * sc
        W_k = jax.random.normal(ks[4], (D_MODEL, D_MODEL), dtype=jnp.float32) * sc
        W_v = jax.random.normal(ks[5], (D_MODEL, D_MODEL), dtype=jnp.float32) * sc
        W_o = jax.random.normal(ks[6], (D_MODEL, D_MODEL), dtype=jnp.float32) * sc
        return {'Query': Query, 'Key': Key, 'Value': Value, 'mask': mask, 'W_q': W_q, 'W_k': W_k, 'W_v': W_v, 'W_o': W_o}
    _L1_xattn_all = _L1_xattn_setup()
    _L1_xattn_in = {k: v for k, v in _L1_xattn_all.items() if k in ('W_q', 'W_k', 'W_v', 'W_o')}
    del _L1_xattn_all

    def _L1_ffn_setup():
        import jax, jax.numpy as jnp
        import numpy as np
        D_MODEL = 256
        HIDDEN = 512
        MOE_DIM = 64
        N_EXPERTS = 8
        TOP_K = 2
        EXP_HIDDEN = HIDDEN // 2
        B, S = (4, 512)
        key = jax.random.key(seed)
        ks = jax.random.split(key, 20)

        def w(k, shape, fan_in):
            return (jax.random.normal(k, shape, dtype=jnp.float32) / np.sqrt(fan_in)).astype(jnp.float32)
        return {'inputs_embeds': jax.random.normal(ks[0], (B, S, D_MODEL), dtype=jnp.float32), 'enc_w': w(ks[1], (D_MODEL, HIDDEN), D_MODEL), 'enc_b': jnp.zeros((HIDDEN,), jnp.float32), 's2c_w': w(ks[2], (HIDDEN, MOE_DIM), HIDDEN), 's2c_b': jnp.zeros((MOE_DIM,), jnp.float32), 'r_w1': w(ks[3], (MOE_DIM, 64), MOE_DIM), 'r_b1': jnp.zeros((64,), jnp.float32), 'r_w2': w(ks[4], (64, N_EXPERTS), 64), 'r_b2': jnp.zeros((N_EXPERTS,), jnp.float32), 'e_w1': w(ks[5], (N_EXPERTS, MOE_DIM, EXP_HIDDEN), MOE_DIM), 'e_b1': jnp.zeros((N_EXPERTS, EXP_HIDDEN), jnp.float32), 'e_w2': w(ks[6], (N_EXPERTS, EXP_HIDDEN, MOE_DIM), EXP_HIDDEN), 'e_b2': jnp.zeros((N_EXPERTS, MOE_DIM), jnp.float32), 'c2s_w': w(ks[7], (MOE_DIM, HIDDEN), MOE_DIM), 'c2s_b': jnp.zeros((HIDDEN,), jnp.float32), 'dec_w': w(ks[8], (HIDDEN, D_MODEL), HIDDEN), 'dec_b': jnp.zeros((D_MODEL,), jnp.float32), 'ln_g': jnp.ones((D_MODEL,), jnp.float32), 'ln_b': jnp.zeros((D_MODEL,), jnp.float32)}
    _L1_ffn_all = _L1_ffn_setup()
    _L1_ffn_in = {k: v for k, v in _L1_ffn_all.items() if k in ('enc_w', 'enc_b', 's2c_w', 's2c_b', 'r_w1', 'r_b1', 'r_w2', 'r_b2', 'e_w1', 'e_b1', 'e_w2', 'e_b2', 'c2s_w', 'c2s_b', 'dec_w', 'dec_b', 'ln_g', 'ln_b')}
    del _L1_ffn_all

    def _L2_attn_setup():
        import jax, jax.numpy as jnp
        import numpy as np
        B, T, D_IN, D_PROJ, D_OUT, MEM = (8, 512, 256, 256, 256, 40)

        def _fsmn_memory(p, memory_weights):
            M = memory_weights.shape[0] - 1
            b, t, d = p.shape
            rhs = memory_weights[1:][::-1].T[:, None, :]
            lhs = jnp.pad(p.transpose(0, 2, 1), ((0, 0), (0, 0), (M - 1, 0)))
            band = jax.lax.conv_general_dilated(lhs, rhs, window_strides=(1,), padding='VALID', feature_group_count=d, dimension_numbers=('NCH', 'OIH', 'NCH')).transpose(0, 2, 1)
            cs = jnp.cumsum(p, axis=1)
            band_sum = cs - jnp.pad(cs, ((0, 0), (M, 0), (0, 0)))[:, :t]
            total = cs[:, -1:]
            return band + memory_weights[0] * (total - band_sum)
        key = jax.random.key(seed)
        k1, k2, k3, k4 = jax.random.split(key, 4)
        x = jax.random.normal(k1, (B, T, D_IN), dtype=jnp.float32)
        lim1 = np.sqrt(6.0 / (D_IN + D_PROJ))
        lim2 = np.sqrt(6.0 / (D_PROJ + D_OUT))
        limm = np.sqrt(6.0 / (MEM + 1 + D_PROJ))
        W1 = jax.random.uniform(k2, (D_IN, D_PROJ), minval=-lim1, maxval=lim1, dtype=jnp.float32)
        W2 = jax.random.uniform(k3, (D_PROJ, D_OUT), minval=-lim2, maxval=lim2, dtype=jnp.float32)
        mw = jax.random.uniform(k4, (MEM + 1, D_PROJ), minval=-limm, maxval=limm, dtype=jnp.float32)
        mw = mw.at[0].set(0.0)
        bias1 = jnp.ones((D_PROJ,), dtype=jnp.float32)
        bias2 = jnp.ones((D_OUT,), dtype=jnp.float32)
        return {'input_data': x, 'W1': W1, 'bias1': bias1, 'W2': W2, 'bias2': bias2, 'memory_weights': mw}
    _L2_attn_all = _L2_attn_setup()
    _L2_attn_in = {k: v for k, v in _L2_attn_all.items() if k in ('W1', 'bias1', 'W2', 'bias2', 'memory_weights')}
    del _L2_attn_all

    def _L2_xattn_setup():
        import jax, jax.numpy as jnp
        import numpy as np
        N_HEADS = 16
        EMBED_DIM = 256
        HEAD_DIM = EMBED_DIM // N_HEADS
        B, T_TGT, T_SRC = (2, 512, 512)
        key = jax.random.key(seed)
        ks = jax.random.split(key, 8)
        s = 1.0 / np.sqrt(EMBED_DIM)
        return {'x_1': jax.random.normal(ks[0], (B, T_TGT, EMBED_DIM), dtype=jnp.float32), 'x_2': jax.random.normal(ks[1], (B, T_SRC, EMBED_DIM), dtype=jnp.float32), 'Wq': jax.random.uniform(ks[2], (EMBED_DIM, EMBED_DIM), jnp.float32, -s, s), 'bq': jax.random.uniform(ks[3], (EMBED_DIM,), jnp.float32, -s, s), 'Wk': jax.random.uniform(ks[4], (EMBED_DIM, EMBED_DIM), jnp.float32, -s, s), 'bk': jax.random.uniform(ks[5], (EMBED_DIM,), jnp.float32, -s, s), 'Wv': jax.random.uniform(ks[6], (EMBED_DIM, EMBED_DIM), jnp.float32, -s, s), 'bv': jax.random.uniform(ks[7], (EMBED_DIM,), jnp.float32, -s, s)}
    _L2_xattn_all = _L2_xattn_setup()
    _L2_xattn_in = {k: v for k, v in _L2_xattn_all.items() if k in ('Wq', 'bq', 'Wk', 'bk', 'Wv', 'bv')}
    del _L2_xattn_all

    def _L2_ffn_setup():
        import jax, jax.numpy as jnp
        import numpy as np
        TOP_K = 2
        NUM_EXPERTS = 8
        DIM = 256
        HIDDEN = 704
        BS, SLEN = (2, 256)

        def _grouped_ffn(x, w1, w2, w3, counts):
            num_experts = w1.shape[0]
            ends = jnp.cumsum(counts)
            starts = ends - counts
            t = jnp.arange(x.shape[0])
            out = jnp.zeros((x.shape[0], w2.shape[-1]), x.dtype)
            for e in range(num_experts):
                m = ((t >= starts[e]) & (t < ends[e])).astype(x.dtype)[:, None]
                xe = x * m
                h = jax.nn.silu(xe @ w1[e]) * (xe @ w3[e])
                out = out + h @ w2[e] * m
            return out
        key = jax.random.key(seed)
        k = jax.random.split(key, 5)
        std = 0.02
        return {'x': jax.random.normal(k[0], (BS, SLEN, DIM), jnp.float32), 'gate_w': jax.random.normal(k[1], (NUM_EXPERTS, DIM), jnp.float32) * std, 'expert_bias': jnp.zeros((NUM_EXPERTS,), jnp.float32), 'w1': jax.random.normal(k[2], (NUM_EXPERTS, DIM, HIDDEN), jnp.float32) * std, 'w2': jax.random.normal(k[3], (NUM_EXPERTS, HIDDEN, DIM), jnp.float32) * std, 'w3': jax.random.normal(k[4], (NUM_EXPERTS, DIM, HIDDEN), jnp.float32) * std}
    _L2_ffn_all = _L2_ffn_setup()
    _L2_ffn_in = {k: v for k, v in _L2_ffn_all.items() if k in ('gate_w', 'expert_bias', 'w1', 'w2', 'w3')}
    del _L2_ffn_all

    def _L3_attn_setup():
        import math
        import jax, jax.numpy as jnp
        import numpy as np
        B, T, D, H = (2, 512, 256, 16)
        N_LAYERS = 24

        def get_slopes(n):

            def pow2(n):
                start = 2 ** (-2 ** (-(math.log2(n) - 3)))
                return [start * start ** i for i in range(n)]
            if math.log2(n).is_integer():
                return pow2(n)
            c = 2 ** math.floor(math.log2(n))
            return pow2(c) + get_slopes(2 * c)[0::2][:n - c]
        key = jax.random.key(seed)
        ks = jax.random.split(key, 5)
        x = jax.random.normal(ks[0], (B, T, D), dtype=jnp.float32)
        Wq = 0.02 * jax.random.normal(ks[1], (D, D), dtype=jnp.float32)
        Wk = 0.02 * jax.random.normal(ks[2], (D, D), dtype=jnp.float32)
        Wv = 0.02 * jax.random.normal(ks[3], (D, D), dtype=jnp.float32)
        Wo = 0.02 / math.sqrt(2 * N_LAYERS) * jax.random.normal(ks[4], (D, D), dtype=jnp.float32)
        z = jnp.zeros((D,), dtype=jnp.float32)
        return {'x': x, 'Wq': Wq, 'bq': z, 'Wk': Wk, 'bk': z, 'Wv': Wv, 'bv': z, 'Wo': Wo, 'bo': z}
    _L3_attn_all = _L3_attn_setup()
    _L3_attn_in = {k: v for k, v in _L3_attn_all.items() if k in ('Wq', 'bq', 'Wk', 'bk', 'Wv', 'bv', 'Wo', 'bo')}
    del _L3_attn_all

    def _L3_xattn_setup():
        import jax, jax.numpy as jnp
        import numpy as np
        D_MODEL = 256
        N_HEADS = 16
        HEAD_DIM = D_MODEL // N_HEADS
        key = jax.random.key(seed)
        ks = jax.random.split(key, 10)
        B, NQ, S = (8, 64, 1024)
        inv = 1.0 / np.sqrt(D_MODEL)
        inp = {'queries': jax.random.normal(ks[0], (B, NQ, D_MODEL), dtype=jnp.float32), 'context': jax.random.normal(ks[1], (B, S, D_MODEL), dtype=jnp.float32), 'wq': jax.random.normal(ks[2], (D_MODEL, D_MODEL), dtype=jnp.float32) * inv, 'bq': jnp.zeros((D_MODEL,), dtype=jnp.float32), 'wk': jax.random.normal(ks[3], (D_MODEL, D_MODEL), dtype=jnp.float32) * inv, 'bk': jnp.zeros((D_MODEL,), dtype=jnp.float32), 'wv': jax.random.normal(ks[4], (D_MODEL, D_MODEL), dtype=jnp.float32) * inv, 'bv': jnp.zeros((D_MODEL,), dtype=jnp.float32), 'wo': jax.random.normal(ks[5], (D_MODEL, D_MODEL), dtype=jnp.float32) * inv, 'bo': jnp.zeros((D_MODEL,), dtype=jnp.float32)}
        return inp
    _L3_xattn_all = _L3_xattn_setup()
    _L3_xattn_in = {k: v for k, v in _L3_xattn_all.items() if k in ('wq', 'bq', 'wk', 'bk', 'wv', 'bv', 'wo', 'bo')}
    del _L3_xattn_all

    def _L3_ffn_setup():
        import jax, jax.numpy as jnp
        import numpy as np
        B, S, D = (2, 512, 256)
        E, K, DFF = (8, 2, 4 * 256)
        EPS_GATE = 1e-08
        EPS_LN = 1e-05
        key = jax.random.key(seed)
        ks = jax.random.split(key, 4)
        scaled = lambda k, shape, fan: jax.random.normal(k, shape, jnp.float32) / np.sqrt(fan).astype(np.float32)
        return {'x': jax.random.normal(ks[0], (B, S, D), jnp.float32), 'Wg': scaled(ks[1], (D, E), D), 'bg': jnp.zeros((E,), jnp.float32), 'W1': scaled(ks[2], (E, D, DFF), D), 'b1': jnp.zeros((E, DFF), jnp.float32), 'W2': scaled(ks[3], (E, DFF, D), DFF), 'b2': jnp.zeros((E, D), jnp.float32), 'gamma': jnp.ones((D,), jnp.float32), 'beta': jnp.zeros((D,), jnp.float32)}
    _L3_ffn_all = _L3_ffn_setup()
    _L3_ffn_in = {k: v for k, v in _L3_ffn_all.items() if k in ('Wg', 'bg', 'W1', 'b1', 'W2', 'b2', 'gamma', 'beta')}
    del _L3_ffn_all
    return {'x': x, 'ctx_1024': ctx_1024, 'mask_1x1xSxS2_if1': mask_1x1xSxS2_if1, 'L0_attn_w_attn': _L0_attn_in['w_attn'], 'L0_attn_w_proj': _L0_attn_in['w_proj'], 'L0_attn_embk': _L0_attn_in['embk'], 'L0_attn_embv': _L0_attn_in['embv'], 'L0_xattn_w_q': _L0_xattn_in['w_q'], 'L0_xattn_w_k': _L0_xattn_in['w_k'], 'L0_xattn_w_v': _L0_xattn_in['w_v'], 'L0_xattn_w_o': _L0_xattn_in['w_o'], 'L0_ffn_gate_w': _L0_ffn_in['gate_w'], 'L0_ffn_gate_b': _L0_ffn_in['gate_b'], 'L0_ffn_expert_w': _L0_ffn_in['expert_w'], 'L0_ffn_expert_b': _L0_ffn_in['expert_b'], 'L1_attn_Wq': _L1_attn_in['Wq'], 'L1_attn_bq': _L1_attn_in['bq'], 'L1_attn_Wk': _L1_attn_in['Wk'], 'L1_attn_bk': _L1_attn_in['bk'], 'L1_attn_Wv': _L1_attn_in['Wv'], 'L1_attn_bv': _L1_attn_in['bv'], 'L1_attn_Wo': _L1_attn_in['Wo'], 'L1_attn_bo': _L1_attn_in['bo'], 'L1_xattn_W_q': _L1_xattn_in['W_q'], 'L1_xattn_W_k': _L1_xattn_in['W_k'], 'L1_xattn_W_v': _L1_xattn_in['W_v'], 'L1_xattn_W_o': _L1_xattn_in['W_o'], 'L1_ffn_enc_w': _L1_ffn_in['enc_w'], 'L1_ffn_enc_b': _L1_ffn_in['enc_b'], 'L1_ffn_s2c_w': _L1_ffn_in['s2c_w'], 'L1_ffn_s2c_b': _L1_ffn_in['s2c_b'], 'L1_ffn_r_w1': _L1_ffn_in['r_w1'], 'L1_ffn_r_b1': _L1_ffn_in['r_b1'], 'L1_ffn_r_w2': _L1_ffn_in['r_w2'], 'L1_ffn_r_b2': _L1_ffn_in['r_b2'], 'L1_ffn_e_w1': _L1_ffn_in['e_w1'], 'L1_ffn_e_b1': _L1_ffn_in['e_b1'], 'L1_ffn_e_w2': _L1_ffn_in['e_w2'], 'L1_ffn_e_b2': _L1_ffn_in['e_b2'], 'L1_ffn_c2s_w': _L1_ffn_in['c2s_w'], 'L1_ffn_c2s_b': _L1_ffn_in['c2s_b'], 'L1_ffn_dec_w': _L1_ffn_in['dec_w'], 'L1_ffn_dec_b': _L1_ffn_in['dec_b'], 'L1_ffn_ln_g': _L1_ffn_in['ln_g'], 'L1_ffn_ln_b': _L1_ffn_in['ln_b'], 'L2_attn_W1': _L2_attn_in['W1'], 'L2_attn_bias1': _L2_attn_in['bias1'], 'L2_attn_W2': _L2_attn_in['W2'], 'L2_attn_bias2': _L2_attn_in['bias2'], 'L2_attn_memory_weights': _L2_attn_in['memory_weights'], 'L2_xattn_Wq': _L2_xattn_in['Wq'], 'L2_xattn_bq': _L2_xattn_in['bq'], 'L2_xattn_Wk': _L2_xattn_in['Wk'], 'L2_xattn_bk': _L2_xattn_in['bk'], 'L2_xattn_Wv': _L2_xattn_in['Wv'], 'L2_xattn_bv': _L2_xattn_in['bv'], 'L2_ffn_gate_w': _L2_ffn_in['gate_w'], 'L2_ffn_expert_bias': _L2_ffn_in['expert_bias'], 'L2_ffn_w1': _L2_ffn_in['w1'], 'L2_ffn_w2': _L2_ffn_in['w2'], 'L2_ffn_w3': _L2_ffn_in['w3'], 'L3_attn_Wq': _L3_attn_in['Wq'], 'L3_attn_bq': _L3_attn_in['bq'], 'L3_attn_Wk': _L3_attn_in['Wk'], 'L3_attn_bk': _L3_attn_in['bk'], 'L3_attn_Wv': _L3_attn_in['Wv'], 'L3_attn_bv': _L3_attn_in['bv'], 'L3_attn_Wo': _L3_attn_in['Wo'], 'L3_attn_bo': _L3_attn_in['bo'], 'L3_xattn_wq': _L3_xattn_in['wq'], 'L3_xattn_bq': _L3_xattn_in['bq'], 'L3_xattn_wk': _L3_xattn_in['wk'], 'L3_xattn_bk': _L3_xattn_in['bk'], 'L3_xattn_wv': _L3_xattn_in['wv'], 'L3_xattn_bv': _L3_xattn_in['bv'], 'L3_xattn_wo': _L3_xattn_in['wo'], 'L3_xattn_bo': _L3_xattn_in['bo'], 'L3_ffn_Wg': _L3_ffn_in['Wg'], 'L3_ffn_bg': _L3_ffn_in['bg'], 'L3_ffn_W1': _L3_ffn_in['W1'], 'L3_ffn_b1': _L3_ffn_in['b1'], 'L3_ffn_W2': _L3_ffn_in['W2'], 'L3_ffn_b2': _L3_ffn_in['b2'], 'L3_ffn_gamma': _L3_ffn_in['gamma'], 'L3_ffn_beta': _L3_ffn_in['beta']}

def reference(x, ctx_1024, mask_1x1xSxS2_if1, L0_attn_w_attn, L0_attn_w_proj, L0_attn_embk, L0_attn_embv, L0_xattn_w_q, L0_xattn_w_k, L0_xattn_w_v, L0_xattn_w_o, L0_ffn_gate_w, L0_ffn_gate_b, L0_ffn_expert_w, L0_ffn_expert_b, L1_attn_Wq, L1_attn_bq, L1_attn_Wk, L1_attn_bk, L1_attn_Wv, L1_attn_bv, L1_attn_Wo, L1_attn_bo, L1_xattn_W_q, L1_xattn_W_k, L1_xattn_W_v, L1_xattn_W_o, L1_ffn_enc_w, L1_ffn_enc_b, L1_ffn_s2c_w, L1_ffn_s2c_b, L1_ffn_r_w1, L1_ffn_r_b1, L1_ffn_r_w2, L1_ffn_r_b2, L1_ffn_e_w1, L1_ffn_e_b1, L1_ffn_e_w2, L1_ffn_e_b2, L1_ffn_c2s_w, L1_ffn_c2s_b, L1_ffn_dec_w, L1_ffn_dec_b, L1_ffn_ln_g, L1_ffn_ln_b, L2_attn_W1, L2_attn_bias1, L2_attn_W2, L2_attn_bias2, L2_attn_memory_weights, L2_xattn_Wq, L2_xattn_bq, L2_xattn_Wk, L2_xattn_bk, L2_xattn_Wv, L2_xattn_bv, L2_ffn_gate_w, L2_ffn_expert_bias, L2_ffn_w1, L2_ffn_w2, L2_ffn_w3, L3_attn_Wq, L3_attn_bq, L3_attn_Wk, L3_attn_bk, L3_attn_Wv, L3_attn_bv, L3_attn_Wo, L3_attn_bo, L3_xattn_wq, L3_xattn_bq, L3_xattn_wk, L3_xattn_bk, L3_xattn_wv, L3_xattn_bv, L3_xattn_wo, L3_xattn_bo, L3_ffn_Wg, L3_ffn_bg, L3_ffn_W1, L3_ffn_b1, L3_ffn_W2, L3_ffn_b2, L3_ffn_gamma, L3_ffn_beta):
    import jax
    import jax.numpy as jnp

    def _L0_attn_ref(x, w_attn, w_proj, embk, embv):
        import jax, jax.numpy as jnp
        import numpy as np
        N_HEAD = 16
        B, T, C = x.shape
        H = N_HEAD
        d = C // H
        qkv = x @ w_attn
        q, k, v = jnp.split(qkv, 3, axis=2)
        q = q.reshape(B, T, H, d).transpose(0, 2, 1, 3)
        k = k.reshape(B, T, H, d).transpose(0, 2, 1, 3)
        v = v.reshape(B, T, H, d).transpose(0, 2, 1, 3)
        idx = jnp.arange(T)
        rel = jnp.tril(idx[:, None] - idx[None, :])
        rk = embk[rel]
        rv = embv[rel]
        scale = 1.0 / np.sqrt(d).astype(np.float32)
        att = jnp.einsum('bhtd,bhsd->bhts', q, k) * scale + jnp.einsum('bhtd,tsd->bhts', q, rk)
        causal = idx[None, :] <= idx[:, None]
        att = jnp.where(causal[None, None], att, -jnp.inf)
        att = jax.nn.softmax(att, axis=-1)
        y = jnp.einsum('bhts,bhsd->bhtd', att, v) + jnp.einsum('bhts,tsd->bhtd', att, rv)
        y = y.transpose(0, 2, 1, 3).reshape(B, T, C)
        return y @ w_proj

    def _L0_xattn_ref(query, kv_source, w_q, w_k, w_v, w_o):
        import jax, jax.numpy as jnp
        import numpy as np
        D_MODEL = 256
        N_HEADS = 16
        HEAD_DIM = D_MODEL // N_HEADS
        B, T_q, _ = query.shape
        T_kv = kv_source.shape[1]
        q = (query @ w_q.T).reshape(B, T_q, N_HEADS, HEAD_DIM)
        k = (kv_source @ w_k.T).reshape(B, T_kv, N_HEADS, HEAD_DIM)
        v = (kv_source @ w_v.T).reshape(B, T_kv, N_HEADS, HEAD_DIM)
        scale = HEAD_DIM ** (-0.5)
        attn = jax.nn.softmax(jnp.einsum('bqhd,bkhd->bhqk', q, k) * scale, axis=-1)
        out = jnp.einsum('bhqk,bkhd->bqhd', attn, v).reshape(B, T_q, D_MODEL)
        return out @ w_o.T

    def _L0_ffn_ref(inputs, gate_w, gate_b, expert_w, expert_b):
        import jax, jax.numpy as jnp
        import numpy as np
        THRESHOLD = 0.1
        d = inputs.shape[-1]
        x = inputs.reshape(-1, d)
        gate_logits = jax.nn.softmax(x @ gate_w + gate_b, axis=-1)
        selected = (gate_logits >= THRESHOLD).astype(x.dtype)
        weights = gate_logits * selected
        wsum = jnp.sum(weights, axis=-1, keepdims=True)
        weights = weights / jnp.where(wsum == 0, jnp.ones_like(wsum), wsum)
        E = expert_w.shape[0]
        out = jnp.zeros((x.shape[0], expert_w.shape[-1]), dtype=x.dtype)
        for e in range(E):
            out = out + weights[:, e:e + 1] * (x @ expert_w[e] + expert_b[e])
        return out.reshape(*inputs.shape[:-1], out.shape[-1])

    def _L1_attn_ref(query, Wq, bq, Wk, bk, Wv, bv, Wo, bo):
        import jax, jax.numpy as jnp
        import numpy as np
        B, L, E, H = (8, 512, 256, 16)
        D = E // H
        EPS = 1e-06
        bsz, tgt_len, embed_dim = query.shape
        n_head = H
        head_dim = embed_dim // n_head
        m = tgt_len
        q = query @ Wq + bq
        k = query @ Wk + bk
        v = query @ Wv + bv

        def to_heads(x):
            return x.reshape(bsz, tgt_len, n_head, head_dim).transpose(0, 2, 1, 3)
        q = jax.nn.softmax(to_heads(q), axis=-1)
        k = jax.nn.softmax(to_heads(k), axis=-1)
        v = to_heads(v)
        comp_q = 1.0 - q
        comp_k = 1.0 - k
        idx = np.pi / 2 * jnp.arange(1, m + 1, dtype=jnp.float32) / m
        sin = jnp.sin(idx)[None, None, :, None]
        cos = jnp.cos(idx)[None, None, :, None]

        def feat(x):
            return jnp.concatenate([x * sin, x * cos], axis=-1)
        qf, comp_qf = (feat(q), feat(comp_q))
        kf, comp_kf = (feat(k), feat(comp_k))

        def branch(qf_, kf_):
            kv = jnp.einsum('bhld,bhlm->bhdm', kf_, v)
            z = 1.0 / jnp.maximum(jnp.einsum('bhld,bhd->bhl', qf_, kf_.sum(axis=2)), EPS)
            return jnp.einsum('bhld,bhdm,bhl->bhlm', qf_, kv, z)
        attn = branch(qf, kf) + branch(comp_qf, comp_kf)
        out = attn.transpose(2, 0, 1, 3).reshape(tgt_len, bsz, embed_dim)
        out = out @ Wo + bo
        return out.reshape(bsz, tgt_len, embed_dim)

    def _L1_xattn_ref(Query, Key, Value, mask, W_q, W_k, W_v, W_o):
        import jax, jax.numpy as jnp
        import numpy as np
        D_MODEL = 256
        HEADS = 16
        D_K = D_MODEL // HEADS
        B, S = (2, 512)
        NEG = -1000000000.0

        def split_heads(x):
            b, s, _ = x.shape
            return x.reshape(b, s, HEADS, D_K).transpose(0, 2, 1, 3)
        Q = split_heads(Query @ W_q.T)
        K = split_heads(Key @ W_k.T)
        V = split_heads(Value @ W_v.T)
        scores = jnp.einsum('bhqd,bhkd->bhqk', Q, K) / jnp.sqrt(jnp.asarray(D_K, dtype=Q.dtype))
        scores = jnp.where(mask == 0, jnp.asarray(NEG, dtype=scores.dtype), scores)
        attn = jax.nn.softmax(scores, axis=-1)
        X = jnp.einsum('bhqk,bhkd->bhqd', attn, V)
        X = X.transpose(0, 2, 1, 3).reshape(X.shape[0], -1, HEADS * D_K)
        return X @ W_o.T

    def _L1_ffn_ref(inputs_embeds, enc_w, enc_b, s2c_w, s2c_b, r_w1, r_b1, r_w2, r_b2, e_w1, e_b1, e_w2, e_b2, c2s_w, c2s_b, dec_w, dec_b, ln_g, ln_b):
        import jax, jax.numpy as jnp
        import numpy as np
        D_MODEL = 256
        HIDDEN = 512
        MOE_DIM = 64
        N_EXPERTS = 8
        TOP_K = 2
        EXP_HIDDEN = HIDDEN // 2
        B, S = (4, 512)
        b, s, _ = inputs_embeds.shape
        spikes = jax.nn.sigmoid(inputs_embeds @ enc_w + enc_b)
        cont = spikes.reshape(b * s, -1) @ s2c_w + s2c_b
        rh = jax.nn.relu(cont @ r_w1 + r_b1)
        probs = jax.nn.softmax(rh @ r_w2 + r_b2, axis=-1)
        topw, topi = jax.lax.top_k(probs, TOP_K)
        topw = topw / jnp.sum(topw, axis=-1, keepdims=True)
        comb = jnp.sum(jax.nn.one_hot(topi, N_EXPERTS, dtype=cont.dtype) * topw[..., None], axis=1)
        eh = jax.nn.relu(jnp.einsum('nd,edh->neh', cont, e_w1) + e_b1)
        eo = jnp.einsum('neh,ehd->ned', eh, e_w2) + e_b2
        moe_out = jnp.einsum('ned,ne->nd', eo, comb)
        rates = jax.nn.sigmoid(moe_out @ c2s_w + c2s_b)
        x = rates.reshape(b, s, -1)
        dec = jax.nn.sigmoid(x @ dec_w + dec_b)
        mu = jnp.mean(dec, axis=-1, keepdims=True)
        var = jnp.var(dec, axis=-1, keepdims=True)
        return (dec - mu) * jax.lax.rsqrt(var + 1e-05) * ln_g + ln_b

    def _L2_attn_ref(input_data, W1, bias1, W2, bias2, memory_weights):
        import jax, jax.numpy as jnp
        import numpy as np
        B, T, D_IN, D_PROJ, D_OUT, MEM = (8, 512, 256, 256, 256, 40)

        def _fsmn_memory(p, memory_weights):
            M = memory_weights.shape[0] - 1
            b, t, d = p.shape
            rhs = memory_weights[1:][::-1].T[:, None, :]
            lhs = jnp.pad(p.transpose(0, 2, 1), ((0, 0), (0, 0), (M - 1, 0)))
            band = jax.lax.conv_general_dilated(lhs, rhs, window_strides=(1,), padding='VALID', feature_group_count=d, dimension_numbers=('NCH', 'OIH', 'NCH')).transpose(0, 2, 1)
            cs = jnp.cumsum(p, axis=1)
            band_sum = cs - jnp.pad(cs, ((0, 0), (M, 0), (0, 0)))[:, :t]
            total = cs[:, -1:]
            return band + memory_weights[0] * (total - band_sum)
        p = jnp.matmul(input_data, W1) + bias1
        p = _fsmn_memory(p, memory_weights)
        return jnp.matmul(p, W2) + bias2

    def _L2_xattn_ref(x_1, x_2, Wq, bq, Wk, bk, Wv, bv):
        import jax, jax.numpy as jnp
        import numpy as np
        N_HEADS = 16
        EMBED_DIM = 256
        HEAD_DIM = EMBED_DIM // N_HEADS
        B, T_TGT, T_SRC = (2, 512, 512)
        Bt, Tt, C = x_1.shape
        q = (x_1 @ Wq.T + bq).reshape(Bt, Tt, N_HEADS, HEAD_DIM).transpose(0, 2, 1, 3)
        k = (x_2 @ Wk.T + bk).reshape(Bt, -1, N_HEADS, HEAD_DIM).transpose(0, 2, 1, 3)
        v = (x_2 @ Wv.T + bv).reshape(Bt, -1, N_HEADS, HEAD_DIM).transpose(0, 2, 1, 3)
        scores = jnp.einsum('bhqd,bhkd->bhqk', q, k) * HEAD_DIM ** (-0.5)
        attn = jax.nn.softmax(scores, axis=-1)
        out = jnp.einsum('bhqk,bhkd->bhqd', attn, v)
        return out.transpose(0, 2, 1, 3).reshape(Bt, Tt, C)

    def _L2_ffn_ref(x, gate_w, expert_bias, w1, w2, w3):
        import jax, jax.numpy as jnp
        import numpy as np
        TOP_K = 2
        NUM_EXPERTS = 8
        DIM = 256
        HIDDEN = 704
        BS, SLEN = (2, 256)

        def _grouped_ffn(x, w1, w2, w3, counts):
            num_experts = w1.shape[0]
            ends = jnp.cumsum(counts)
            starts = ends - counts
            t = jnp.arange(x.shape[0])
            out = jnp.zeros((x.shape[0], w2.shape[-1]), x.dtype)
            for e in range(num_experts):
                m = ((t >= starts[e]) & (t < ends[e])).astype(x.dtype)[:, None]
                xe = x * m
                h = jax.nn.silu(xe @ w1[e]) * (xe @ w3[e])
                out = out + h @ w2[e] * m
            return out
        bs, slen, dim = x.shape
        num_experts = gate_w.shape[0]
        xf = x.reshape(bs * slen, dim)
        scores = jax.nn.softmax((xf @ gate_w.T).astype(jnp.float32), axis=-1)
        _, sel = jax.lax.top_k(scores + expert_bias, TOP_K)
        top_scores = jnp.take_along_axis(scores, sel, axis=1).reshape(-1)
        sel_flat = sel.reshape(-1)
        counts = jnp.zeros((num_experts,), jnp.int32).at[sel_flat].add(1)
        order = jnp.argsort(sel_flat, stable=True)
        top_scores_sorted = top_scores[order]
        token_idx = order // TOP_K
        routed = xf[token_idx] * top_scores_sorted[:, None].astype(xf.dtype)
        routed_out = _grouped_ffn(routed, w1, w2, w3, counts)
        out = jnp.zeros_like(xf).at[token_idx].add(routed_out)
        return out.reshape(bs, slen, dim)

    def _L3_attn_ref(x, Wq, bq, Wk, bk, Wv, bv, Wo, bo):
        import math
        import jax, jax.numpy as jnp
        import numpy as np
        B, T, D, H = (2, 512, 256, 16)
        N_LAYERS = 24

        def get_slopes(n):

            def pow2(n):
                start = 2 ** (-2 ** (-(math.log2(n) - 3)))
                return [start * start ** i for i in range(n)]
            if math.log2(n).is_integer():
                return pow2(n)
            c = 2 ** math.floor(math.log2(n))
            return pow2(c) + get_slopes(2 * c)[0::2][:n - c]
        Bb, Tt, C = x.shape
        hd = C // H
        q = (x @ Wq + bq).reshape(Bb, Tt, H, hd).transpose(0, 2, 1, 3)
        k = (x @ Wk + bk).reshape(Bb, Tt, H, hd).transpose(0, 2, 1, 3)
        v = (x @ Wv + bv).reshape(Bb, Tt, H, hd).transpose(0, 2, 1, 3)
        attn = jnp.einsum('bhqd,bhkd->bhqk', q, k) / jnp.sqrt(jnp.asarray(hd, x.dtype))
        slopes = jnp.asarray(get_slopes(H), dtype=x.dtype)
        alibi = -slopes[None, :, None, None] * (Tt - 1 - jnp.arange(Tt, dtype=x.dtype))[None, None, None, :]
        attn = attn + alibi
        causal = jnp.tril(jnp.ones((Tt, Tt), dtype=bool))[None, None, :, :]
        attn = jnp.where(causal, attn, jnp.finfo(x.dtype).min)
        p = jax.nn.softmax(attn, axis=-1)
        out = jnp.einsum('bhqk,bhkd->bqhd', p, v).reshape(Bb, Tt, C)
        return out @ Wo + bo

    def _L3_xattn_ref(queries, context, wq, bq, wk, bk, wv, bv, wo, bo):
        import jax, jax.numpy as jnp
        import numpy as np
        D_MODEL = 256
        N_HEADS = 16
        HEAD_DIM = D_MODEL // N_HEADS
        B, NQ, D = queries.shape
        S = context.shape[1]
        H, HD = (N_HEADS, HEAD_DIM)
        scale = HD ** (-0.5)
        q = queries @ wq.T + bq
        k = context @ wk.T + bk
        v = context @ wv.T + bv
        q = q.reshape(B, NQ, H, HD).transpose(0, 2, 1, 3)
        k = k.reshape(B, S, H, HD).transpose(0, 2, 1, 3)
        v = v.reshape(B, S, H, HD).transpose(0, 2, 1, 3)
        attn = jnp.einsum('bhnd,bhsd->bhns', q, k) * scale
        attn = jax.nn.softmax(attn, axis=-1)
        out = jnp.einsum('bhns,bhsd->bhnd', attn, v)
        out = out.transpose(0, 2, 1, 3).reshape(B, NQ, D)
        return out @ wo.T + bo

    def _L3_ffn_ref(x, Wg, bg, W1, b1, W2, b2, gamma, beta):
        import jax, jax.numpy as jnp
        import numpy as np
        B, S, D = (2, 512, 256)
        E, K, DFF = (8, 2, 4 * 256)
        EPS_GATE = 1e-08
        EPS_LN = 1e-05
        b, s, d = x.shape
        xf = x.reshape(-1, d)
        T = xf.shape[0]
        num_experts = Wg.shape[1]
        logits = xf @ Wg + bg
        w = jax.nn.softmax(logits, axis=-1)
        top_w, top_idx = jax.lax.top_k(w, K)
        top_w = top_w / (top_w.sum(axis=-1, keepdims=True) + EPS_GATE)
        cw = jnp.zeros((T, num_experts), xf.dtype).at[jnp.arange(T)[:, None], top_idx].add(top_w)
        out = jnp.zeros_like(xf)
        for e in range(num_experts):
            h = jax.nn.gelu(xf @ W1[e] + b1[e], approximate=False)
            y = h @ W2[e] + b2[e]
            out = out + cw[:, e:e + 1] * y
        mu = out.mean(axis=-1, keepdims=True)
        var = out.var(axis=-1, keepdims=True)
        out = (out - mu) / jnp.sqrt(var + EPS_LN) * gamma + beta
        return out.reshape(b, s, d)
    x = x + _L0_attn_ref(_layernorm(x, axis=-1), L0_attn_w_attn, L0_attn_w_proj, L0_attn_embk, L0_attn_embv)
    x = x + _L0_xattn_ref(_layernorm(x, axis=-1), ctx_1024, L0_xattn_w_q, L0_xattn_w_k, L0_xattn_w_v, L0_xattn_w_o)
    x = x + _L0_ffn_ref(_layernorm(x, axis=-1), L0_ffn_gate_w, L0_ffn_gate_b, L0_ffn_expert_w, L0_ffn_expert_b)
    x = x + _L1_attn_ref(_layernorm(x, axis=-1), L1_attn_Wq, L1_attn_bq, L1_attn_Wk, L1_attn_bk, L1_attn_Wv, L1_attn_bv, L1_attn_Wo, L1_attn_bo)
    x = x + _L1_xattn_ref(_layernorm(x, axis=-1), ctx_1024, ctx_1024, mask_1x1xSxS2_if1, L1_xattn_W_q, L1_xattn_W_k, L1_xattn_W_v, L1_xattn_W_o)
    x = x + _L1_ffn_ref(_layernorm(x, axis=-1), L1_ffn_enc_w, L1_ffn_enc_b, L1_ffn_s2c_w, L1_ffn_s2c_b, L1_ffn_r_w1, L1_ffn_r_b1, L1_ffn_r_w2, L1_ffn_r_b2, L1_ffn_e_w1, L1_ffn_e_b1, L1_ffn_e_w2, L1_ffn_e_b2, L1_ffn_c2s_w, L1_ffn_c2s_b, L1_ffn_dec_w, L1_ffn_dec_b, L1_ffn_ln_g, L1_ffn_ln_b)
    x = x + _L2_attn_ref(_layernorm(x, axis=-1), L2_attn_W1, L2_attn_bias1, L2_attn_W2, L2_attn_bias2, L2_attn_memory_weights)
    x = x + _L2_xattn_ref(_layernorm(x, axis=-1), ctx_1024, L2_xattn_Wq, L2_xattn_bq, L2_xattn_Wk, L2_xattn_bk, L2_xattn_Wv, L2_xattn_bv)
    x = x + _L2_ffn_ref(_layernorm(x, axis=-1), L2_ffn_gate_w, L2_ffn_expert_bias, L2_ffn_w1, L2_ffn_w2, L2_ffn_w3)
    x = x + _L3_attn_ref(_layernorm(x, axis=-1), L3_attn_Wq, L3_attn_bq, L3_attn_Wk, L3_attn_bk, L3_attn_Wv, L3_attn_bv, L3_attn_Wo, L3_attn_bo)
    x = x + _L3_xattn_ref(_layernorm(x, axis=-1), ctx_1024, L3_xattn_wq, L3_xattn_bq, L3_xattn_wk, L3_xattn_bk, L3_xattn_wv, L3_xattn_bv, L3_xattn_wo, L3_xattn_bo)
    x = x + _L3_ffn_ref(_layernorm(x, axis=-1), L3_ffn_Wg, L3_ffn_bg, L3_ffn_W1, L3_ffn_b1, L3_ffn_W2, L3_ffn_b2, L3_ffn_gamma, L3_ffn_beta)
    return x

_drawn_inputs = setup_inputs


def setup_inputs(seed=0):
    import zlib

    import numpy as np

    out = dict(_drawn_inputs(seed))
    spreads = {'L0_ffn_gate_b': (0.0, 0.1),
     'L0_ffn_expert_b': (0.0, 0.1),
     'L1_ffn_enc_b': (0.0, 0.1),
     'L1_ffn_s2c_b': (0.0, 0.1),
     'L1_ffn_r_b1': (0.0, 0.1),
     'L1_ffn_r_b2': (0.0, 0.1),
     'L1_ffn_e_b1': (0.0, 0.1),
     'L1_ffn_e_b2': (0.0, 0.1),
     'L1_ffn_c2s_b': (0.0, 0.1),
     'L1_ffn_dec_b': (0.0, 0.1),
     'L1_ffn_ln_g': (1.0, 0.2),
     'L1_ffn_ln_b': (0.0, 0.1),
     'L2_attn_bias1': (1.0, 0.2),
     'L2_attn_bias2': (1.0, 0.2),
     'L2_ffn_expert_bias': (0.0, 0.8),
     'L3_attn_bq': (0.0, 2.0),
     'L3_attn_bk': (0.0, 2.0),
     'L3_attn_bv': (0.0, 2.0),
     'L3_attn_bo': (0.0, 0.681),
     'L3_xattn_bq': (0.0, 0.8),
     'L3_xattn_bk': (0.0, 2.0),
     'L3_xattn_bv': (0.0, 0.552),
     'L3_xattn_bo': (0.0, 0.601),
     'L3_ffn_bg': (0.0, 0.1),
     'L3_ffn_b1': (0.0, 0.757),
     'L3_ffn_b2': (0.0, 0.525),
     'L3_ffn_gamma': (1.0, 0.6),
     'L3_ffn_beta': (0.0, 0.8)}
    factors = {'L0_attn_embk': 50.503,
     'L0_attn_embv': 21.759,
     'L1_attn_Wq': 5.13,
     'L1_attn_bq': 30.947,
     'L1_attn_Wk': 4.886,
     'L1_attn_bk': 29.156,
     'L2_xattn_bq': 5.468,
     'L2_xattn_bk': 64.0,
     'L2_ffn_gate_w': 8.0,
     'L2_ffn_w1': 8.0,
     'L2_ffn_w2': 8.0,
     'L2_ffn_w3': 8.0,
     'L3_attn_Wq': 64.0,
     'L3_attn_Wk': 64.0,
     'L3_attn_Wv': 8.0,
     'L3_attn_Wo': 8.0}
    for name, (base, spread) in spreads.items():
        noise = np.random.default_rng([zlib.crc32(name.encode()), seed]).standard_normal(out[name].shape)
        drawn = base * np.exp(spread * noise) if base else spread * noise
        out[name] = jnp.asarray(drawn.astype(out[name].dtype))
    for name, factor in factors.items():
        out[name] = (out[name] * factor).astype(out[name].dtype)
    return out
```

```python
from contextlib import ExitStack

import numpy as np
import concourse.bass as bass
from concourse import mybir

ALU = mybir.AluOpType
ACT = mybir.ActivationFunctionType
AX = mybir.AxisListType
F32 = mybir.dt.float32
F32R = mybir.dt.float32r
I32 = mybir.dt.int32

P = 128
B, S, D = 8, 256, 256
T = B * S
KT = D // P
H, HD = 16, 16
HB = 32
QB = H * HB // P
TB = S // P
SC = 77
E = 8
CH = 512
NCH = T // CH
HALF = T // 2
NEG = -1.0e30
LN_EPS = 1e-5
SEMAPHORES = 120
TAPS = 40


class Count:

    def __init__(self, core, name, credit=None):
        self.sem = core.semaphore(name)
        self.credit = credit + 1 if credit is not None else 0

    def at(self, events):
        return events + self.credit


class Chain:

    def __init__(self, core, name):
        self.sem = core.semaphore(name)
        self.n = 0

    def restart(self, engine):
        engine.sem_clear(self.sem)
        self.n = 0

    def link(self, engine, instruction):
        instruction.then_inc(self.sem, 1)
        self.n += 1
        engine.wait_ge(self.sem, self.n)

    def mark(self, instruction):
        instruction.then_inc(self.sem, 1)
        self.n += 1
        return self.n


class Core:

    def __init__(self, nc, stack):
        self.nc = nc
        self.stack = stack
        self.free_semaphores = sorted(nc.free_semaphores)[:SEMAPHORES]
        self.x = self.sbuf("x_residual", [P, KT, T])
        self.xn = self.sbuf("x_normed", [P, KT, T])
        self.ctx = self.sbuf("context", [P, KT, B * SC])
        self.ident = self.sbuf("identity", [P, P])
        self.mean_w = self.sbuf("mean_weights", [P, P])
        self.eps = self.sbuf("ln_eps", [P, 1])
        self.tri = self.sbuf("earlier_expert", [P, E, E])
        self.psum = stack.enter_context(nc.psum_tensor("psum", [P, 8, CH], F32))

    def sbuf(self, name, shape, dtype=F32, stack=None):
        return (stack or self.stack).enter_context(self.nc.sbuf_tensor(name, shape, dtype))


class Stage:

    def __init__(self, core, name):
        self.nc, self.core, self.name = core.nc, core, name
        self.stack = ExitStack()
        self.semaphores = []

    def __enter__(self):
        return self

    def __exit__(self, *failure):
        self.nc.clear_and_free_semaphores(self.semaphores)
        self.core.free_semaphores.extend(s.num for s in self.semaphores)
        return self.stack.__exit__(*failure)

    def semaphore(self, name):
        self.semaphores.append(self.nc.alloc_semaphore(name, num=self.core.free_semaphores.pop(0)))
        return self.semaphores[-1]

    def buf(self, name, shape, dtype=F32):
        return self.stack.enter_context(self.nc.sbuf_tensor(f"{self.name}_{name}", shape, dtype))

    def count(self, name, credit=None):
        return Count(self, f"{self.name}_{name}", credit)

    def chain(self, name):
        return Chain(self, f"{self.name}_{name}")


def load_inputs(core, a):
    with Stage(core, "load") as st:
        nc = core.nc
        loaded = st.count("loaded")
        with nc.Block() as block:

            @block.sync
            def _(sp):
                sp.dma_start(core.x[:], a["xT"].rearrange("(k p) t -> p k t", p=P)).then_inc(loaded.sem, 16)
                sp.dma_start(core.ident[:], a["identity"]).then_inc(loaded.sem, 16)
                sp.dma_start(core.tri[:], a["earlier"].rearrange("(o e) f -> o e f", o=1).to_broadcast([P, E, E])).then_inc(loaded.sem, 16)
                sp.dma_start(core.ctx[:], a["ctxT"].rearrange("(k p) t -> p k t", p=P)).then_inc(loaded.sem, 16)
                sp.wait_ge(loaded.sem, loaded.at(64))

            @block.vector
            def _(dve):
                nc.vector.memset(core.mean_w[:], 1.0 / D)
                nc.vector.memset(core.eps[:], LN_EPS)


def store_output(core, out):
    with Stage(core, "store") as st:
        stored = st.count("stored")
        with core.nc.Block() as block:

            @block.sync
            def _(sp):
                sp.dma_start(out.rearrange("(k p) t -> p k t", p=P), core.x[:]).then_inc(stored.sem, 16)
                sp.wait_ge(stored.sem, stored.at(16))


def layernorm(core, name, src, dst, affine=None, parts=None):
    nc = core.nc
    with Stage(core, name) as st:
        centred = st.buf("centred", [P, 2, KT, CH])
        square = st.buf("square", [P, 2, KT, CH])
        std = st.buf("std", [P, 2, CH])
        rstd = st.buf("rstd", [P, 2, CH])
        gb = st.buf("gamma_beta", [P, 2, KT])
        mean_done, var_done = st.count("mean_done", 2), st.count("var_done")
        centre_done, square_done = st.count("centre_done", 2), st.count("square_done")
        std_done, normed = st.count("std_done", 2), st.count("normed", 2)
        split_high, loaded, chain = st.count("split_high"), st.count("loaded"), st.chain("dve_chain")

        def tokens(q, j):
            return bass.ds((q * 2 + j) * CH, CH)

        with nc.Block() as block:

            @block.sync
            def _(sp):
                if affine is not None:
                    for n, v in enumerate(affine):
                        sp.dma_start(gb[:, n, :], v).then_inc(loaded.sem, 16)
                    sp.wait_ge(loaded.sem, loaded.at(32))

            @block.tensor
            def _(pe):
                pe.sem_inc(mean_done.sem, mean_done.credit)
                with pe.Fori(0, NCH // 2) as q:
                    for j in range(2):
                        pe.wait_ge(centre_done.sem, centre_done.at(q * 2 + j - 1))
                        for k in range(KT):
                            mm = nc.tensor.matmul(core.psum[:, j, :], core.mean_w[:], src[:, k, tokens(q, j)],
                                                  start=(k == 0), stop=(k == KT - 1))
                        mm.then_inc(mean_done.sem, 1)
                    for j in range(2):
                        pe.wait_ge(square_done.sem, square_done.at(q * 2 + j + 1))
                        pe.wait_ge(std_done.sem, std_done.at(q * 2 + j - 1))
                        for k in range(KT):
                            mm = nc.tensor.matmul(core.psum[:, 2 + j, :], core.mean_w[:], square[:, j, k, :],
                                                  start=(k == 0), stop=(k == KT - 1))
                        mm.then_inc(var_done.sem, 1)

            @block.scalar
            def _(act):
                act.sem_inc(std_done.sem, std_done.credit)
                with act.Fori(0, NCH // 2) as q:
                    for j in range(2):
                        act.wait_ge(centre_done.sem, centre_done.at(q * 2 + j + 1))
                        nc.scalar.activation(square[:, j], centred[:, j], ACT.Square).then_inc(square_done.sem, 1)
                    for j in range(2):
                        act.wait_ge(var_done.sem, var_done.at(q * 2 + j + 1))
                        nc.scalar.activation(std[:, j], core.psum[:, 2 + j, :], ACT.Sqrt,
                                             bias=core.eps[:, 0:1]).then_inc(std_done.sem, 1)
                    if parts is not None:
                        for j in range(2):
                            act.wait_ge(normed.sem, normed.at(q * 2 + j + 1))
                            nc.scalar.activation(parts[0][:, :, tokens(q, j)], dst[:, :, tokens(q, j)],
                                                 ACT.Copy).then_inc(split_high.sem, 1)

            @block.gpsimd
            def _(pool):
                if parts is not None:
                    with pool.Fori(0, NCH // 2) as q:
                        for j in range(2):
                            pool.wait_ge(split_high.sem, split_high.at(q * 2 + j + 1))
                            nc.gpsimd.tensor_tensor(parts[1][:, :, tokens(q, j)], dst[:, :, tokens(q, j)],
                                                    parts[0][:, :, tokens(q, j)].bitcast(F32), ALU.subtract)

            @block.vector
            def _(dve):
                dve.sem_inc(centre_done.sem, centre_done.credit)
                dve.sem_inc(normed.sem, normed.credit)
                if affine is not None:
                    dve.wait_ge(loaded.sem, loaded.at(32))
                with dve.Fori(0, NCH // 2) as q:
                    chain.restart(dve)
                    for j in range(2):
                        dve.wait_ge(mean_done.sem, mean_done.at(q * 2 + j + 1))
                        dve.wait_ge(normed.sem, normed.at(q * 2 + j - 1))
                        mean = core.psum[:, j:j + 1, :].to_broadcast([P, KT, CH])
                        nc.vector.tensor_tensor(centred[:, j], src[:, :, tokens(q, j)], mean,
                                                ALU.subtract).then_inc(centre_done.sem, 1)
                    for j in range(2):
                        dve.wait_ge(std_done.sem, std_done.at(q * 2 + j + 1))
                        chain.link(dve, nc.vector.reciprocal(rstd[:, j], std[:, j]))
                        scale = rstd[:, j:j + 1, :].to_broadcast([P, KT, CH])
                        if affine is None:
                            nc.vector.tensor_tensor(dst[:, :, tokens(q, j)], centred[:, j], scale,
                                                    ALU.mult).then_inc(normed.sem, 1)
                        else:
                            chain.link(dve, nc.vector.tensor_tensor(centred[:, j], centred[:, j], scale, ALU.mult))
                            for k in range(KT):
                                ins = nc.vector.tensor_scalar(centred[:, j, k], centred[:, j, k], gb[:, 0, k:k + 1],
                                                              gb[:, 1, k:k + 1], ALU.mult, ALU.add)
                            chain.link(dve, ins)
                            nc.vector.tensor_tensor(dst[:, :, tokens(q, j)], dst[:, :, tokens(q, j)], centred[:, j],
                                                    ALU.add).then_inc(normed.sem, 1)


def attention(core, name, w, kv="self", mask=None, project=True, rel=None):
    nc = core.nc
    causal = kv == "self"
    NK = S if causal else SC
    SEG = [(0, P), (P, S)] if causal else [(0, SC), (SC, SC)]
    W = SEG[1][0] + SEG[1][1]
    KP = P if causal else SC
    SB = NK // P if causal else 1
    TR = [(0, 0, 0), (P, 0, 1), (2 * P, 1, 1)] if causal else [(0, 0, 0), (SC, 0, 1)]
    TW = len(TR) * P
    NPROJ = 5
    RING = 4 if rel else 2
    with Stage(core, name) as st:
        wq = st.buf("wq", [P, KT, H * HB])
        wk = st.buf("wk", [P, KT, H * HB])
        wv = st.buf("wv", [P, KT, D])
        wo = st.buf("wo", [P, KT, D])
        bq = st.buf("bq", [P, QB])
        bk = st.buf("bk", [P, QB])
        bv = st.buf("bv", [P, KT])
        bo = st.buf("bo", [P, KT])
        xb = st.buf("tokens", [P, 2, KT, S])
        kvb = xb if causal else st.buf("ctx_tokens", [P, 2, KT, SC])
        q_sb = st.buf("q", [P, 2, QB, S])
        k_sb = st.buf("k", [P, 2, QB, NK])
        v_sb = st.buf("v", [P, 2, SB, D])
        s_sb = st.buf("scores", [P, 2, W])
        negmax = st.buf("negmax", [P, 2, TB])
        p_sb = st.buf("probs", [P, RING, W])
        pT = st.buf("probsT", [P, 2, TW])
        sums = st.buf("sums", [P, 2, TB, H])
        rsum = st.buf("rsums", [P, 2, TB, H])
        y_sb = st.buf("y", [P, 2, TB, D])
        yT = st.buf("yT", [P, 2, KT, S])
        if causal:
            bias = st.buf("bias", [P, 2 if rel else 1, H, W])
            cmask = st.buf("causal", [P, W])
        if mask is not None:
            mask_i = st.buf("mask_int", [P, W], I32)
            mask_off = st.buf("mask_off", [P, W])
            mask_on = st.buf("mask_on", [P, W])
        loaded, copied, projected = st.count("loaded"), st.count("copied"), st.count("projected")
        evacuated = st.count("evacuated", 2)
        scored = st.count("scored")
        biased = st.count("biased", 2)
        maxed = st.count("maxed")
        exped = st.count("exped", 2)
        transposed = st.count("transposed", RING)
        turned = st.count("turned", 2)
        valued = st.count("valued", 2)
        summed = st.count("summed")
        normed = st.count("normed", 1)
        y_turned, y_moved = st.count("y_turned"), st.count("y_moved", 1)
        out_done, added = st.count("out_done"), st.count("added", 1)
        prepared = st.count("prepared")
        bias_in, bias_used = [st.count(f"bias_in{j}") for j in range(2)], st.count("bias_used", 2)
        bias_masked = st.count("bias_masked")
        p_out = [st.count(f"probs_out{r}", 32) for r in range(RING)] if rel else []
        act_chain, dve_chain = st.chain("act_chain"), st.chain("dve_chain")
        ps = core.psum
        S_BANK, T_BANK, Y_BANK, O_BANK = 2, 4, 6, 7
        xn = core.xn[:].rearrange("p k (b s) -> p k b s", b=B)
        x = core.x[:].rearrange("p k (b s) -> p k b s", b=B)
        ctx = core.ctx[:].rearrange("p k (b s) -> p k b s", b=B)
        biases = [(bq, "bq"), (bk, "bk"), (bv, "bv"), (bo, "bo")]
        loads = [(wq[:], w["wq"].rearrange("(k p) n -> p k n", p=P)), (wk[:], w["wk"].rearrange("(k p) n -> p k n", p=P)),
                 (wv[:], w["wv"].rearrange("(k p) n -> p k n", p=P))]
        if project:
            loads.append((wo[:], w["wo"].rearrange("(k p) n -> p k n", p=P)))
        loads += [(t[:], w[key]) for t, key in biases if key in w]
        if causal and not rel:
            loads.append((bias[:, 0], w["bias"]))
        if rel:
            loads.append((cmask[:], w["causal"]))
        if mask is not None:
            loads.append((mask_i[:].rearrange("p (t s) -> p t s", t=TB), mask.rearrange("a b (t p) s -> p (a b t) s", p=P)))
        scale_k = float(HD) ** -0.5

        with nc.Block() as block:

            @block.sync
            def _(sp):
                for dst, src in loads:
                    sp.dma_start(dst, src).then_inc(loaded.sem, 16)
                if rel:
                    for done in p_out:
                        sp.sem_inc(done.sem, done.credit)
                    with sp.Fori(0, B // 2) as i:
                        for j in range(2):
                            n = i * 2 + j
                            sp.wait_ge(bias_used.sem, bias_used.at((n - 1) * 1))
                            sp.dma_start(bias[:, j, :, 0:P], rel["scores0_read"][n]).then_inc(bias_in[j].sem, 16)
                            sp.dma_start(bias[:, j, :, P:W], rel["scores1_read"][n]).then_inc(bias_in[j].sem, 16)
                            for h in range(H):
                                sp.wait_ge(exped.sem, exped.at(n * H + h + 1))
                                r = (j * H + h) % RING
                                sp.dma_start(rel["probs0_write"][n, h], p_sb[:, r, 0:P]).then_inc(p_out[r].sem, 16)
                                sp.dma_start(rel["probs1_write"][n, h], p_sb[:, r, P:W]).then_inc(p_out[r].sem, 16)
                    for done in p_out:
                        sp.wait_ge(done.sem, done.at(32 * B * H // RING))
                sp.wait_ge(loaded.sem, loaded.at(16 * len(loads)))

            @block.gpsimd
            def _(pool):
                if rel:
                    pool.wait_ge(loaded.sem, loaded.at(16 * len(loads)))
                    with pool.Fori(0, B // 2) as i:
                        for j in range(2):
                            n = i * 2 + j
                            pool.wait_ge(bias_in[j].sem, bias_in[j].at(32 * (i + 1)))
                            nc.gpsimd.tensor_tensor(bias[:, j], bias[:, j],
                                                    cmask[:].rearrange("p (o w) -> p o w", o=1).to_broadcast([P, H, W]),
                                                    ALU.add).then_inc(bias_masked.sem, 1)

            @block.tensor
            def _(pe):
                pe.sem_inc(transposed.sem, transposed.credit)
                pe.sem_inc(valued.sem, valued.credit)
                pe.wait_ge(loaded.sem, loaded.at(16 * len(loads)))

                def projections(n, j):
                    pe.wait_ge(copied.sem, copied.at((n + 1) * (1 if causal else 2)))
                    for g in range(NPROJ):
                        bank = (j * NPROJ + g) % 2
                        pe.wait_ge(evacuated.sem, evacuated.at(n * NPROJ + g - 1))
                        if g == NPROJ - 1:
                            for t in range(SB):
                                for k in range(KT):
                                    mm = nc.tensor.matmul(ps[0:KP, bank, t * D:(t + 1) * D],
                                                          kvb[:, j, k, t * P:t * P + KP], wv[:, k, :],
                                                          start=(k == 0), stop=(k == KT - 1))
                        else:
                            wt, src, n_cols = (wq, xb, S) if g < 2 else (wk, kvb, NK)
                            for m in range(2):
                                blk = (g % 2) * 2 + m
                                for k in range(KT):
                                    mm = nc.tensor.matmul(ps[:, bank, m * S:m * S + n_cols],
                                                          wt[:, k, blk * P:(blk + 1) * P], src[:, j, k, :],
                                                          start=(k == 0), stop=(k == KT - 1))
                        mm.then_inc(projected.sem, 1)

                def heads(n, j):
                    pe.wait_ge(evacuated.sem, evacuated.at((n + 1) * NPROJ))
                    for step in range(H + 2):
                        if step < H:
                            h = step
                            before = biased if causal or mask is not None else exped
                            pe.wait_ge(before.sem, before.at(n * H + h - 1))
                            blk, r = h // 4, HB * (h % 4)
                            for t, (c0, nk) in enumerate(SEG):
                                mm = nc.tensor.matmul(ps[:, S_BANK + h % 2, c0:c0 + nk],
                                                      q_sb[r:r + HB, j, blk, t * P:(t + 1) * P],
                                                      k_sb[r:r + HB, j, blk, 0:nk], start=True, stop=True,
                                                      tile_position=(r, 0))
                            mm.then_inc(scored.sem, 1)
                        if 1 <= step <= H:
                            h = step - 1
                            pe.wait_ge(exped.sem, exped.at(n * H + h + 1))
                            pe.wait_ge(turned.sem, turned.at(n * H + h - 1))
                            for o, (c0, _, _) in enumerate(TR):
                                mm = nc.tensor.transpose(ps[0:KP, T_BANK + h % 2, o * P:(o + 1) * P],
                                                         p_sb[:, (j * H + h) % RING, c0:c0 + KP], core.ident[:])
                            mm.then_inc(transposed.sem, 1)
                        if step >= 2:
                            h = step - 2
                            pe.wait_ge(turned.sem, turned.at(n * H + h + 1))
                            if h == 0:
                                pe.wait_ge(normed.sem, normed.at(n))
                            for t in range(TB):
                                mine = [(o, sb) for o, (_, sb, tt) in enumerate(TR) if tt == t]
                                for a, (o, sb) in enumerate(mine):
                                    mm = nc.tensor.matmul(ps[:, Y_BANK, t * D + h * HD:t * D + (h + 1) * HD],
                                                          pT[0:KP, h % 2, o * P:(o + 1) * P],
                                                          v_sb[0:KP, j, sb, h * HD:(h + 1) * HD],
                                                          start=(a == 0), stop=(a == len(mine) - 1))
                            mm.then_inc(valued.sem, 1)

                def output(n, j):
                    pe.wait_ge(normed.sem, normed.at(n + 1))
                    pe.wait_ge(added.sem, added.at(n))
                    for c in range(KT):
                        for t in range(TB):
                            mm = nc.tensor.transpose(ps[:, O_BANK, c * S + t * P:c * S + (t + 1) * P],
                                                     y_sb[:, j, t, c * P:(c + 1) * P], core.ident[:])
                    mm.then_inc(y_turned.sem, 1)
                    if project:
                        pe.wait_ge(y_moved.sem, y_moved.at(n + 1))
                        for m in range(KT):
                            for k in range(KT):
                                mm = nc.tensor.matmul(ps[:, O_BANK, m * S:(m + 1) * S], wo[:, k, m * P:(m + 1) * P],
                                                      yT[:, j, k, :], start=(k == 0), stop=(k == KT - 1))
                        mm.then_inc(out_done.sem, 1)

                with pe.Fori(0, B // 2) as i:
                    projections(i * 2, 0)
                    heads(i * 2, 0)
                    projections(i * 2 + 1, 1)
                    if not rel:
                        output(i * 2, 0)
                    heads(i * 2 + 1, 1)
                    if not rel:
                        output(i * 2 + 1, 1)

            @block.scalar
            def _(act):
                act.sem_inc(evacuated.sem, evacuated.credit)
                act.sem_inc(exped.sem, exped.credit)
                if causal:
                    act.sem_inc(turned.sem, turned.credit)
                act.sem_inc(y_moved.sem, y_moved.credit)
                act.wait_ge(loaded.sem, loaded.at(16 * len(loads)))
                if "bk" in w:
                    act_chain.link(act, nc.scalar.mul(bk[:], bk[:], scale_k))

                def copy_tokens(n, j):
                    nc.scalar.copy(xb[:, j], xn[:, :, n, :]).then_inc(copied.sem, 1)
                    if not causal:
                        nc.scalar.copy(kvb[:, j], ctx[:, :, n, :]).then_inc(copied.sem, 1)

                def evacuate(n, j):
                    for g in range(NPROJ):
                        bank = (j * NPROJ + g) % 2
                        act.wait_ge(projected.sem, projected.at(n * NPROJ + g + 1))
                        src = ps[:, bank, :].rearrange("p (m s) -> p m s", m=2)
                        if g == NPROJ - 1:
                            ins = nc.scalar.copy(v_sb[0:KP, j], ps[0:KP, bank, 0:SB * D].rearrange("p (t d) -> p t d", t=SB))
                        elif g < 2:
                            for m in range(2):
                                if "bq" in w:
                                    ins = nc.scalar.activation(q_sb[:, j, g * 2 + m, :], src[:, m, :], ACT.Identity,
                                                               bias=bq[:, g * 2 + m:g * 2 + m + 1])
                                else:
                                    ins = nc.scalar.copy(q_sb[:, j, g * 2 + m, :], src[:, m, :])
                        else:
                            for m in range(2):
                                blk = (g - 2) * 2 + m
                                if "bk" in w:
                                    ins = nc.scalar.activation(k_sb[:, j, blk, :], src[:, m, 0:NK], ACT.Identity,
                                                               bias=bk[:, blk:blk + 1], scale=scale_k)
                                else:
                                    ins = nc.scalar.mul(k_sb[:, j, blk, :], src[:, m, 0:NK], scale_k)
                        ins.then_inc(evacuated.sem, 1)

                def heads(n, j):
                    for step in range(H + 1):
                        if step < H:
                            h = step
                            act.wait_ge(maxed.sem, maxed.at(n * H + h + 1))
                            r = (j * H + h) % RING
                            act.wait_ge(transposed.sem, transposed.at(n * H + h + 1 - RING))
                            if rel:
                                act.wait_ge(p_out[r].sem, p_out[r].at(32 * (n * (H // RING) + h // RING)))
                            for t, (c0, nk) in enumerate(SEG):
                                src = s_sb[:, h % 2, c0:c0 + nk] if causal or mask is not None else \
                                    ps[:, S_BANK + h % 2, c0:c0 + nk]
                                ins = nc.scalar.activation(p_sb[:, r, c0:c0 + nk], src, ACT.Exp,
                                                           bias=negmax[:, h % 2, t:t + 1],
                                                           accum_out=sums[:, j, t, h:h + 1])
                            ins.then_inc(exped.sem, 1)
                        if causal and step >= 1:
                            h = step - 1
                            act.wait_ge(transposed.sem, transposed.at(n * H + h + 1))
                            act.wait_ge(valued.sem, valued.at(n * H + h - 1))
                            nc.scalar.copy(pT[0:KP, h % 2, :], ps[0:KP, T_BANK + h % 2, 0:TW]).then_inc(turned.sem, 1)

                def output(n, j):
                    act.wait_ge(y_turned.sem, y_turned.at(n + 1))
                    for c in range(KT):
                        src = ps[:, O_BANK, c * S:(c + 1) * S]
                        if "bv" in w:
                            ins = nc.scalar.activation(yT[:, j, c, :], src, ACT.Identity, bias=bv[:, c:c + 1])
                        else:
                            ins = nc.scalar.copy(yT[:, j, c, :], src)
                    ins.then_inc(y_moved.sem, 1)

                with act.Fori(0, B // 2) as i:
                    for j in range(2):
                        copy_tokens(i * 2 + j, j)
                    evacuate(i * 2, 0)
                    heads(i * 2, 0)
                    evacuate(i * 2 + 1, 1)
                    if not rel:
                        output(i * 2, 0)
                    heads(i * 2 + 1, 1)
                    if not rel:
                        output(i * 2 + 1, 1)

            @block.vector
            def _(dve):
                dve.sem_inc(biased.sem, biased.credit)
                if not causal:
                    dve.sem_inc(turned.sem, turned.credit)
                dve.sem_inc(normed.sem, normed.credit)
                dve.sem_inc(added.sem, added.credit)
                dve.sem_inc(bias_used.sem, bias_used.credit)
                dve.wait_ge(loaded.sem, loaded.at(16 * len(loads)))
                if mask is not None:
                    dve_chain.link(dve, nc.vector.tensor_scalar(mask_off[:], mask_i[:], 0.0, None, ALU.is_equal))
                    dve_chain.link(dve, nc.vector.tensor_scalar(mask_on[:], mask_off[:], -1.0, 1.0, ALU.mult, ALU.add))
                    dve_chain.link(dve, nc.vector.tensor_scalar(mask_off[:], mask_off[:], -1.0e9, None, ALU.mult))

                def heads(n, j):
                    if rel:
                        dve.wait_ge(bias_masked.sem, bias_masked.at(n + 1))
                    for step in range(H + 2):
                        if step == 4 and j == 1 and not rel:
                            add_output(n - 1, 0)
                        if step < H:
                            h = step
                            dve.wait_ge(scored.sem, scored.at(n * H + h + 1))
                            dve.wait_ge(exped.sem, exped.at(n * H + h - 1))
                            tile = ps[:, S_BANK + h % 2, 0:W]
                            if causal:
                                nc.vector.tensor_tensor(s_sb[:, h % 2, :], tile, bias[:, j if rel else 0, h, :],
                                                        ALU.add).then_inc(biased.sem, 1)
                                dve.wait_ge(biased.sem, biased.at(n * H + h + 1))
                                tile = s_sb[:, h % 2, :]
                            elif mask is not None:
                                dve_chain.link(dve, nc.vector.tensor_tensor(s_sb[:, h % 2, :], tile, mask_on[:], ALU.mult))
                                nc.vector.tensor_tensor(s_sb[:, h % 2, :], s_sb[:, h % 2, :], mask_off[:],
                                                        ALU.add).then_inc(biased.sem, 1)
                                dve.wait_ge(biased.sem, biased.at(n * H + h + 1))
                                tile = s_sb[:, h % 2, :]
                            if causal:
                                for t, (c0, nk) in enumerate(SEG):
                                    ins = nc.vector.tensor_reduce(negmax[:, h % 2, t:t + 1], tile[:, c0:c0 + nk], AX.X,
                                                                  ALU.max, negate=True)
                            else:
                                ins = nc.vector.tensor_reduce(negmax[:, h % 2, :], tile.rearrange("p (t s) -> p t s", t=TB),
                                                              AX.X, ALU.max, negate=True)
                            ins.then_inc(maxed.sem, 1)
                        if not causal and step >= 2:
                            h = step - 2
                            dve.wait_ge(transposed.sem, transposed.at(n * H + h + 1))
                            dve.wait_ge(valued.sem, valued.at(n * H + h - 1))
                            nc.vector.tensor_copy(pT[0:KP, h % 2, :], ps[0:KP, T_BANK + h % 2, 0:TW]).then_inc(turned.sem, 1)

                def normalise(n, j):
                    dve.wait_ge(exped.sem, exped.at((n + 1) * H))
                    dve.wait_ge(valued.sem, valued.at((n + 1) * H))
                    if rel:
                        nc.vector.tensor_copy(rel["sums"][:, n, :],
                                              sums[:, j].rearrange("p t h -> p (t h)")).then_inc(bias_used.sem, 1)
                        nc.vector.tensor_copy(rel["y"][:, n, :], ps[:, Y_BANK, :]).then_inc(normed.sem, 1)
                        return
                    dve_chain.link(dve, nc.vector.reciprocal(rsum[:, j], sums[:, j]))
                    nc.vector.tensor_tensor(y_sb[:, j].rearrange("p t (h d) -> p (t h) d", h=H),
                                            ps[:, Y_BANK, :].rearrange("p (a d) -> p a d", d=HD),
                                            rsum[:, j].rearrange("p t (h o) -> p (t h) o", o=1).to_broadcast([P, TB * H, HD]),
                                            ALU.mult).then_inc(normed.sem, 1)

                def add_output(n, j):
                    if project:
                        dve.wait_ge(out_done.sem, out_done.at(n + 1))
                    else:
                        dve.wait_ge(y_moved.sem, y_moved.at(n + 1))
                    for m in range(KT):
                        src = ps[:, O_BANK, m * S:(m + 1) * S] if project else yT[:, j, m, :]
                        dst = x[:, m, n, :]
                        if "bo" in w:
                            ins = nc.vector.scalar_tensor_tensor(out=dst, in0=src, scalar=bo[:, m:m + 1], in1=dst,
                                                                 op0=ALU.add, op1=ALU.add)
                        else:
                            ins = nc.vector.tensor_tensor(dst, src, dst, ALU.add)
                    ins.then_inc(added.sem, 1)

                with dve.Fori(0, B // 2) as i:
                    dve_chain.restart(dve)
                    for j in range(2):
                        heads(i * 2 + j, j)
                        normalise(i * 2 + j, j)
                    if not rel:
                        add_output(i * 2 + 1, 1)


def relative_attention(core, name, w):
    nc = core.nc
    W0, W1 = P, S
    W = W0 + W1
    scores0 = nc.dram_tensor("rel_scores0", (B, H, P * W0), F32).ap()
    scores1 = nc.dram_tensor("rel_scores1", (B, H, P * W1), F32).ap()
    Z0, Z1 = P, P - 1
    probs0 = nc.dram_tensor("rel_probs0", (B, H, Z0 + P * W0), F32).ap()
    probs1 = nc.dram_tensor("rel_probs1", (B, H, Z1 + P * W1), F32).ap()

    def dram_view(t, offset, pitch, rows, cols):
        flat = t.shape[2]
        return bass.AP(tensor=t.tensor, offset=offset, ap=[[H * flat, B], [pitch, rows], [flat, H], [1, cols]])

    rel = {
        "scores0_read": dram_view(scores0, P - 1, W0 - 1, P, W0),
        "scores1_read": dram_view(scores1, P - 1, W1 - 1, P, W1),
        "probs0_write": probs0[:, :, Z0:].rearrange("b h (t s) -> b h t s", t=P),
        "probs1_write": probs1[:, :, Z1:].rearrange("b h (t s) -> b h t s", t=P),
    }
    scores0_write = scores0.rearrange("b h (t u) -> b t h u", t=P)
    scores1_write = scores1.rearrange("b h (t u) -> b t h u", t=P)
    probs0_read = dram_view(probs0, 1, W0 + 1, P, W0)
    probs1_read = dram_view(probs1, 0, W1 + 1, P, W1)

    with Stage(core, name + "_rel") as keep:
        rel["y"] = keep.buf("y_content", [P, B, TB * D])
        rel["sums"] = keep.buf("sums", [P, B, TB * H])
        relative_scores(core, name + "_scores", w, scores0_write, scores1_write, probs0[:, :, 0:Z0], probs1[:, :, 0:Z1])
        attention(core, name, w, rel=rel)
        relative_values(core, name + "_values", w, rel, probs0_read, probs1_read)


def relative_scores(core, name, w, scores0_write, scores1_write, zeros0, zeros1):
    nc = core.nc
    ps = core.psum
    with Stage(core, name) as st:
        wq = st.buf("wq", [P, KT, H * HB])
        embk = st.buf("embk", [P, S])
        q_sb = st.buf("q", [P, 2, QB, S])
        dist = st.buf("by_distance", [P, 2, H, P + S])
        zeros = st.buf("zeros", [P, P])
        loaded, projected, evacuated = st.count("loaded"), st.count("projected"), st.count("evacuated", 2)
        scored, moved = st.count("scored"), st.count("moved", 4)
        stored = [st.count(f"stored{j}", 0) for j in range(2)]
        zeroed, cleared = st.count("zeroed"), st.count("cleared")
        xn = core.xn[:].rearrange("p k (b s) -> p k b s", b=B)
        G = QB // 2
        with nc.Block() as block:

            @block.sync
            def _(sp):
                sp.dma_start(wq[:], w["wq"].rearrange("(k p) n -> p k n", p=P)).then_inc(loaded.sem, 16)
                for r in range(P // HB):
                    sp.dma_start(embk[r * HB:(r + 1) * HB, :], w["embkT"]).then_inc(loaded.sem, 16)
                sp.wait_ge(cleared.sem, cleared.at(1))
                sp.dma_start(zeros0.rearrange("b h z -> (b h) z"), zeros[:, 0:zeros0.shape[2]]).then_inc(zeroed.sem, 16)
                sp.dma_start(zeros1.rearrange("b h z -> (b h) z"), zeros[:, 0:zeros1.shape[2]]).then_inc(zeroed.sem, 16)
                for j in range(2):
                    sp.sem_inc(stored[j].sem, stored[j].credit)
                with sp.Fori(0, B // 2) as i:
                    for j in range(2):
                        n = i * 2 + j
                        sp.wait_ge(moved.sem, moved.at((n + 1) * H))
                        sp.dma_start(scores0_write[n], dist[:, j, :, 0:P]).then_inc(stored[j].sem, 16)
                        sp.dma_start(scores1_write[n], dist[:, j, :, P:P + S]).then_inc(stored[j].sem, 16)
                for j in range(2):
                    sp.wait_ge(stored[j].sem, stored[j].at(32 * B // 2))
                sp.wait_ge(zeroed.sem, zeroed.at(32))

            @block.tensor
            def _(pe):
                pe.wait_ge(loaded.sem, loaded.at(16 * (1 + P // HB)))
                with pe.Fori(0, B // 2) as i:
                    for j in range(2):
                        n = i * 2 + j
                        for g in range(G):
                            pe.wait_ge(evacuated.sem, evacuated.at(n * G + g - 1))
                            for m in range(2):
                                blk = g * 2 + m
                                for k in range(KT):
                                    mm = nc.tensor.matmul(ps[:, g, m * S:(m + 1) * S], wq[:, k, blk * P:(blk + 1) * P],
                                                          xn[:, k, n, :], start=(k == 0), stop=(k == KT - 1))
                            mm.then_inc(projected.sem, 1)
                        pe.wait_ge(evacuated.sem, evacuated.at((n + 1) * G))
                        for h in range(H):
                            pe.wait_ge(moved.sem, moved.at(n * H + h - 3))
                            blk, r = h // 4, HB * (h % 4)
                            bank = 4 + h % 4
                            for t, (c0, u0, nu) in enumerate([(0, S - P, P), (P, 0, S)]):
                                mm = nc.tensor.matmul(ps[:, bank, c0:c0 + nu], q_sb[r:r + HB, j, blk, t * P:(t + 1) * P],
                                                      embk[r:r + HB, u0:u0 + nu], start=True, stop=True,
                                                      tile_position=(r, 0))
                            mm.then_inc(scored.sem, 1)

            @block.scalar
            def _(act):
                act.sem_inc(evacuated.sem, evacuated.credit)
                with act.Fori(0, B // 2) as i:
                    for j in range(2):
                        for g in range(G):
                            act.wait_ge(projected.sem, projected.at((i * 2 + j) * G + g + 1))
                            act.wait_ge(moved.sem, moved.at((i * 2 + j) * H))
                            nc.scalar.copy(q_sb[:, j, g * 2:g * 2 + 2, :],
                                           ps[:, g, :].rearrange("p (m s) -> p m s", m=2)).then_inc(evacuated.sem, 1)

            @block.vector
            def _(dve):
                nc.vector.memset(zeros[:], 0.0).then_inc(cleared.sem, 1)
                dve.sem_inc(moved.sem, moved.credit)
                with dve.Fori(0, B // 2) as i:
                    for j in range(2):
                        n = i * 2 + j
                        dve.wait_ge(stored[j].sem, stored[j].at(32 * i))
                        for h in range(H):
                            dve.wait_ge(scored.sem, scored.at(n * H + h + 1))
                            nc.vector.tensor_copy(dist[:, j, h, :], ps[:, 4 + h % 4, 0:P + S]).then_inc(moved.sem, 1)


def relative_values(core, name, w, rel, probs0_read, probs1_read):
    nc = core.nc
    ps = core.psum
    T_BANK, Y_BANK, O_BANK = 0, 4, 6
    NT = 3
    with Stage(core, name) as st:
        wo = st.buf("wo", [P, KT, D])
        embv = st.buf("embv", [P, TB, HD])
        shifted = st.buf("by_distance", [P, 2, H, P + S])
        pT = st.buf("probsT", [P, 4, NT * P])
        rsum = st.buf("rsums", [P, 2, TB * H])
        y_sb = st.buf("y", [P, 2, TB * D])
        yT = st.buf("yT", [P, 2, KT, S])
        loaded, shifted_in = st.count("loaded"), [st.count(f"shifted_in{j}") for j in range(2)]
        transposed, turned = st.count("transposed"), st.count("turned", 4)
        valued, normed = st.count("valued", 4), st.count("normed", 2)
        summed, recip = st.count("summed"), st.count("reciprocal")
        y_turned, y_moved = st.count("y_turned"), st.count("y_moved", 2)
        out_done, added = st.count("out_done"), st.count("added", 2)
        x = core.x[:].rearrange("p k (b s) -> p k b s", b=B)
        with nc.Block() as block:

            @block.sync
            def _(sp):
                sp.dma_start(wo[:], w["wo"].rearrange("(k p) n -> p k n", p=P)).then_inc(loaded.sem, 16)
                sp.dma_start(embv[:], w["embv"]).then_inc(loaded.sem, 16)
                with sp.Fori(0, B // 2) as i:
                    for j in range(2):
                        n = i * 2 + j
                        sp.wait_ge(normed.sem, normed.at(n - 1))
                        sp.dma_start(shifted[:, j, :, 0:P], probs0_read[n]).then_inc(shifted_in[j].sem, 16)
                        sp.dma_start(shifted[:, j, :, P:P + S], probs1_read[n]).then_inc(shifted_in[j].sem, 16)
                sp.wait_ge(loaded.sem, loaded.at(32))

            @block.tensor
            def _(pe):
                pe.sem_inc(valued.sem, valued.credit)
                pe.wait_ge(loaded.sem, loaded.at(32))
                with pe.Fori(0, B // 2) as i:
                    for j in range(2):
                        n = i * 2 + j
                        pe.wait_ge(shifted_in[j].sem, shifted_in[j].at(32 * (i + 1)))
                        for step in range(H + 2):
                            if step < H:
                                h = step
                                pe.wait_ge(turned.sem, turned.at(n * H + h - 3))
                                for o in range(NT):
                                    mm = nc.tensor.transpose(ps[:, T_BANK + h % 4, o * P:(o + 1) * P],
                                                             shifted[:, j, h, o * P:(o + 1) * P], core.ident[:])
                                mm.then_inc(transposed.sem, 1)
                            if step >= 2:
                                h = step - 2
                                pe.wait_ge(turned.sem, turned.at(n * H + h + 1))
                                if h == 0:
                                    pe.wait_ge(normed.sem, normed.at(n - 1))
                                for t, mine in enumerate([[(0, 1)], [(1, 0), (2, 1)]]):
                                    for q, (o, half) in enumerate(mine):
                                        mm = nc.tensor.matmul(ps[:, Y_BANK + j, t * D + h * HD:t * D + (h + 1) * HD],
                                                              pT[:, h % 4, o * P:(o + 1) * P], embv[:, half, :],
                                                              start=(q == 0), stop=(q == len(mine) - 1))
                                mm.then_inc(valued.sem, 1)
                        pe.wait_ge(normed.sem, normed.at(n + 1))
                        pe.wait_ge(added.sem, added.at(n - 1))
                        for c in range(KT):
                            for t in range(TB):
                                mm = nc.tensor.transpose(ps[:, O_BANK + j, c * S + t * P:c * S + (t + 1) * P],
                                                         y_sb[:, j, t * D + c * P:t * D + (c + 1) * P], core.ident[:])
                        mm.then_inc(y_turned.sem, 1)
                        pe.wait_ge(y_moved.sem, y_moved.at(n + 1))
                        for m in range(KT):
                            for k in range(KT):
                                mm = nc.tensor.matmul(ps[:, O_BANK + j, m * S:(m + 1) * S], wo[:, k, m * P:(m + 1) * P],
                                                      yT[:, j, k, :], start=(k == 0), stop=(k == KT - 1))
                        mm.then_inc(out_done.sem, 1)

            @block.scalar
            def _(act):
                act.sem_inc(turned.sem, turned.credit)
                act.sem_inc(y_moved.sem, y_moved.credit)
                with act.Fori(0, B // 2) as i:
                    for j in range(2):
                        n = i * 2 + j
                        for h in range(H):
                            act.wait_ge(transposed.sem, transposed.at(n * H + h + 1))
                            act.wait_ge(valued.sem, valued.at(n * H + h - 3))
                            nc.scalar.copy(pT[:, h % 4, :], ps[:, T_BANK + h % 4, 0:NT * P]).then_inc(turned.sem, 1)
                        act.wait_ge(y_turned.sem, y_turned.at(n + 1))
                        nc.scalar.copy(yT[:, j], ps[:, O_BANK + j, :].rearrange("p (c s) -> p c s", c=KT)).then_inc(y_moved.sem, 1)

            @block.vector
            def _(dve):
                dve.sem_inc(normed.sem, normed.credit)
                dve.sem_inc(added.sem, added.credit)
                with dve.Fori(0, B // 2) as i:
                    for j in range(2):
                        n = i * 2 + j
                        dve.wait_ge(normed.sem, normed.at(n - 1))
                        nc.vector.reciprocal(rsum[:, j], rel["sums"][:, n, :]).then_inc(recip.sem, 1)
                        dve.wait_ge(valued.sem, valued.at((n + 1) * H))
                        nc.vector.tensor_tensor(rel["y"][:, n, :], rel["y"][:, n, :], ps[:, Y_BANK + j, :],
                                                ALU.add).then_inc(summed.sem, 1)
                        dve.wait_ge(recip.sem, recip.at(n + 1))
                        dve.wait_ge(summed.sem, summed.at(n + 1))
                        nc.vector.tensor_tensor(y_sb[:, j].rearrange("p (a d) -> p a d", d=HD),
                                                rel["y"][:, n, :].rearrange("p (a d) -> p a d", d=HD),
                                                rsum[:, j].rearrange("p (a o) -> p a o", o=1).to_broadcast([P, TB * H, HD]),
                                                ALU.mult).then_inc(normed.sem, 1)
                        dve.wait_ge(out_done.sem, out_done.at(n + 1))
                        nc.vector.tensor_tensor(x[:, :, n, :], ps[:, O_BANK + j, :].rearrange("p (m s) -> p m s", m=KT),
                                                x[:, :, n, :], ALU.add).then_inc(added.sem, 1)


def gate(core, name, src, rows, weight, bias, mode, gT, gate_dram, select_bias=None):
    nc = core.nc
    ps = core.psum
    NT = T // P
    kt = src.shape[1]
    eps = 1e-8 if mode == "top2_eps" else None
    with Stage(core, name) as st:
        wg = st.buf("wg", [P, kt, E])
        bg = st.buf("bg", [P, E])
        sb = st.buf("select_bias", [P, E])
        p = st.buf("p", [P, NT, E])
        key = st.buf("key", [P, NT, E])
        stat = st.buf("stat", [P, NT])
        pair = st.buf("pair", [P, NT, E, E])
        tie = st.buf("tie", [P, NT, E, E])
        rank = st.buf("rank", [P, NT, E])
        loaded, logits_done = st.count("loaded"), st.count("logits_done")
        shifted, exped = st.count("shifted"), st.count("exped")
        weighted, turned, moved, stored = st.count("weighted"), st.count("turned"), st.count("moved"), st.count("stored")
        chain = st.chain("chain")
        n_loads = 1 + (bias is not None) + (select_bias is not None)

        def over_experts(t):
            return t.rearrange("p (n o) -> p n o", o=1).to_broadcast([P, NT, E])

        def over_tiles(t):
            return t.rearrange("p (o e) -> p o e", o=1).to_broadcast([P, NT, E])

        with nc.Block() as block:

            @block.sync
            def _(sp):
                sp.dma_start(wg[0:rows], weight.rearrange("(k p) e -> p k e", p=rows)).then_inc(loaded.sem, 16)
                for dst, vec in ((bg, bias), (sb, select_bias)):
                    if vec is not None:
                        sp.dma_start(dst[:], vec.rearrange("(o e) -> o e", o=1).to_broadcast([P, E])).then_inc(loaded.sem, 16)
                sp.wait_ge(moved.sem, moved.at(4))
                sp.dma_start(gate_dram, gT[0:E, :]).then_inc(stored.sem, 16)
                sp.wait_ge(stored.sem, stored.at(16))
                sp.wait_ge(loaded.sem, loaded.at(16 * n_loads))

            @block.tensor
            def _(pe):
                pe.wait_ge(loaded.sem, loaded.at(16 * n_loads))
                for t in range(NT):
                    for k in range(kt):
                        mm = nc.tensor.matmul(ps[:, 0, t * E:(t + 1) * E], src[0:rows, k, t * P:(t + 1) * P],
                                              wg[0:rows, k, :], start=(k == 0), stop=(k == kt - 1))
                mm.then_inc(logits_done.sem, 1)
                pe.wait_ge(weighted.sem, weighted.at(1))
                for t in range(NT):
                    c, o = t * P // CH, t * P % CH
                    mm = nc.tensor.transpose(ps[0:E, 1 + c, o:o + P], p[:, t, :], core.ident[:])
                    if o + P == CH:
                        mm.then_inc(turned.sem, 1)

            @block.scalar
            def _(act):
                act.wait_ge(shifted.sem, shifted.at(1))
                nc.scalar.activation(p[:], p[:], ACT.Exp).then_inc(exped.sem, 1)
                for c in range(T // CH):
                    act.wait_ge(turned.sem, turned.at(c + 1))
                    nc.scalar.copy(gT[0:E, c * CH:(c + 1) * CH], ps[0:E, 1 + c, :]).then_inc(moved.sem, 1)

            @block.vector
            def _(dve):
                def do(ins):
                    chain.link(dve, ins)

                def tt(out, a, b, op):
                    do(nc.vector.tensor_tensor(out, a, b, op))

                dve.wait_ge(loaded.sem, loaded.at(16 * n_loads))
                dve.wait_ge(logits_done.sem, logits_done.at(1))
                logits = ps[:, 0, 0:NT * E].rearrange("p (n e) -> p n e", e=E)
                if bias is not None:
                    tt(p[:], logits, over_tiles(bg[:]), ALU.add)
                else:
                    do(nc.vector.tensor_copy(p[:], logits))
                do(nc.vector.tensor_reduce(stat[:], p[:], AX.X, ALU.max))
                nc.vector.tensor_tensor(p[:], p[:], over_experts(stat[:]), ALU.subtract).then_inc(shifted.sem, 1)
                dve.wait_ge(exped.sem, exped.at(1))
                do(nc.vector.tensor_reduce(stat[:], p[:], AX.X, ALU.add))
                do(nc.vector.reciprocal(stat[:], stat[:]))
                tt(p[:], p[:], over_experts(stat[:]), ALU.mult)
                if mode == "threshold":
                    do(nc.vector.tensor_scalar(rank[:], p[:], 0.1, None, ALU.is_ge))
                    tt(p[:], p[:], rank[:], ALU.mult)
                    do(nc.vector.tensor_reduce(stat[:], p[:], AX.X, ALU.add))
                    do(nc.vector.tensor_scalar(rank[:, :, 0], stat[:], 0.0, None, ALU.is_equal))
                    tt(stat[:], stat[:], rank[:, :, 0], ALU.add)
                    do(nc.vector.reciprocal(stat[:], stat[:]))
                else:
                    if select_bias is not None:
                        tt(key[:], p[:], over_tiles(sb[:]), ALU.add)
                    else:
                        do(nc.vector.tensor_copy(key[:], p[:]))
                    for t in range(NT):
                        mine = key[:, t, :].rearrange("p (e o) -> p e o", o=1).to_broadcast([P, E, E])
                        other = key[:, t, :].rearrange("p (o f) -> p o f", o=1).to_broadcast([P, E, E])
                        nc.vector.tensor_tensor(pair[:, t], other, mine, ALU.is_gt)
                        ins = nc.vector.tensor_tensor(tie[:, t], other, mine, ALU.is_equal)
                    do(ins)
                    tri = core.tri[:].rearrange("p (o e) f -> p o (e f)", o=1).to_broadcast([P, NT, E * E])
                    tt(tie[:].rearrange("p n e f -> p n (e f)"), tie[:].rearrange("p n e f -> p n (e f)"), tri, ALU.mult)
                    tt(pair[:], pair[:], tie[:], ALU.add)
                    do(nc.vector.tensor_reduce(rank[:], pair[:], AX.X, ALU.add))
                    do(nc.vector.tensor_scalar(rank[:], rank[:], 2.0, None, ALU.is_lt))
                    if mode == "top2_raw":
                        nc.vector.tensor_tensor(p[:], p[:], rank[:], ALU.mult).then_inc(weighted.sem, 1)
                        return
                    tt(p[:], p[:], rank[:], ALU.mult)
                    do(nc.vector.tensor_reduce(stat[:], p[:], AX.X, ALU.add))
                    if eps:
                        do(nc.vector.tensor_scalar(stat[:], stat[:], eps, None, ALU.add))
                    do(nc.vector.reciprocal(stat[:], stat[:]))
                nc.vector.tensor_tensor(p[:], p[:], over_experts(stat[:]), ALU.mult).then_inc(weighted.sem, 1)


def experts(core, name, kind, w, gT, gate_dram, src, parts=None, rows=P, hidden=0, out_rows=P, out_tiles=KT,
            act_fn=None, store=None):
    nc = core.nc
    ps = core.psum
    kt = src.shape[1]
    MT = kt if kind == "linear" else hidden // P
    NC = HALF // CH
    U = NC * MT
    NW1 = {"linear": 0, "mlp": 1, "swiglu": 2}[kind]
    W1 = kt * hidden
    WT = NW1 * W1 + MT * out_tiles * out_rows
    O2 = NW1 * W1
    LAG = 2
    R = 4
    H_RING = 4 // max(NW1, 1)
    with Stage(core, name) as st:
        raw = st.buf("raw", [P, WT])
        w_hi = st.buf("w_hi", [P, 2, WT], F32R)
        w_lo = st.buf("w_lo", [P, 2, WT], F32R)
        gates = st.buf("gates", [P, 2, HALF])
        zeros = st.buf("zeros", [P, CH], F32R)
        act_out = st.buf("act_out", [P, 2, CH])
        gated = st.buf("gated", [P, 2, CH])
        h_hi = st.buf("h_hi", [P, R, CH], F32R)
        h_lo = st.buf("h_lo", [P, R, CH], F32R)
        b1 = st.buf("b1", [P, E, max(MT, 1)])
        b2 = st.buf("b2", [E, out_tiles * out_rows])
        if kind == "swiglu":
            xs = st.buf("scaled_in", [P, kt, CH])
            xs_hi = st.buf("scaled_in_hi", [P, NC, kt, CH], F32R)
            xs_lo = st.buf("scaled_in_lo", [P, NC, kt, CH], F32R)
        loaded, zeroed = st.count("loaded"), st.count("zeroed")
        raw_in, w_split = st.count("raw_in"), st.count("w_split", 0)
        gates_in = [st.count(f"gates_in{j}") for j in range(2)]
        hidden_done, act_done = st.count("hidden_done", 2 * U), st.count("act_done", H_RING)
        gate_done, high_done, low_done = st.count("gate_done", U), st.count("high_done"), st.count("low_done", 2)
        product_done = st.count("product_done", max(R, U))
        in_split = st.count("in_split", NC)
        closed, emptied = st.count("closed"), st.count("emptied", 0)
        pool_chain = st.chain("pool_chain")
        step_on = st.count("step_on").sem
        has_b1, has_b2 = "b1" in w, "b2" in w
        n_loads = has_b1 + has_b2
        views = []
        if NW1:
            views.append((w["w1"].rearrange("e (k p) n -> e p k n", p=rows), 0, rows, kt))
        if NW1 == 2:
            views.append((w["w3"].rearrange("e (k p) n -> e p k n", p=rows), W1, rows, kt))
        views.append((w["w2"].rearrange("e (k p) n -> e p k n", p=P), O2, P, MT))
        RAWS = 16 * len(views)

        def w1_cols(which, k, m):
            o = which * W1 + k * hidden + m * P
            return slice(o, o + P)

        def w2_cols(m, mo):
            o = O2 + (m * out_tiles + mo) * out_rows
            return slice(o, o + out_rows)

        def tokens(half, c):
            return bass.ds(half * HALF + c * CH, CH)

        with nc.Block() as block:

            @block.sync
            def _(sp):
                if rows < P:
                    sp.wait_ge(zeroed.sem, zeroed.at(2))
                if has_b1:
                    sp.dma_start(b1[:], w["b1"]).then_inc(loaded.sem, 16)
                if has_b2:
                    sp.dma_start(b2[:], w["b2"]).then_inc(loaded.sem, 16)
                with sp.Fori(0, 2) as half:
                    with sp.Fori(0, E // 2) as pair:
                        for j in range(2):
                            turn = half * (E // 2) + pair
                            n = turn * 2 + j
                            sp.wait_ge(w_split.sem, w_split.at(n))
                            for view, o, r, tiles in views:
                                width = view.shape[3] * tiles
                                sp.dma_start(raw[0:r, o:o + width].rearrange("p (k n) -> p k n", k=tiles),
                                             view[pair * 2 + j]).then_inc(raw_in.sem, 16)
                            if kind == "swiglu":
                                sp.wait_ge(in_split.sem, in_split.at((n - 1) * NC))
                            else:
                                sp.wait_ge(gate_done.sem, gate_done.at((n - 1) * U))
                            sp.dma_start(gates[:, j, :], gate_dram[bass.ds(pair * 2 + j, 1), bass.ds(half * HALF, HALF)]
                                         .to_broadcast([P, HALF])).then_inc(gates_in[j].sem, 16)
                if n_loads:
                    sp.wait_ge(loaded.sem, loaded.at(16 * n_loads))

            @block.gpsimd
            def _(pool):
                pool.sem_inc(in_split.sem, in_split.credit)
                pool.sem_inc(w_split.sem, w_split.credit)
                nc.gpsimd.memset(zeros[:].bitcast(F32), 0.0).then_inc(zeroed.sem, 1)
                if rows < P:
                    nc.gpsimd.memset(raw[:], 0.0).then_inc(zeroed.sem, 1)
                with pool.Fori(0, 2) as half:
                    with pool.Fori(0, E // 2) as pair:
                        pool_chain.restart(pool)
                        for j in range(2):
                            turn = half * (E // 2) + pair
                            n = turn * 2 + j
                            pool.wait_ge(raw_in.sem, raw_in.at(RAWS * (n + 1)))
                            pool.wait_ge(product_done.sem, product_done.at((n - 1) * U))
                            pool.sem_inc(step_on, 1)
                            pool_chain.link(pool, nc.gpsimd.tensor_copy(w_hi[:, j, :], raw[:]))
                            nc.gpsimd.tensor_tensor(w_lo[:, j, :], raw[:], w_hi[:, j, :].bitcast(F32),
                                                    ALU.subtract).then_inc(w_split.sem, 1)
                            if kind == "swiglu":
                                pool.wait_ge(gates_in[j].sem, gates_in[j].at(16 * (turn + 1)))
                                for c in range(NC):
                                    pool.wait_ge(hidden_done.sem, hidden_done.at((n - 1) * U + (c + 1) * MT))
                                    pool.wait_ge(in_split.sem, in_split.at(n * NC + c))
                                    pool.sem_inc(step_on, 1)
                                    g = gates[:, j:j + 1, c * CH:(c + 1) * CH].to_broadcast([P, kt, CH])
                                    pool_chain.link(pool, nc.gpsimd.tensor_tensor(xs[:], src[:, :, tokens(half, c)], g, ALU.mult))
                                    pool_chain.link(pool, nc.gpsimd.tensor_copy(xs_hi[:, c], xs[:]))
                                    nc.gpsimd.tensor_tensor(xs_lo[:, c], xs[:], xs_hi[:, c].bitcast(F32),
                                                            ALU.subtract).then_inc(in_split.sem, 1)

            @block.tensor
            def _(pe):
                pe.sem_inc(hidden_done.sem, hidden_done.credit)
                pe.sem_inc(product_done.sem, product_done.credit)
                if n_loads:
                    pe.wait_ge(loaded.sem, loaded.at(16 * n_loads))
                pe.wait_ge(zeroed.sem, zeroed.at(1))

                def three(out, hi_w, lo_w, hi_x, lo_x, start, stop):
                    nc.tensor.matmul(out, hi_w, hi_x, start=start, stop=False, skip_group_check=True)
                    nc.tensor.matmul(out, hi_w, lo_x, start=False, stop=False, skip_group_check=True)
                    return nc.tensor.matmul(out, lo_w, hi_x, start=False, stop=stop, skip_group_check=True)

                def first_product(half, n, j, u):
                    c, m = divmod(u, MT)
                    if kind == "swiglu":
                        if m == 0:
                            pe.wait_ge(in_split.sem, in_split.at(n * NC + c + 1))
                        pe.wait_ge(gate_done.sem, gate_done.at(n * U + u + 1 - H_RING))
                        hi, lo = xs_hi[:, c], xs_lo[:, c]
                    else:
                        pe.wait_ge(act_done.sem, act_done.at(n * U + u + 1 - H_RING))
                        hi, lo = parts[0][0:rows, :, tokens(half, c)], parts[1][0:rows, :, tokens(half, c)]
                    for which in range(NW1):
                        bank = 4 + (u % H_RING) * NW1 + which
                        for k in range(kt):
                            cols = w1_cols(which, k, m)
                            mm = three(ps[:, bank, :], w_hi[0:rows, j, cols], w_lo[0:rows, j, cols], hi[:, k], lo[:, k],
                                       k == 0, k == kt - 1)
                    mm.then_inc(hidden_done.sem, 1)

                def last_product(n, j, u):
                    c, m = divmod(u, MT)
                    pe.wait_ge(low_done.sem, low_done.at(n * U + u + 1))
                    for mo in range(out_tiles):
                        mm = three(ps[0:out_rows, c * out_tiles + mo, :], w_hi[:, j, w2_cols(m, mo)],
                                   w_lo[:, j, w2_cols(m, mo)], h_hi[:, u % R, :], h_lo[:, u % R, :], False, False)
                    mm.then_inc(product_done.sem, 1)

                with pe.Fori(0, 2) as half:
                    pe.wait_ge(emptied.sem, emptied.at(half))
                    for c in range(NC):
                        for mo in range(out_tiles):
                            nc.tensor.matmul(ps[0:out_rows, c * out_tiles + mo, :], zeros[:, 0:out_rows], zeros[:],
                                             start=True, stop=False, skip_group_check=True)
                    with pe.Fori(0, E // 2) as pair:
                        for j in range(2):
                            n = (half * (E // 2) + pair) * 2 + j
                            pe.wait_ge(w_split.sem, w_split.at(n + 1))
                            for step in range(U + LAG):
                                if NW1 and step < U:
                                    first_product(half, n, j, step)
                                if step >= LAG:
                                    last_product(n, j, step - LAG)
                    for c in range(NC):
                        for mo in range(out_tiles):
                            out = ps[0:out_rows, c * out_tiles + mo, :]
                            if has_b2:
                                mm = nc.tensor.matmul(out, b2[:, mo * out_rows:(mo + 1) * out_rows], gT[0:E, tokens(half, c)],
                                                      start=False, stop=True, skip_group_check=True)
                            else:
                                mm = nc.tensor.matmul(out, zeros[:, 0:out_rows], zeros[:], start=False, stop=True,
                                                      skip_group_check=True)
                    mm.then_inc(closed.sem, 1)

            @block.scalar
            def _(act):
                act.sem_inc(act_done.sem, act_done.credit)
                if n_loads:
                    act.wait_ge(loaded.sem, loaded.at(16 * n_loads))
                with act.Fori(0, 2) as half:
                    with act.Fori(0, E // 2) as pair:
                        for j in range(2):
                            n = (half * (E // 2) + pair) * 2 + j
                            for step in range(U + 1):
                                if NW1 and step < U:
                                    u = step
                                    act.wait_ge(hidden_done.sem, hidden_done.at(n * U + u + 1))
                                    act.wait_ge(gate_done.sem, gate_done.at(n * U + u - 1))
                                    hidden_ps = ps[:, 4 + (u % H_RING) * NW1, :]
                                    if has_b1:
                                        act.sem_inc(step_on, 1)
                                        ins = nc.scalar.activation(act_out[:, u % 2, :], hidden_ps, act_fn,
                                                                   bias=b1[:, pair * 2 + j, u % MT:u % MT + 1])
                                    else:
                                        ins = nc.scalar.activation(act_out[:, u % 2, :], hidden_ps, act_fn)
                                    ins.then_inc(act_done.sem, 1)
                                if step >= 1:
                                    u = step - 1
                                    act.wait_ge(gate_done.sem, gate_done.at(n * U + u + 1))
                                    act.wait_ge(product_done.sem, product_done.at(n * U + u + 1 - R))
                                    nc.scalar.copy(h_hi[:, u % R, :], gated[:, u % 2, :]).then_inc(high_done.sem, 1)

            @block.vector
            def _(dve):
                dve.sem_inc(gate_done.sem, gate_done.credit)
                dve.sem_inc(low_done.sem, low_done.credit)
                dve.sem_inc(emptied.sem, emptied.credit)
                with dve.Fori(0, 2) as half:
                    with dve.Fori(0, E // 2) as pair:
                        for j in range(2):
                            turn = half * (E // 2) + pair
                            n = turn * 2 + j
                            dve.wait_ge(gates_in[j].sem, gates_in[j].at(16 * (turn + 1)))
                            for step in range(U + 1):
                                if step < U:
                                    u = step
                                    c, m = divmod(u, MT)
                                    dve.wait_ge(low_done.sem, low_done.at(n * U + u - 1))
                                    g = gates[:, j, c * CH:(c + 1) * CH]
                                    if kind == "linear":
                                        a, b = src[:, m, tokens(half, c)], g
                                    else:
                                        dve.wait_ge(act_done.sem, act_done.at(n * U + u + 1))
                                        a = act_out[:, u % 2, :]
                                        b = ps[:, 5 + (u % H_RING) * NW1, :] if kind == "swiglu" else g
                                    nc.vector.tensor_tensor(gated[:, u % 2, :], a, b, ALU.mult).then_inc(gate_done.sem, 1)
                                if step >= 1:
                                    u = step - 1
                                    dve.wait_ge(high_done.sem, high_done.at(n * U + u + 1))
                                    nc.vector.tensor_tensor(h_lo[:, u % R, :], gated[:, u % 2, :],
                                                            h_hi[:, u % R, :].bitcast(F32), ALU.subtract).then_inc(low_done.sem, 1)
                    dve.wait_ge(closed.sem, closed.at(half + 1))
                    for c in range(NC):
                        sums = ps[0:out_rows, c * out_tiles:(c + 1) * out_tiles, :]
                        if store is None:
                            dst = core.x[:, :, tokens(half, c)]
                            ins = nc.vector.tensor_tensor(dst, dst, sums, ALU.add)
                        else:
                            ins = nc.vector.tensor_copy(store[0:out_rows, :, tokens(half, c)], sums)
                    ins.then_inc(emptied.sem, 1)


def two_layers(core, name, w, src, rows, dst, out_rows, out_tiles, last_fn, parts=None, third=None):
    nc = core.nc
    ps = core.psum
    kt = src.shape[1]
    M1 = w["w1"].shape[1] // P
    with Stage(core, name) as st:
        w1 = st.buf("w1", [P, kt, M1 * P])
        w2 = st.buf("w2", [P, M1, out_tiles * out_rows])
        b1 = st.buf("b1", [P, M1])
        b2 = st.buf("b2", [P, out_tiles])
        w3 = st.buf("w3", [P, P])
        b3 = st.buf("b3", [P, 1])
        hid = st.buf("hidden", [P, 2, M1, CH])
        loaded, hidden_done, squashed = st.count("loaded"), st.count("hidden_done"), st.count("squashed", M1)
        out_done, moved = st.count("out_done", 2), st.count("moved", 2)
        third_done, third_moved = st.count("third_done"), st.count("third_moved", 2)
        split_high = st.count("split_high")
        loads = [(w1[0:rows], w["w1"].rearrange("(k p) n -> p k n", p=rows)), (w2[:], w["w2"].rearrange("(k p) n -> p k n", p=P)),
                 (b1[:], w["b1"]), (b2[0:out_rows], w["b2"])]
        if third:
            loads += [(w3[0:out_rows, 0:out_rows], third[0]), (b3[0:out_rows], third[1])]

        def tokens(q, j):
            return bass.ds((q * 2 + j) * CH, CH)

        with nc.Block() as block:

            @block.sync
            def _(sp):
                for to, of in loads:
                    sp.dma_start(to, of).then_inc(loaded.sem, 16)
                sp.wait_ge(loaded.sem, loaded.at(16 * len(loads)))

            @block.tensor
            def _(pe):
                pe.sem_inc(out_done.sem, out_done.credit)
                pe.wait_ge(loaded.sem, loaded.at(16 * len(loads)))
                with pe.Fori(0, NCH // 2) as q:
                    for j in range(2):
                        n = q * 2 + j
                        pe.wait_ge(out_done.sem, out_done.at(n - 1))
                        for m in range(M1):
                            pe.wait_ge(squashed.sem, squashed.at(n * M1 + m + 1 - M1))
                            for k in range(kt):
                                mm = nc.tensor.matmul(ps[:, m, :], w1[0:rows, k, m * P:(m + 1) * P],
                                                      src[0:rows, k, tokens(q, j)], start=(k == 0), stop=(k == kt - 1))
                            mm.then_inc(hidden_done.sem, 1)
                    for j in range(2):
                        n = q * 2 + j
                        pe.wait_ge(squashed.sem, squashed.at((n + 1) * M1))
                        before = third_moved if third else moved
                        pe.wait_ge(before.sem, before.at(n - 1))
                        for mo in range(out_tiles):
                            for m in range(M1):
                                mm = nc.tensor.matmul(ps[0:out_rows, 4 + j * 2 + mo, :],
                                                      w2[:, m, mo * out_rows:(mo + 1) * out_rows], hid[:, j, m, :],
                                                      start=(m == 0), stop=(m == M1 - 1))
                        mm.then_inc(out_done.sem, 1)
                        if third:
                            pe.wait_ge(moved.sem, moved.at(n + 1))
                            nc.tensor.matmul(ps[0:out_rows, 5 + j * 2, :], w3[0:out_rows, 0:out_rows],
                                             dst[0:out_rows, 0, tokens(q, j)], start=True, stop=True).then_inc(third_done.sem, 1)

            @block.scalar
            def _(act):
                act.sem_inc(squashed.sem, squashed.credit)
                act.sem_inc(moved.sem, moved.credit)
                act.sem_inc(third_moved.sem, third_moved.credit)
                act.wait_ge(loaded.sem, loaded.at(16 * len(loads)))
                with act.Fori(0, NCH // 2) as q:
                    for j in range(2):
                        n = q * 2 + j
                        act.wait_ge(out_done.sem, out_done.at(n - 1))
                        for m in range(M1):
                            act.wait_ge(hidden_done.sem, hidden_done.at(n * M1 + m + 1))
                            nc.scalar.activation(hid[:, j, m, :], ps[:, m, :], ACT.Sigmoid,
                                                 bias=b1[:, m:m + 1]).then_inc(squashed.sem, 1)
                    for j in range(2):
                        n = q * 2 + j
                        act.wait_ge(out_done.sem, out_done.at(n + 1))
                        for mo in range(out_tiles):
                            ins = nc.scalar.activation(dst[0:out_rows, mo, tokens(q, j)], ps[0:out_rows, 4 + j * 2 + mo, :],
                                                       last_fn, bias=b2[0:out_rows, mo:mo + 1])
                        ins.then_inc(moved.sem, 1)
                        if third:
                            act.wait_ge(third_done.sem, third_done.at(n + 1))
                            nc.scalar.activation(third[2][0:out_rows, 0, tokens(q, j)], ps[0:out_rows, 5 + j * 2, :],
                                                 ACT.Relu, bias=b3[0:out_rows, 0:1]).then_inc(third_moved.sem, 1)
                        if parts:
                            nc.scalar.copy(parts[0][0:out_rows, :, tokens(q, j)],
                                           dst[0:out_rows, :, tokens(q, j)]).then_inc(split_high.sem, 1)

            @block.vector
            def _(dve):
                if parts:
                    with dve.Fori(0, NCH // 2) as q:
                        for j in range(2):
                            dve.wait_ge(split_high.sem, split_high.at(q * 2 + j + 1))
                            nc.vector.tensor_tensor(parts[1][0:out_rows, :, tokens(q, j)], dst[0:out_rows, :, tokens(q, j)],
                                                    parts[0][0:out_rows, :, tokens(q, j)].bitcast(F32), ALU.subtract)


def mixture_buffers(core, name, stack):
    gT = core.sbuf(name + "_gateT", [E, T], stack=stack)
    return gT, core.nc.dram_tensor(name + "_gate_dram", (E, T), F32).ap()


def stage_L0_ffn(core, name, w, a):
    with ExitStack() as stack:
        gT, gate_dram = mixture_buffers(core, name, stack)
        layernorm(core, name + "_ln", core.x, core.xn)
        gate(core, name + "_gate", core.xn, P, w["gate_w"], w["gate_b"], "threshold", gT, gate_dram)
        experts(core, name, "linear", w, gT, gate_dram, core.xn)


def stage_L1_ffn(core, name, w, a):
    F = w["pre_w2"].shape[1]
    with ExitStack() as stack:
        gT, gate_dram = mixture_buffers(core, name, stack)
        cont = core.sbuf(name + "_cont", [P, 1, T], stack=stack)
        router = core.sbuf(name + "_router", [P, 1, T], stack=stack)
        parts = [core.sbuf(name + f"_cont_{p}", [P, 1, T], F32R, stack) for p in ("high", "low")]
        layernorm(core, name + "_ln", core.x, core.xn)
        two_layers(core, name + "_pre", {k[4:]: v for k, v in w.items() if k.startswith("pre_")}, core.xn, P, cont, F, 1,
                   ACT.Identity, parts, (w["r_w1"], w["r_b1"], router))
        gate(core, name + "_gate", router, F, w["r_w2"], w["r_b2"], "top2", gT, gate_dram)
        experts(core, name, "mlp", w, gT, gate_dram, cont, parts, rows=F, hidden=w["w1"].shape[2], out_rows=F, out_tiles=1,
                act_fn=ACT.Relu, store=cont)
        two_layers(core, name + "_post", {k[5:]: v for k, v in w.items() if k.startswith("post_")}, cont, F, core.xn, P, KT,
                   ACT.Sigmoid)
        layernorm(core, name + "_out", core.xn, core.x, affine=(w["ln_g"], w["ln_b"]))


def stage_L2_ffn(core, name, w, a):
    with ExitStack() as stack:
        gT, gate_dram = mixture_buffers(core, name, stack)
        layernorm(core, name + "_ln", core.x, core.xn)
        gate(core, name + "_gate", core.xn, P, w["gate_w"], None, "top2_raw", gT, gate_dram, w["expert_bias"])
        experts(core, name, "swiglu", w, gT, gate_dram, core.xn, hidden=w["w1"].shape[2], act_fn=ACT.Silu)


def stage_L3_ffn(core, name, w, a):
    with ExitStack() as stack:
        gT, gate_dram = mixture_buffers(core, name, stack)
        parts = [core.sbuf(name + f"_x_{p}", [P, KT, T], F32R, stack) for p in ("high", "low")]
        layernorm(core, name + "_ln", core.x, core.xn, parts=parts)
        gate(core, name + "_gate", core.xn, P, w["Wg"], w["bg"], "top2_eps", gT, gate_dram)
        experts(core, name, "mlp", w, gT, gate_dram, core.xn, parts, hidden=w["w1"].shape[2], act_fn=ACT.Gelu, store=core.xn)
        layernorm(core, name + "_out", core.xn, core.x, affine=(w["gamma"], w["beta"]))


def lay_out_mixtures(a, n):
    def hidden_bias(b):
        return b.reshape(E, -1, P).transpose(2, 0, 1)

    for k in ("gate_w", "gate_b"):
        a[f"L0_ffn_{k}"] = n[f"L0_ffn_{k}"]
    a["L0_ffn_w2"], a["L0_ffn_b2"] = n["L0_ffn_expert_w"], n["L0_ffn_expert_b"]

    p = "L1_ffn_"
    a[p + "pre_w1"], a[p + "pre_b1"] = n[p + "enc_w"], by_partition(n[p + "enc_b"])
    def filled(t, *axes):
        return np.pad(t, [(0, P - t.shape[i]) if i in axes else (0, 0) for i in range(t.ndim)])

    a[p + "pre_w2"], a[p + "pre_b2"] = filled(n[p + "s2c_w"], 1), filled(n[p + "s2c_b"], 0).reshape(-1, 1)
    a[p + "r_w1"], a[p + "r_b1"] = filled(n[p + "r_w1"], 0, 1), filled(n[p + "r_b1"], 0).reshape(-1, 1)
    a[p + "r_w2"], a[p + "r_b2"] = filled(n[p + "r_w2"], 0), n[p + "r_b2"]
    a[p + "w1"], a[p + "b1"] = filled(n[p + "e_w1"], 1), hidden_bias(n[p + "e_b1"])
    a[p + "w2"], a[p + "b2"] = filled(n[p + "e_w2"], 2), filled(n[p + "e_b2"], 1)
    a[p + "post_w1"], a[p + "post_b1"] = filled(n[p + "c2s_w"], 0), by_partition(n[p + "c2s_b"])
    a[p + "post_w2"], a[p + "post_b2"] = n[p + "dec_w"], by_partition(n[p + "dec_b"])
    a[p + "ln_g"], a[p + "ln_b"] = by_partition(n[p + "ln_g"]), by_partition(n[p + "ln_b"])

    p = "L2_ffn_"
    short = -n[p + "w1"].shape[2] % P
    a[p + "gate_w"], a[p + "expert_bias"] = n[p + "gate_w"].T, n[p + "expert_bias"]
    a[p + "w1"] = np.pad(n[p + "w1"], ((0, 0), (0, 0), (0, short)))
    a[p + "w3"] = np.pad(n[p + "w3"], ((0, 0), (0, 0), (0, short)))
    a[p + "w2"] = np.pad(n[p + "w2"], ((0, 0), (0, short), (0, 0)))

    p = "L3_ffn_"
    a[p + "Wg"], a[p + "bg"] = n[p + "Wg"], n[p + "bg"]
    a[p + "w1"], a[p + "b1"] = n[p + "W1"], hidden_bias(n[p + "b1"])
    a[p + "w2"], a[p + "b2"] = n[p + "W2"], n[p + "b2"]
    a[p + "gamma"], a[p + "beta"] = by_partition(n[p + "gamma"]), by_partition(n[p + "beta"])


def linear_attention(core, name, w):
    nc = core.nc
    ps = core.psum
    NG = H // 4
    F = 2 * HD
    VC = HD + 1
    BR = 2
    with Stage(core, name) as st:
        wt = {c: st.buf("w" + c, [P, KT, D]) for c in "qkvo"}
        bt = {c: st.buf("b" + c, [P, D]) for c in "qkv"}
        bo = st.buf("bo", [P, KT])
        angle = st.buf("sin_cos", [P, TB, 2])
        xb = st.buf("tokens", [P, 2, KT, S])
        qk = st.buf("qk", [P, 2, TB, 2 * D])
        mx = st.buf("max", [P, TB, 2 * H])
        total = st.buf("total", [P, TB, 2 * H])
        feat = st.buf("features", [P, TB, 2, BR, H, F])
        v = st.buf("v", [P, TB, H, VC])
        kv = st.buf("kv", [P, BR * NG, 4, VC])
        qfT = st.buf("q_featuresT", [P, BR * NG, S])
        z = st.buf("z", [P, BR, TB, H])
        part = st.buf("branch", [P, BR, TB, D])
        y = st.buf("y", [P, TB, D])
        yT = st.buf("yT", [P, KT, S])
        loaded, copied, projected = st.count("loaded"), st.count("copied"), st.count("projected")
        biased, shifted, exped, featured = (st.count(k) for k in ("biased", "shifted", "exped", "featured"))
        kv_done, kv_moved, qf_turned, qf_moved = (st.count(k) for k in ("kv_done", "kv_moved", "qf_turned", "qf_moved"))
        attended, summed, y_turned, y_moved = (st.count(k) for k in ("attended", "summed", "y_turned", "y_moved"))
        out_done, added = st.count("out_done"), st.count("added", 1)
        chain = st.chain("chain")
        xn = core.xn[:].rearrange("p k (b s) -> p k b s", b=B)
        x = core.x[:].rearrange("p k (s b) -> p k b s", b=B)
        loads = [(wt[c][:], w["W" + c].rearrange("(k p) n -> p k n", p=P)) for c in "qkvo"]
        loads += [(bt[c][:], w["b" + c].rearrange("(o n) -> o n", o=1).to_broadcast([P, D])) for c in "qkv"]
        loads += [(bo[:], w["bo"]), (angle[:], w["sin_cos"])]
        with nc.Block() as block:

            @block.sync
            def _(sp):
                for to, of in loads:
                    sp.dma_start(to, of).then_inc(loaded.sem, 16)
                sp.wait_ge(loaded.sem, loaded.at(16 * len(loads)))

            @block.tensor
            def _(pe):
                pe.wait_ge(loaded.sem, loaded.at(16 * len(loads)))
                with pe.Fori(0, B // 2) as i:
                    for j in range(2):
                        n = i * 2 + j
                        pe.wait_ge(copied.sem, copied.at(n + 1))
                        pe.wait_ge(added.sem, added.at(n))
                        for t in range(TB):
                            for o, c in ((0, "q"), (D, "k")):
                                for k in range(KT):
                                    nc.tensor.matmul(ps[:, t, o:o + D], xb[:, j, k, t * P:(t + 1) * P], wt[c][:, k, :],
                                                     start=(k == 0), stop=(k == KT - 1))
                        for t in range(TB):
                            for k in range(KT):
                                mm = nc.tensor.matmul(ps[:, 2, t * D:(t + 1) * D], xb[:, j, k, t * P:(t + 1) * P],
                                                      wt["v"][:, k, :], start=(k == 0), stop=(k == KT - 1))
                        mm.then_inc(projected.sem, 1)
                        pe.wait_ge(featured.sem, featured.at(n + 1))
                        for br in range(BR):
                            for g in range(NG):
                                for t in range(TB):
                                    mm = nc.tensor.matmul(ps[:, 4 + br, g * 4 * VC:(g + 1) * 4 * VC],
                                                          feat[:, t, 1, br, g * 4:(g + 1) * 4, :].rearrange("p h f -> p (h f)"),
                                                          v[:, t, g * 4:(g + 1) * 4, :].rearrange("p h c -> p (h c)"),
                                                          start=(t == 0), stop=(t == TB - 1))
                        mm.then_inc(kv_done.sem, 1)
                        for br in range(BR):
                            for g in range(NG):
                                for t in range(TB):
                                    o = br * NG + g
                                    mm = nc.tensor.transpose(ps[:, o // 2, (o % 2) * S + t * P:(o % 2) * S + (t + 1) * P],
                                                             feat[:, t, 0, br, g * 4:(g + 1) * 4, :].rearrange("p h f -> p (h f)"),
                                                             core.ident[:])
                        mm.then_inc(qf_turned.sem, 1)
                        pe.wait_ge(kv_moved.sem, kv_moved.at(n + 1))
                        pe.wait_ge(qf_moved.sem, qf_moved.at(n + 1))
                        for br in range(BR):
                            for t in range(TB):
                                bank = (6 if br == 0 else 4) + t
                                for g in range(NG):
                                    o = br * NG + g
                                    mm = nc.tensor.matmul(ps[:, bank, g * 4 * VC:(g + 1) * 4 * VC],
                                                          qfT[:, o, t * P:(t + 1) * P],
                                                          kv[:, o].rearrange("p h c -> p (h c)"), start=True, stop=True)
                        mm.then_inc(attended.sem, 1)
                        pe.wait_ge(summed.sem, summed.at(n + 1))
                        for c in range(KT):
                            for t in range(TB):
                                mm = nc.tensor.transpose(ps[:, 0, c * S + t * P:c * S + (t + 1) * P],
                                                         y[:, t, c * P:(c + 1) * P], core.ident[:])
                        mm.then_inc(y_turned.sem, 1)
                        pe.wait_ge(y_moved.sem, y_moved.at(n + 1))
                        for m in range(KT):
                            for k in range(KT):
                                mm = nc.tensor.matmul(ps[:, 1, m * S:(m + 1) * S], wt["o"][:, k, m * P:(m + 1) * P],
                                                      yT[:, k, :], start=(k == 0), stop=(k == KT - 1))
                        mm.then_inc(out_done.sem, 1)

            @block.scalar
            def _(act):
                with act.Fori(0, B // 2) as i:
                    for j in range(2):
                        n = i * 2 + j
                        nc.scalar.copy(xb[:, j], xn[:, :, n, :]).then_inc(copied.sem, 1)
                        act.wait_ge(shifted.sem, shifted.at(n + 1))
                        nc.scalar.activation(qk[:, 0], qk[:, 0], ACT.Exp).then_inc(exped.sem, 1)
                        act.wait_ge(qf_turned.sem, qf_turned.at(n + 1))
                        nc.scalar.copy(qfT[:].rearrange("p (a b) s -> p a (b s)", b=2), ps[:, 0:4, :]).then_inc(qf_moved.sem, 1)
                        act.wait_ge(y_turned.sem, y_turned.at(n + 1))
                        nc.scalar.copy(yT[:], ps[:, 0, :].rearrange("p (c s) -> p c s", c=KT)).then_inc(y_moved.sem, 1)

            @block.vector
            def _(dve):
                dve.sem_inc(added.sem, added.credit)
                chain.link(dve, nc.vector.memset(kv[:], 0.0))
                chain.link(dve, nc.vector.memset(v[:], 1.0))
                dve.wait_ge(loaded.sem, loaded.at(16 * len(loads)))
                with dve.Fori(0, B // 2) as i:
                    chain.restart(dve)
                    for j in range(2):
                        n = i * 2 + j

                        def link(ins):
                            chain.link(dve, ins)

                        dve.wait_ge(projected.sem, projected.at(n + 1))
                        cur = qk[:, 0].rearrange("p t (h d) -> p t h d", d=HD)
                        for t in range(TB):
                            for o, c in ((0, "q"), (D, "k")):
                                nc.vector.tensor_tensor(qk[:, 0, t, o:o + D], ps[:, t, o:o + D], bt[c][:], ALU.add)
                            ins = nc.vector.tensor_tensor(v[:, t, :, 0:HD],
                                                          ps[:, 2, t * D:(t + 1) * D].rearrange("p (h d) -> p h d", d=HD),
                                                          bt["v"][:].rearrange("p (h d) -> p h d", d=HD), ALU.add)
                        link(ins)
                        rows = qk[:, 0].rearrange("p t (h d) -> p (t h) d", d=HD)

                        def over_channels(s):
                            return s[:].rearrange("p t (h o) -> p (t h) o", o=1).to_broadcast([P, TB * 2 * H, HD])

                        link(nc.vector.tensor_reduce(mx[:].rearrange("p t h -> p (t h)"), rows, AX.X, ALU.max))
                        nc.vector.tensor_tensor(rows, rows, over_channels(mx), ALU.subtract).then_inc(shifted.sem, 1)
                        dve.wait_ge(exped.sem, exped.at(n + 1))
                        link(nc.vector.tensor_reduce(total[:].rearrange("p t h -> p (t h)"), rows, AX.X, ALU.add))
                        link(nc.vector.reciprocal(total[:], total[:]))
                        link(nc.vector.tensor_tensor(rows, rows, over_channels(total), ALU.mult))
                        link(nc.vector.tensor_scalar(qk[:, 1], qk[:, 0], -1.0, 1.0, ALU.mult, ALU.add))
                        for t in range(TB):
                            for which in range(2):
                                for br in range(BR):
                                    src = qk[:, br, t, which * D:(which + 1) * D].rearrange("p (h d) -> p h d", d=HD)
                                    for f in range(2):
                                        ins = nc.vector.tensor_scalar(feat[:, t, which, br, :, f * HD:(f + 1) * HD], src,
                                                                      angle[:, t, f:f + 1], None, ALU.mult)
                        ins.then_inc(featured.sem, 1)
                        dve.wait_ge(kv_done.sem, kv_done.at(n + 1))
                        for br in range(BR):
                            for hh in range(4):
                                r = slice(hh * F, (hh + 1) * F)
                                src = ps[r, 4 + br, 0:NG * 4 * VC].rearrange("p (g h c) -> p g h c", g=NG, c=VC)[:, :, hh, :]
                                ins = nc.vector.tensor_copy(kv[r, br * NG:(br + 1) * NG, hh, :], src)
                        ins.then_inc(kv_moved.sem, 1)
                        dve.wait_ge(attended.sem, attended.at(n + 1))
                        for br in range(BR):
                            for t in range(TB):
                                bank = (6 if br == 0 else 4) + t
                                res = ps[:, bank, 0:H * VC].rearrange("p (h c) -> p h c", c=VC)
                                ins = nc.vector.tensor_scalar(z[:, br, t, :], res[:, :, HD], 1e-6, None, ALU.max)
                        link(ins)
                        link(nc.vector.reciprocal(z[:], z[:]))
                        for br in range(BR):
                            for t in range(TB):
                                bank = (6 if br == 0 else 4) + t
                                res = ps[:, bank, 0:H * VC].rearrange("p (h c) -> p h c", c=VC)
                                ins = nc.vector.tensor_tensor(part[:, br, t, :].rearrange("p (h d) -> p h d", d=HD),
                                                              res[:, :, 0:HD],
                                                              z[:, br, t, :].rearrange("p (h o) -> p h o", o=1).to_broadcast([P, H, HD]),
                                                              ALU.mult)
                        link(ins)
                        nc.vector.tensor_tensor(y[:], part[:, 0], part[:, 1], ALU.add).then_inc(summed.sem, 1)
                        dve.wait_ge(out_done.sem, out_done.at(n + 1))
                        for m in range(KT):
                            ins = nc.vector.scalar_tensor_tensor(out=x[:, m, n, :], in0=ps[:, 1, m * S:(m + 1) * S],
                                                                 scalar=bo[:, m:m + 1], in1=x[:, m, n, :],
                                                                 op0=ALU.add, op1=ALU.add)
                        ins.then_inc(added.sem, 1)


def memory_filter(core, name, w):
    nc = core.nc
    ps = core.psum
    PAD = TAPS - 1
    with Stage(core, name) as st:
        w1, w2 = st.buf("w1", [P, KT, D]), st.buf("w2", [P, KT, D])
        b1, b2 = st.buf("b1", [P, KT]), st.buf("b2", [P, KT])
        taps = st.buf("taps", [P, KT, TAPS + 1])
        tap_diff = st.buf("tap_diff", [P, KT, TAPS])
        p = st.buf("projected", [P, KT, B, PAD + S])
        acc = st.buf("filtered", [P, KT, B, S])
        total = st.buf("total", [P, KT, B])
        loaded, padded = st.count("loaded"), st.count("padded")
        proj_done, moved, filtered = st.count("proj_done"), st.count("moved", 4), st.count("filtered")
        out_done, added, chain = st.count("out_done"), st.count("added", 4), st.chain("chain")
        x = core.x
        loads = [(w1[:], w["W1"].rearrange("(k p) n -> p k n", p=P)), (w2[:], w["W2"].rearrange("(k p) n -> p k n", p=P)),
                 (b1[:], w["bias1"]), (b2[:], w["bias2"]), (taps[:], w["taps"])]
        with nc.Block() as block:

            @block.sync
            def _(sp):
                for to, of in loads:
                    sp.dma_start(to, of).then_inc(loaded.sem, 16)
                sp.wait_ge(loaded.sem, loaded.at(16 * len(loads)))

            @block.tensor
            def _(pe):
                pe.wait_ge(loaded.sem, loaded.at(16 * len(loads)))
                for m in range(KT):
                    for c in range(NCH):
                        n = m * NCH + c
                        if n >= 4:
                            pe.wait_ge(moved.sem, moved.at(n + 1 - 4))
                        for k in range(KT):
                            mm = nc.tensor.matmul(ps[:, n % 4, :], w1[:, k, m * P:(m + 1) * P], core.xn[:, k, c * CH:(c + 1) * CH],
                                                  start=(k == 0), stop=(k == KT - 1))
                        mm.then_inc(proj_done.sem, 1)
                pe.wait_ge(filtered.sem, filtered.at(1))
                for c in range(NCH):
                    for m in range(KT):
                        n = c * KT + m
                        if n >= 4:
                            pe.wait_ge(added.sem, added.at(n + 1 - 4))
                        for k in range(KT):
                            mm = nc.tensor.matmul(ps[:, 4 + n % 4, :], w2[:, k, m * P:(m + 1) * P],
                                                  acc[:, k].rearrange("p b s -> p (b s)")[:, c * CH:(c + 1) * CH],
                                                  start=(k == 0), stop=(k == KT - 1))
                        mm.then_inc(out_done.sem, 1)

            @block.scalar
            def _(act):
                act.sem_inc(moved.sem, moved.credit)
                act.wait_ge(loaded.sem, loaded.at(16 * len(loads)))
                for m in range(KT):
                    for c in range(NCH):
                        n = m * NCH + c
                        act.wait_ge(proj_done.sem, proj_done.at(n + 1))
                        bs = slice(c * CH // S, (c + 1) * CH // S)
                        nc.scalar.activation(p[:, m, bs, PAD:], ps[:, n % 4, :].rearrange("p (b s) -> p b s", s=S),
                                             ACT.Identity, bias=b1[:, m:m + 1]).then_inc(moved.sem, 1)

            @block.vector
            def _(dve):
                dve.sem_inc(added.sem, added.credit)
                for m in range(KT):
                    chain.link(dve, nc.vector.memset(p[:, m, :, 0:PAD], 0.0))
                dve.wait_ge(loaded.sem, loaded.at(16 * len(loads)))
                for m in range(KT):
                    chain.link(dve, nc.vector.tensor_scalar(tap_diff[:, m, :], taps[:, m, 1:], taps[:, m, 0:1], None, ALU.subtract))
                for m in range(KT):
                    dve.wait_ge(moved.sem, moved.at((m + 1) * NCH))
                    chain.link(dve, nc.vector.tensor_reduce(total[:, m, :], p[:, m, :, PAD:], AX.X, ALU.add))
                    chain.link(dve, nc.vector.tensor_scalar(total[:, m, :], total[:, m, :], taps[:, m, 0:1], None, ALU.mult))
                    chain.link(dve, nc.vector.scalar_tensor_tensor(
                        out=acc[:, m], in0=p[:, m, :, PAD:], scalar=tap_diff[:, m, 0:1],
                        in1=total[:, m, :].rearrange("p (b o) -> p b o", o=1).to_broadcast([P, B, S]),
                        op0=ALU.mult, op1=ALU.add))
                    for tap in range(1, TAPS):
                        ins = nc.vector.scalar_tensor_tensor(
                            out=acc[:, m], in0=p[:, m, :, PAD - tap:PAD - tap + S], scalar=tap_diff[:, m, tap:tap + 1],
                            in1=acc[:, m], op0=ALU.mult, op1=ALU.add)
                        if tap == TAPS - 1 and m == KT - 1:
                            ins.then_inc(filtered.sem, 1)
                        else:
                            chain.link(dve, ins)
                for c in range(NCH):
                    for m in range(KT):
                        n = c * KT + m
                        dve.wait_ge(out_done.sem, out_done.at(n + 1))
                        dst = x[:, m, c * CH:(c + 1) * CH]
                        nc.vector.scalar_tensor_tensor(out=dst, in0=ps[:, 4 + n % 4, :], scalar=b2[:, m:m + 1], in1=dst,
                                                       op0=ALU.add, op1=ALU.add).then_inc(added.sem, 1)


def stage_L1_attn(core, name, w, a):
    layernorm(core, name + "_ln", core.x, core.xn)
    linear_attention(core, name, w)


def stage_L2_attn(core, name, w, a):
    layernorm(core, name + "_ln", core.x, core.xn)
    memory_filter(core, name, w)


def lay_out_others(a, n):
    for c in "qkvo":
        a[f"L1_attn_W{c}"] = n[f"L1_attn_W{c}"]
    for c in "qkv":
        a[f"L1_attn_b{c}"] = n[f"L1_attn_b{c}"]
    a["L1_attn_bo"] = by_partition(n["L1_attn_bo"])
    index = np.float32(np.pi / 2) * np.arange(1, S + 1, dtype=np.float32) / np.float32(S)
    a["L1_attn_sin_cos"] = np.stack([np.sin(index), np.cos(index)], -1).astype(np.float32).reshape(TB, P, 2).transpose(1, 0, 2)
    p = "L2_attn_"
    a[p + "W1"], a[p + "W2"] = n[p + "W1"], n[p + "W2"]
    a[p + "bias1"], a[p + "bias2"] = by_partition(n[p + "bias1"]), by_partition(n[p + "bias2"])
    a[p + "taps"] = n[p + "memory_weights"].T.reshape(KT, P, TAPS + 1).transpose(1, 0, 2)


STAGES = ["L0_attn", "L0_xattn", "L0_ffn", "L1_attn", "L1_xattn", "L1_ffn",
          "L2_attn", "L2_xattn", "L2_ffn", "L3_attn", "L3_xattn", "L3_ffn"]


def build(nc, a, out, stages=STAGES):
    with ExitStack() as stack:
        core = Core(nc, stack)
        load_inputs(core, a)
        for name in stages:
            layer, part = name.split("_")
            w = {k[len(name) + 1:]: v for k, v in a.items() if k.startswith(name + "_")}
            STAGE[name](core, name, w, a)
        store_output(core, out)


def stage_L0_attn(core, name, w, a):
    layernorm(core, name + "_ln", core.x, core.xn)
    relative_attention(core, name, w)


def stage_L0_xattn(core, name, w, a):
    layernorm(core, name + "_ln", core.x, core.xn)
    attention(core, name, w, kv="ctx")


def stage_L1_xattn(core, name, w, a):
    layernorm(core, name + "_ln", core.x, core.xn)
    attention(core, name, w, kv="ctx", mask=a["mask_1x1xSxS2_if1"])


def stage_L2_xattn(core, name, w, a):
    layernorm(core, name + "_ln", core.x, core.xn)
    attention(core, name, w, kv="ctx", project=False)


def stage_L3_attn(core, name, w, a):
    layernorm(core, name + "_ln", core.x, core.xn)
    attention(core, name, w)


STAGE = {
    "L0_attn": stage_L0_attn, "L0_xattn": stage_L0_xattn,
    "L1_xattn": stage_L1_xattn, "L2_xattn": stage_L2_xattn,
    "L3_attn": stage_L3_attn, "L3_xattn": stage_L0_xattn,
    "L1_attn": stage_L1_attn, "L2_attn": stage_L2_attn,
    "L0_ffn": stage_L0_ffn, "L1_ffn": stage_L1_ffn, "L2_ffn": stage_L2_ffn, "L3_ffn": stage_L3_ffn,
}


def padded_heads(weight):
    heads = weight.reshape(weight.shape[:-1] + (H, HD))
    pads = [(0, 0)] * (heads.ndim - 1) + [(0, HB - HD)]
    return np.pad(heads, pads).reshape(weight.shape[:-1] + (H * HB,))


def by_partition(v):
    return np.ascontiguousarray(v.reshape(-1, P).T)


def lay_out(x):
    a = {}
    n = {k: np.asarray(v) for k, v in x.items()}
    a["xT"] = n["x"].reshape(T, D).T
    a["ctxT"] = n["ctx_1024"].reshape(B * SC, D).T
    a["identity"] = np.eye(P, dtype=np.float32)
    a["earlier"] = np.tril(np.ones((E, E), np.float32), -1)
    a["mask_1x1xSxS2_if1"] = n["mask_1x1xSxS2_if1"]
    qkv = n["L0_attn_w_attn"]
    names = {
        "L0_attn": (qkv[:, :D], qkv[:, D:2 * D], qkv[:, 2 * D:], n["L0_attn_w_proj"], None),
        "L0_xattn": tuple(n[f"L0_xattn_w_{c}"].T for c in "qkvo") + (None,),
        "L1_xattn": tuple(n[f"L1_xattn_W_{c}"].T for c in "qkvo") + (None,),
        "L2_xattn": tuple(n[f"L2_xattn_W{c}"].T for c in "qkv") + (None, "L2_xattn_b"),
        "L3_attn": tuple(n[f"L3_attn_W{c}"] for c in "qkvo") + ("L3_attn_b",),
        "L3_xattn": tuple(n[f"L3_xattn_w{c}"].T for c in "qkvo") + ("L3_xattn_b",),
    }
    for name, (wq, wk, wv, wo, biases) in names.items():
        a[f"{name}_wq"], a[f"{name}_wk"], a[f"{name}_wv"] = padded_heads(wq), padded_heads(wk), wv
        if wo is not None:
            a[f"{name}_wo"] = wo
        if biases:
            a[f"{name}_bq"] = by_partition(padded_heads(n[f"{biases}q"]))
            a[f"{name}_bk"] = by_partition(padded_heads(n[f"{biases}k"]))
            a[f"{name}_bv"] = by_partition(n[f"{biases}v"])
            if wo is not None:
                a[f"{name}_bo"] = by_partition(n[f"{biases}o"])
    t, s = np.arange(P)[:, None], np.arange(S)[None, :]
    mask = np.concatenate([np.where(s[:, :P] <= t, 0.0, NEG), np.where(s <= t + P, 0.0, NEG)], 1)
    a["L0_attn_causal"] = mask.astype(np.float32)
    slopes = np.array([0.5 ** ((i + 1) * 8 / H) for i in range(H)])
    keys = np.concatenate([np.arange(P), np.arange(S)])
    alibi = -slopes[:, None] * (S - 1 - keys)[None, :]
    a["L3_attn_bias"] = (alibi[None] + mask[:, None, :]).astype(np.float32)
    a["L0_attn_embkT"] = np.pad(n["L0_attn_embk"][::-1].T, ((0, HB - HD), (0, 0)))
    a["L0_attn_embv"] = n["L0_attn_embv"][::-1].reshape(TB, P, HD).transpose(1, 0, 2)
    lay_out_mixtures(a, n)
    lay_out_others(a, n)
    return {k: np.ascontiguousarray(v) for k, v in a.items()}


def kernel(**inputs):
    import concourse.bacc as _bacc
    from concourse.bass_utils import run_bass_kernel_spmd as _run

    nc = _bacc.Bacc("TRN2", target_bir_lowering=False, num_devices=1)
    arrays = lay_out(inputs)
    args = {k: nc.dram_tensor(f"in_{k}", v.shape, mybir.dt.from_np(v.dtype), kind="ExternalInput").ap()
            for k, v in arrays.items()}
    out = nc.dram_tensor("out_xT", (D, T), F32, kind="ExternalOutput").ap()
    build(nc, args, out)
    r = _run(nc, [{f"in_{k}": v for k, v in arrays.items()}], core_ids=[0])
    got = r.results[0]["out_xT"]
    return np.ascontiguousarray(got.T).reshape(B, S, D)
```

```python
from contextlib import ExitStack

import numpy as np
import concourse.bass as bass
from concourse import mybir

ALU = mybir.AluOpType
ACT = mybir.ActivationFunctionType
AX = mybir.AxisListType
F32 = mybir.dt.float32
F32R = mybir.dt.float32r
I32 = mybir.dt.int32

P = 128
B, S, D = 8, 256, 256
T = B * S
KT = D // P
H, HD = 16, 16
QB = D // P
HB = P // HD
VP = P + HD
TB = S // P
SC = 77
E = 8
CH = 512
NCH = T // CH
HALF = T // 2
NEG = -1.0e30
LN_EPS = 1e-5
SEMAPHORES = 120
TAPS = 40


class Count:

    def __init__(self, core, name, credit=None):
        self.sem = core.semaphore(name)
        self.credit = credit + 1 if credit is not None else 0

    def at(self, events):
        return events + self.credit


class Chain:

    def __init__(self, core, name):
        self.sem = core.semaphore(name)
        self.n = 0

    def restart(self, engine):
        engine.sem_clear(self.sem)
        self.n = 0

    def link(self, engine, instruction):
        instruction.then_inc(self.sem, 1)
        self.n += 1
        engine.wait_ge(self.sem, self.n)

    def mark(self, instruction):
        instruction.then_inc(self.sem, 1)
        self.n += 1
        return self.n


class Core:

    def __init__(self, nc, stack):
        self.nc = nc
        self.stack = stack
        self.free_semaphores = sorted(nc.free_semaphores)[:SEMAPHORES]
        self.x = self.sbuf("x_residual", [P, KT, T])
        self.xn = self.sbuf("x_normed", [P, KT, T])
        self.ctx = self.sbuf("context", [P, KT, B * SC])
        self.ident = self.sbuf("identity", [P, P])
        self.mean_w = self.sbuf("mean_weights", [P, P])
        self.eps = self.sbuf("ln_eps", [P, 1])
        self.key_scale = self.sbuf("key_scale", [P, HB])
        self.tri = self.sbuf("earlier_expert", [P, E, E])
        self.psum = stack.enter_context(nc.psum_tensor("psum", [P, 8, CH], F32))

    def sbuf(self, name, shape, dtype=F32, stack=None):
        return (stack or self.stack).enter_context(self.nc.sbuf_tensor(name, shape, dtype))


class Stage:

    def __init__(self, core, name):
        self.nc, self.core, self.name = core.nc, core, name
        self.stack = ExitStack()
        self.semaphores = []

    def __enter__(self):
        return self

    def __exit__(self, *failure):
        self.nc.clear_and_free_semaphores(self.semaphores)
        self.core.free_semaphores.extend(s.num for s in self.semaphores)
        return self.stack.__exit__(*failure)

    def semaphore(self, name):
        self.semaphores.append(self.nc.alloc_semaphore(name, num=self.core.free_semaphores.pop(0)))
        return self.semaphores[-1]

    def buf(self, name, shape, dtype=F32):
        return self.stack.enter_context(self.nc.sbuf_tensor(f"{self.name}_{name}", shape, dtype))

    def count(self, name, credit=None):
        return Count(self, f"{self.name}_{name}", credit)

    def chain(self, name):
        return Chain(self, f"{self.name}_{name}")


def load_inputs(core, a):
    with Stage(core, "load") as st:
        nc = core.nc
        loaded = st.count("loaded")
        with nc.Block() as block:

            @block.sync
            def _(sp):
                sp.dma_start(core.x[:], a["xT"].rearrange("(k p) t -> p k t", p=P)).then_inc(loaded.sem, 16)
                sp.dma_start(core.ident[:], a["identity"]).then_inc(loaded.sem, 16)
                sp.dma_start(core.key_scale[:], a["key_scale"]).then_inc(loaded.sem, 16)
                sp.dma_start(core.tri[:], a["earlier"].rearrange("(o e) f -> o e f", o=1).to_broadcast([P, E, E])).then_inc(loaded.sem, 16)
                sp.dma_start(core.ctx[:], a["ctxT"].rearrange("(k p) t -> p k t", p=P)).then_inc(loaded.sem, 16)
                sp.wait_ge(loaded.sem, loaded.at(80))

            @block.vector
            def _(dve):
                nc.vector.memset(core.mean_w[:], 1.0 / D)
                nc.vector.memset(core.eps[:], LN_EPS)


def store_output(core, out):
    with Stage(core, "store") as st:
        stored = st.count("stored")
        with core.nc.Block() as block:

            @block.sync
            def _(sp):
                sp.dma_start(out.rearrange("(k p) t -> p k t", p=P), core.x[:]).then_inc(stored.sem, 16)
                sp.wait_ge(stored.sem, stored.at(16))


def layernorm(core, name, src, dst, affine=None, parts=None, preload=()):
    nc = core.nc
    CT = CH // P
    with Stage(core, name) as st:
        centred = st.buf("centred", [P, KT, T]) if affine is not None else dst
        square = st.buf("square", [P, NCH, KT, CH])
        pair = st.buf("channel_tiles_added", [P, NCH, CH])
        pair_square = st.buf("squares_added", [P, NCH, CH])
        std = st.buf("std", [P, NCH, CT])
        rstd = st.buf("rstd", [P, NCH, CT])
        gb = st.buf("gamma_beta", [P, 2, KT])
        pair_done, pair_square_done = st.count("pair_done"), st.count("pair_square_done")
        mean_done, var_done, spread = st.count("mean_done"), st.count("var_done"), st.count("spread")
        centre_done, square_done = st.count("centre_done"), st.count("square_done")
        std_done, rstd_done, normed = st.count("std_done"), st.count("rstd_done"), st.count("normed")
        split_high, loaded, chain = st.count("split_high"), st.count("loaded"), st.chain("dve_chain")
        preloaded = st.count("preloaded")
        ps = core.psum
        MEAN, VAR = 0, 4

        def tokens(c):
            return slice(c * CH, (c + 1) * CH)

        with nc.Block() as block:

            @block.sync
            def _(sp):
                if affine is not None:
                    for n, v in enumerate(affine):
                        sp.dma_start(gb[:, n, :], v).then_inc(loaded.sem, 16)
                    sp.wait_ge(loaded.sem, loaded.at(32))
                for to, of in preload:
                    sp.dma_start(to, of).then_inc(preloaded.sem, 16)
                if preload:
                    sp.wait_ge(preloaded.sem, preloaded.at(16 * len(preload)))

            @block.tensor
            def _(pe):
                for c in range(NCH):
                    pe.wait_ge(pair_done.sem, pair_done.at(c + 1))
                    nc.tensor.matmul(ps[:, MEAN + c, :], core.mean_w[:], pair[:, c, :],
                                     start=True, stop=True).then_inc(mean_done.sem, 1)
                for c in range(NCH):
                    pe.wait_ge(pair_square_done.sem, pair_square_done.at(c + 1))
                    for t in range(CT):
                        mm = nc.tensor.matmul(ps[:, VAR + c, t:t + 1], pair_square[:, c, t * P:(t + 1) * P],
                                              core.mean_w[:, 0:1], start=True, stop=True)
                    mm.then_inc(var_done.sem, 1)
                for c in range(NCH):
                    pe.wait_ge(centre_done.sem, centre_done.at(c + 1))
                    pe.wait_ge(rstd_done.sem, rstd_done.at(c + 1))
                    for t in range(CT):
                        mm = nc.tensor.matmul(ps[:, MEAN + c, t * P:(t + 1) * P],
                                              rstd[:, c, t:t + 1].to_broadcast([P, P]), core.ident[:],
                                              start=True, stop=True)
                    mm.then_inc(spread.sem, 1)

            @block.scalar
            def _(act):
                for c in range(NCH):
                    act.wait_ge(centre_done.sem, centre_done.at(c + 1))
                    nc.scalar.activation(square[:, c], centred[:, :, tokens(c)], ACT.Square).then_inc(square_done.sem, 1)
                for c in range(NCH):
                    act.wait_ge(var_done.sem, var_done.at(c + 1))
                    nc.scalar.activation(std[:, c], ps[:, VAR + c, 0:CT], ACT.Sqrt,
                                         bias=core.eps[:, 0:1]).then_inc(std_done.sem, 1)
                if parts is not None:
                    for c in range(NCH):
                        act.wait_ge(normed.sem, normed.at(c + 1))
                        nc.scalar.activation(parts[0][:, :, tokens(c)], dst[:, :, tokens(c)],
                                             ACT.Copy).then_inc(split_high.sem, 1)

            @block.gpsimd
            def _(pool):
                for c in range(NCH):
                    pool.wait_ge(square_done.sem, square_done.at(c + 1))
                    nc.gpsimd.tensor_tensor(pair_square[:, c], square[:, c, 0], square[:, c, 1],
                                            ALU.add).then_inc(pair_square_done.sem, 1)
                if parts is not None:
                    for c in range(NCH):
                        pool.wait_ge(split_high.sem, split_high.at(c + 1))
                        nc.gpsimd.tensor_tensor(parts[1][:, :, tokens(c)], dst[:, :, tokens(c)],
                                                parts[0][:, :, tokens(c)].bitcast(F32), ALU.subtract)

            @block.vector
            def _(dve):
                for c in range(NCH):
                    nc.vector.tensor_tensor(pair[:, c], src[:, 0, tokens(c)], src[:, 1, tokens(c)],
                                            ALU.add).then_inc(pair_done.sem, 1)
                for c in range(NCH):
                    dve.wait_ge(mean_done.sem, mean_done.at(c + 1))
                    nc.vector.tensor_tensor(centred[:, :, tokens(c)], src[:, :, tokens(c)],
                                            ps[:, MEAN + c:MEAN + c + 1, :].to_broadcast([P, KT, CH]),
                                            ALU.subtract).then_inc(centre_done.sem, 1)
                if affine is not None:
                    dve.wait_ge(loaded.sem, loaded.at(32))
                for c in range(NCH):
                    dve.wait_ge(std_done.sem, std_done.at(c + 1))
                    nc.vector.reciprocal(rstd[:, c], std[:, c]).then_inc(rstd_done.sem, 1)
                for c in range(NCH):
                    dve.wait_ge(spread.sem, spread.at(c + 1))
                    dve.wait_ge(square_done.sem, square_done.at(c + 1))
                    scale = ps[:, MEAN + c:MEAN + c + 1, :].to_broadcast([P, KT, CH])
                    scaled = nc.vector.tensor_tensor(centred[:, :, tokens(c)], centred[:, :, tokens(c)], scale, ALU.mult)
                    if affine is None:
                        scaled.then_inc(normed.sem, 1)
                    else:
                        chain.link(dve, scaled)
                        for k in range(KT):
                            ins = nc.vector.tensor_scalar(centred[:, k, tokens(c)], centred[:, k, tokens(c)],
                                                          gb[:, 0, k:k + 1], gb[:, 1, k:k + 1], ALU.mult, ALU.add)
                        chain.link(dve, ins)
                        nc.vector.tensor_tensor(dst[:, :, tokens(c)], dst[:, :, tokens(c)], centred[:, :, tokens(c)],
                                                ALU.add).then_inc(normed.sem, 1)


def attention(core, name, w, kv="self", mask=None, project=True, rel=None):
    nc = core.nc
    ps = core.psum
    causal = kv == "self"
    PH = 1 if causal else 2
    NS = H // PH
    NK = S if causal else SC
    SEG = [(0, P), (P, S)] if causal else [(0, PH * SC), (PH * SC, PH * SC)]
    W = SEG[1][0] + SEG[1][1]
    KP = P if causal else SC
    SB = NK // P if causal else 1
    if causal:
        TR = [[(0, 0, 0), (P, 0, 1), (2 * P, 1, 1)]]
    else:
        TR = [[(t * PH * SC + i * SC, 0, t) for t in range(TB)] for i in range(PH)]
    TW = len(TR[0]) * P
    T_LAG, COPY_LAG, Y_LAG = 2, 3, 4
    NPROJ = 3
    PROJ_AT = [4, 7, 10] if causal else [3, 4, 5]
    EVAC_AT = [s + 1 for s in PROJ_AT]
    RECIP_AT, SPREAD_AT, NORM_AT, BIAS_AT = 1, 2, Y_LAG, Y_LAG + 1
    OUT_AT, ADD_AT = (8, 10) if causal else (6, 7)
    R = 4
    T_BANK, Y_BANK, P_BANK = 3, 5, 7
    PERIOD = 2 * NS
    S_BANK = [u % 3 for u in range(PERIOD)]
    if PERIOD % 3 == 1:
        S_BANK[-1] = 1
    S_AGO = [next(d for d in range(1, PERIOD) if S_BANK[(u - d) % PERIOD] == S_BANK[u]) for u in range(PERIOD)]

    with Stage(core, name) as st:
        wq = st.buf("wq", [P, KT, D])
        wk = st.buf("wk", [P, KT, D])
        wv = st.buf("wv", [P, KT, D])
        wo = st.buf("wo", [P, KT, D])
        bq = st.buf("bq", [P, QB])
        bk = st.buf("bk", [P, QB])
        bk_kept = st.buf("bk_kept", [P, HB, QB])
        bv = st.buf("bv", [P, KT])
        bo = st.buf("bo", [P, KT])
        xb = st.buf("tokens", [P, 2, KT, S])
        kvb = xb if causal else st.buf("ctx_tokens", [P, 2, KT, SC])
        q_sb = st.buf("q", [P, 2, QB, S])
        k_sb = st.buf("k", [P, 2, QB, HB, NK])
        v_sb = st.buf("v", [P, 2, SB, QB, HB * VP])
        s_sb = st.buf("scores", [P, R, W])
        top = st.buf("max", [P, R, PH * TB])
        p_sb = st.buf("probs", [P, R, W])
        pT = st.buf("probsT", [P, 2, PH * TW])
        sums = st.buf("sums", [P, 2, TB, H])
        rsum = st.buf("rsums", [P, TB, H])
        rsum_wide = st.buf("rsums_by_channel", [P, TB, D])
        divisor = st.buf("divisor", [P, KT, S])
        y_sb = st.buf("y", [P, 2, KT, S])
        yT = st.buf("yT", [P, 2, KT, S]) if "bv" in w else y_sb
        if causal:
            bias = st.buf("bias", [P, 2 if rel else 1, H, W])
            cmask = st.buf("causal", [P, W])
        if mask is not None:
            mask_i = st.buf("mask_int", [P, TB, SC], I32)
            mask_off = st.buf("mask_off", [P, TB, PH, SC])
            mask_on = st.buf("mask_on", [P, TB, PH, SC])
        copied, projected, evacuated = st.count("copied"), st.count("projected", 0), st.count("evacuated")
        scored = st.count("scored")
        taken = st.count("taken", PERIOD)
        ready = st.count("ready", PERIOD)
        exped, summed = st.count("exped", R), st.count("summed", R)
        transposed, turned = st.count("transposed", R), st.count("turned", 2)
        valued = st.count("valued", 2)
        widened, spread, spread_moved = st.count("widened", 1), st.count("spread"), st.count("spread_moved", 1)
        normed, y_biased, zeroed = st.count("normed"), st.count("y_biased"), st.count("v_zeroed")
        y_done = y_biased if "bv" in w else normed
        out_done, added = st.count("out_done"), st.count("added", 2)
        step_on = st.count("step_on").sem
        bias_in, bias_used = [st.count(f"bias_in{j}") for j in range(2)], st.count("bias_used", 2)
        bias_masked = st.count("bias_masked")
        p_out = [st.count(f"probs_out{r}", 32) for r in range(R)] if rel else []
        chain, act_chain = st.chain("chain"), st.chain("act_chain")
        bank_free = taken if causal or mask is not None else ready
        xn = core.xn[:].rearrange("p k (b s) -> p k b s", b=B)
        x = core.x[:].rearrange("p k (b s) -> p k b s", b=B)
        ctx = core.ctx[:].rearrange("p k (b s) -> p k b s", b=B)
        loads = [(wq[:], w["wq"].rearrange("(k p) n -> p k n", p=P)), (wk[:], w["wk"].rearrange("(k p) n -> p k n", p=P)),
                 (wv[:], w["wv"].rearrange("(k p) n -> p k n", p=P))]
        if project:
            loads.append((wo[:], w["wo"].rearrange("(k p) n -> p k n", p=P)))
        loads += [(t[:], w[key]) for t, key in [(bq, "bq"), (bk, "bk"), (bv, "bv"), (bo, "bo")] if key in w]
        if causal:
            loads.append((cmask[:], w["causal"]) if rel else (bias[:, 0], w["bias"]))
        if mask is not None:
            loads.append((mask_i[:], mask.rearrange("a b (t p) s -> p (a b t) s", p=P)))
        if rel:
            load_block(core, name + "_load", loads)
        else:
            layernorm(core, name + "_ln", core.x, core.xn, preload=loads)

        def batches(engine, body):
            body(0, True, False)
            with engine.Fori(1, B // 2 - 1) as i:
                body(i, False, False)
            body(B // 2 - 1, False, True)

        def buffer_of(j, s):
            return (j * NS + s) % R

        with nc.Block() as block:

            @block.sync
            def _(sp):
                if not rel:
                    return

                def fetch_bias(n, i, j):
                    sp.wait_ge(bias_used.sem, bias_used.at(n - 1))
                    sp.dma_start(bias[:, j, :, 0:P], rel["scores0_read"][n]).then_inc(bias_in[j].sem, 16)
                    sp.dma_start(bias[:, j, :, P:W], rel["scores1_read"][n]).then_inc(bias_in[j].sem, 16)

                def body(i, first, last):
                    for j in range(2):
                        n = i * 2 + j
                        for s in range(NS):
                            if s == 4 and not (last and j == 1):
                                fetch_bias(n + 1, i + j, 1 - j)
                            r = buffer_of(j, s)
                            sp.wait_ge(exped.sem, exped.at(n * NS + s + 1))
                            sp.dma_start(rel["probs0_write"][n, s], p_sb[:, r, 0:P]).then_inc(p_out[r].sem, 16)
                            sp.dma_start(rel["probs1_write"][n, s], p_sb[:, r, P:W]).then_inc(p_out[r].sem, 16)

                for done in p_out:
                    sp.sem_inc(done.sem, done.credit)
                fetch_bias(0, 0, 0)
                batches(sp, body)
                for done in p_out:
                    sp.wait_ge(done.sem, done.at(32 * B * H // R))

            @block.gpsimd
            def _(pool):
                def prepare(n, i, j):
                    if not (isinstance(n, int) and n < 2):
                        pool.wait_ge(projected.sem, projected.at((n - 1) * NPROJ))
                    pool.sem_inc(step_on, 1)
                    if not causal:
                        nc.gpsimd.tensor_copy(kvb[:, j], ctx[:, :, n, :])
                    nc.gpsimd.tensor_copy(xb[:, j], xn[:, :, n, :]).then_inc(copied.sem, 1)
                    if rel:
                        pool.wait_ge(bias_in[j].sem, bias_in[j].at(32 * (i + 1)))
                        nc.gpsimd.tensor_tensor(bias[:, j], bias[:, j],
                                                cmask[:].rearrange("p (o w) -> p o w", o=1).to_broadcast([P, H, W]),
                                                ALU.add).then_inc(bias_masked.sem, 1)

                nc.gpsimd.memset(v_sb[:], 0.0).then_inc(zeroed.sem, 1)
                prepare(0, 0, 0)
                prepare(1, 0, 1)
                with pool.Fori(1, B // 2) as i:
                    for j in range(2):
                        prepare(i * 2 + j, i, j)

            @block.tensor
            def _(pe):
                def projection(n, j, g):
                    pe.wait_ge(copied.sem, copied.at(n + 1))
                    pe.wait_ge(evacuated.sem, evacuated.at(n * NPROJ + g))
                    if not rel:
                        pe.wait_ge(spread_moved.sem, spread_moved.at(n - 1))
                    if g == NPROJ - 1:
                        for t in range(SB):
                            for k in range(KT):
                                mm = nc.tensor.matmul(ps[0:KP, P_BANK, t * D:(t + 1) * D],
                                                      kvb[:, j, k, t * P:t * P + KP], wv[:, k, :],
                                                      start=(k == 0), stop=(k == KT - 1))
                    else:
                        wt, src, n_cols = (wq, xb, S) if g == 0 else (wk, kvb, NK)
                        for m in range(QB):
                            for k in range(KT):
                                mm = nc.tensor.matmul(ps[:, P_BANK, m * S:m * S + n_cols],
                                                      wt[:, k, m * P:(m + 1) * P], src[:, j, k, :],
                                                      start=(k == 0), stop=(k == KT - 1))
                    mm.then_inc(projected.sem, 1)

                def scores(n, j, s):
                    u = j * NS + s
                    if s == 0:
                        pe.wait_ge(evacuated.sem, evacuated.at((n + 1) * NPROJ))
                    pe.wait_ge(bank_free.sem, bank_free.at(n * NS + s + 1 - S_AGO[u]))
                    blk, h = s * PH // HB, s * PH % HB
                    for t, (c0, nk) in enumerate(SEG):
                        keys = k_sb[:, j, blk, h:h + PH, 0:nk // PH].rearrange("p h s -> p (h s)")
                        mm = nc.tensor.matmul(ps[:, S_BANK[u], c0:c0 + nk], q_sb[:, j, blk, t * P:(t + 1) * P],
                                              keys, start=True, stop=True)
                    mm.then_inc(scored.sem, 1)

                def transposes(n, j, s):
                    pe.wait_ge(exped.sem, exped.at(n * NS + s + 1))
                    pe.wait_ge(turned.sem, turned.at(n * NS + s - 1))
                    for i in range(PH):
                        for o, (c0, _, _) in enumerate(TR[i]):
                            mm = nc.tensor.transpose(ps[0:KP, T_BANK + s % 2, i * TW + o * P:i * TW + (o + 1) * P],
                                                     p_sb[:, buffer_of(j, s), c0:c0 + KP], core.ident[:])
                    mm.then_inc(transposed.sem, 1)

                def values(n, j, s):
                    pe.wait_ge(turned.sem, turned.at(n * NS + s + 1))
                    if s == 0:
                        pe.wait_ge(added.sem, added.at(n - 1))
                    for i in range(PH):
                        blk, h = divmod(s * PH + i, HB)
                        for sb in range(SB):
                            o = sum(1 for _, b, _ in TR[i] if b < sb)
                            mm = nc.tensor.matmul(ps[:, Y_BANK + j, blk * S + sb * P:(blk + 1) * S],
                                                  v_sb[0:KP, j, sb, blk, h * P:(h + 1) * P],
                                                  pT[0:KP, s % 2, i * TW + o * P:i * TW + (o + TB - sb) * P],
                                                  start=(h == 0 and sb == 0), stop=(h == HB - 1 and sb == SB - 1))
                    mm.then_inc(valued.sem, 1)

                def spread_sums(n):
                    pe.wait_ge(widened.sem, widened.at(n + 1))
                    for c in range(KT):
                        for t in range(TB):
                            mm = nc.tensor.matmul(ps[:, P_BANK, c * S + t * P:c * S + (t + 1) * P],
                                                  rsum_wide[:, t, c * P:(c + 1) * P], core.ident[:], start=True, stop=True)
                    mm.then_inc(spread.sem, 1)

                def output(n, j):
                    pe.wait_ge(y_done.sem, y_done.at(n + 1))
                    for m in range(KT):
                        for k in range(KT):
                            mm = nc.tensor.matmul(ps[:, Y_BANK + j, m * S:(m + 1) * S], wo[:, k, m * P:(m + 1) * P],
                                                  yT[:, j, k, :], start=(k == 0), stop=(k == KT - 1))
                    mm.then_inc(out_done.sem, 1)

                def late(work, lag, n, j, s, before):
                    if s >= lag:
                        if s - lag < NS:
                            work(n, j, s - lag)
                    elif before:
                        work(n - 1, 1 - j, NS + s - lag)

                def body(i, first, last):
                    for j in range(2):
                        n = i * 2 + j
                        before, behind = not (first and j == 0), not (last and j == 1)
                        for s in range(NS):
                            scores(n, j, s)
                            late(transposes, T_LAG, n, j, s, before)
                            late(values, Y_LAG, n, j, s, before)
                            if s in PROJ_AT and behind:
                                projection(n + 1, 1 - j, PROJ_AT.index(s))
                            if before and not rel:
                                if s == SPREAD_AT:
                                    spread_sums(n - 1)
                                if s == OUT_AT and project:
                                    output(n - 1, 1 - j)

                pe.sem_inc(transposed.sem, transposed.credit)
                pe.sem_inc(valued.sem, valued.credit)
                pe.sem_inc(projected.sem, projected.credit)
                for g in range(NPROJ):
                    projection(0, 0, g)
                batches(pe, body)
                for s in range(NS, NS + Y_LAG):
                    late(transposes, T_LAG, B - 1, 1, s, True)
                    late(values, Y_LAG, B - 1, 1, s, True)
                if not rel:
                    spread_sums(B - 1)
                    if project:
                        output(B - 1, 1)

            @block.scalar
            def _(act):
                def evacuate(n, j, g):
                    act.wait_ge(projected.sem, projected.at(n * NPROJ + g + 1))
                    src = ps[:, P_BANK, :].rearrange("p (m s) -> p m s", m=2)
                    if g == NPROJ - 1:
                        if not (isinstance(n, int) and n < 2):
                            act.wait_ge(valued.sem, valued.at((n - 1) * NS))
                        for sb in range(SB):
                            heads = v_sb[0:KP, j, sb].rearrange("p b (h c) -> p b h c", c=VP)[:, :, :, 0:HD]
                            ins = nc.scalar.copy(heads, ps[0:KP, P_BANK, sb * D:(sb + 1) * D]
                                                 .rearrange("p (b h d) -> p b h d", b=QB, d=HD))
                    elif g == 0:
                        if "bq" in w:
                            for m in range(QB):
                                ins = nc.scalar.activation(q_sb[:, j, m, :], src[:, m, :], ACT.Identity, bias=bq[:, m:m + 1])
                        else:
                            ins = nc.scalar.copy(q_sb[:, j], src)
                    elif "bk" in w:
                        for h in range(HB):
                            for m in range(QB):
                                ins = nc.scalar.activation(k_sb[:, j, m, h, :], src[:, m, 0:NK], ACT.Identity,
                                                           bias=bk_kept[:, h, m:m + 1],
                                                           scale=core.key_scale[:, h:h + 1])
                    else:
                        for h in range(HB):
                            ins = nc.scalar.mul(k_sb[:, j, :, h, :], src[:, :, 0:NK],
                                                core.key_scale[:, h:h + 1])
                    ins.then_inc(evacuated.sem, 1)

                def exponentiate(n, j, s):
                    act.wait_ge(ready.sem, ready.at(n * NS + s + 1))
                    act.wait_ge(transposed.sem, transposed.at(n * NS + s + 1 - R))
                    r = buffer_of(j, s)
                    if rel:
                        act.wait_ge(p_out[r].sem, p_out[r].at(32 * (n * (NS // R) + s // R)))
                    if causal:
                        for t, (c0, nk) in enumerate(SEG):
                            ins = nc.scalar.activation(p_sb[:, r, c0:c0 + nk], s_sb[:, r, c0:c0 + nk], ACT.Exp,
                                                       bias=top[:, r, t:t + 1], accum_out=sums[:, j, t, s:s + 1])
                    else:
                        act.wait_ge(summed.sem, summed.at(n * NS + s + 1 - R))
                        ins = nc.scalar.activation(p_sb[:, r, :], s_sb[:, r, :], ACT.Exp)
                    ins.then_inc(exped.sem, 1)

                def turn(n, j, s):
                    act.wait_ge(transposed.sem, transposed.at(n * NS + s + 1))
                    act.wait_ge(valued.sem, valued.at(n * NS + s - 1))
                    nc.scalar.copy(pT[0:KP, s % 2, :], ps[0:KP, T_BANK + s % 2, 0:PH * TW]).then_inc(turned.sem, 1)

                def move_spread(n):
                    act.wait_ge(spread.sem, spread.at(n + 1))
                    act.wait_ge(normed.sem, normed.at(n))
                    nc.scalar.copy(divisor[:], ps[:, P_BANK, :].rearrange("p (c s) -> p c s", c=KT)).then_inc(spread_moved.sem, 1)

                def add_bias(n, j):
                    act.wait_ge(normed.sem, normed.at(n + 1))
                    for c in range(KT):
                        ins = nc.scalar.activation(yT[:, j, c, :], y_sb[:, j, c, :], ACT.Identity, bias=bv[:, c:c + 1])
                    ins.then_inc(y_biased.sem, 1)

                def body(i, first, last):
                    for j in range(2):
                        n = i * 2 + j
                        before, behind = not (first and j == 0), not (last and j == 1)
                        for s in range(NS):
                            if s >= COPY_LAG:
                                turn(n, j, s - COPY_LAG)
                            elif before:
                                turn(n - 1, 1 - j, NS + s - COPY_LAG)
                            if s in EVAC_AT and behind:
                                evacuate(n + 1, 1 - j, EVAC_AT.index(s))
                            if s == SPREAD_AT and before and not rel:
                                move_spread(n - 1)
                            if s == BIAS_AT and before and "bv" in w:
                                add_bias(n - 1, 1 - j)
                            exponentiate(n, j, s)

                act.sem_inc(exped.sem, exped.credit)
                act.sem_inc(turned.sem, turned.credit)
                act.sem_inc(spread_moved.sem, spread_moved.credit)
                act.wait_ge(zeroed.sem, zeroed.at(1))
                if "bk" in w:
                    for h in range(HB):
                        ins = nc.scalar.mul(bk_kept[:, h], bk[:], core.key_scale[:, h:h + 1])
                    act_chain.link(act, ins)
                for g in range(NPROJ):
                    evacuate(0, 0, g)
                batches(act, body)
                for s in range(NS - COPY_LAG, NS):
                    turn(B - 1, 1, s)
                if not rel:
                    move_spread(B - 1)
                if "bv" in w:
                    add_bias(B - 1, 1)

            @block.vector
            def _(dve):
                def prepare_scores(n, j, s):
                    if rel and s == 0:
                        dve.wait_ge(bias_masked.sem, bias_masked.at(n + 1))
                    r = buffer_of(j, s)
                    dve.wait_ge(scored.sem, scored.at(n * NS + s + 1))
                    dve.wait_ge(exped.sem, exped.at(n * NS + s + 1 - R))
                    tile = ps[:, S_BANK[j * NS + s], 0:W]
                    if causal:
                        nc.vector.tensor_tensor(s_sb[:, r, :], tile, bias[:, j if rel else 0, s, :],
                                                ALU.add).then_inc(taken.sem, 1)
                        dve.wait_ge(taken.sem, taken.at(n * NS + s + 1))
                        for t, (c0, nk) in enumerate(SEG):
                            ins = nc.vector.tensor_reduce(top[:, r, t:t + 1], s_sb[:, r, c0:c0 + nk], AX.X, ALU.max,
                                                          negate=True)
                        ins.then_inc(ready.sem, 1)
                        return
                    if mask is not None:
                        nc.vector.tensor_tensor(s_sb[:, r, :], tile, mask_on[:].rearrange("p t i s -> p (t i s)"),
                                                ALU.mult).then_inc(taken.sem, 1)
                        dve.wait_ge(taken.sem, taken.at(n * NS + s + 1))
                        tile = s_sb[:, r, :]
                        chain.link(dve, nc.vector.tensor_tensor(tile, tile, mask_off[:].rearrange("p t i s -> p (t i s)"), ALU.add))
                    rows = tile.rearrange("p (a s) -> p a s", s=SC)
                    chain.link(dve, nc.vector.tensor_reduce(top[:, r, :], rows, AX.X, ALU.max))
                    nc.vector.tensor_tensor(s_sb[:, r, :].rearrange("p (a s) -> p a s", s=SC), rows,
                                            top[:, r, :].rearrange("p (a o) -> p a o", o=1).to_broadcast([P, PH * TB, SC]),
                                            ALU.subtract).then_inc(ready.sem, 1)

                def sum_rows(n, j, s):
                    dve.wait_ge(exped.sem, exped.at(n * NS + s + 1))
                    nc.vector.tensor_reduce(sums[:, j, :, s * PH:(s + 1) * PH],
                                            p_sb[:, buffer_of(j, s), :].rearrange("p (t i s) -> p t i s", i=PH, s=SC),
                                            AX.X, ALU.add).then_inc(summed.sem, 1)

                def widen_sums(n, j):
                    if causal:
                        dve.wait_ge(exped.sem, exped.at((n + 1) * NS))
                    else:
                        dve.wait_ge(summed.sem, summed.at((n + 1) * NS))
                    if rel:
                        nc.vector.tensor_copy(rel["sums"][:, n, :],
                                              sums[:, j].rearrange("p t h -> p (t h)")).then_inc(bias_used.sem, 1)
                        return
                    dve.wait_ge(widened.sem, widened.at(n))
                    chain.link(dve, nc.vector.reciprocal(rsum[:], sums[:, j]))
                    if not (isinstance(n, int) and n == 0):
                        dve.wait_ge(spread.sem, spread.at(n))
                    nc.vector.tensor_copy(rsum_wide[:].rearrange("p t (h d) -> p t h d", d=HD),
                                          rsum[:].rearrange("p t (h o) -> p t h o", o=1).to_broadcast([P, TB, H, HD])
                                          ).then_inc(widened.sem, 1)

                def normalise(n, j):
                    dve.wait_ge(valued.sem, valued.at((n + 1) * NS))
                    y = ps[:, Y_BANK + j, :].rearrange("p (c s) -> p c s", c=KT)
                    if rel:
                        nc.vector.tensor_copy(rel["y"][:, :, n, :], y).then_inc(added.sem, 1)
                        return
                    dve.wait_ge(spread_moved.sem, spread_moved.at(n + 1))
                    nc.vector.tensor_tensor(y_sb[:, j], y, divisor[:], ALU.mult).then_inc(normed.sem, 1)

                def add_output(n, j):
                    done = out_done if project else y_done
                    dve.wait_ge(done.sem, done.at(n + 1))
                    for m in range(KT):
                        src = ps[:, Y_BANK + j, m * S:(m + 1) * S] if project else yT[:, j, m, :]
                        dst = x[:, m, n, :]
                        if "bo" in w:
                            ins = nc.vector.scalar_tensor_tensor(out=dst, in0=src, scalar=bo[:, m:m + 1], in1=dst,
                                                                 op0=ALU.add, op1=ALU.add)
                        else:
                            ins = nc.vector.tensor_tensor(dst, src, dst, ALU.add)
                    ins.then_inc(added.sem, 1)

                def body(i, first, last):
                    chain.restart(dve)
                    for j in range(2):
                        n = i * 2 + j
                        before = not (first and j == 0)
                        for s in range(NS):
                            if s == RECIP_AT and before:
                                widen_sums(n - 1, 1 - j)
                            if s == NORM_AT and before:
                                normalise(n - 1, 1 - j)
                            prepare_scores(n, j, s)
                            if not causal:
                                if s >= 1:
                                    sum_rows(n, j, s - 1)
                                elif before:
                                    sum_rows(n - 1, 1 - j, NS - 1)
                            if s == ADD_AT and before and not rel:
                                add_output(n - 1, 1 - j)

                for c in (taken, ready, summed, added, bias_used, widened):
                    dve.sem_inc(c.sem, c.credit)
                if mask is not None:
                    for i in range(PH):
                        chain.link(dve, nc.vector.tensor_scalar(mask_off[:, :, i, :], mask_i[:], 0.0, None, ALU.is_equal))
                    chain.link(dve, nc.vector.tensor_scalar(mask_on[:], mask_off[:], -1.0, 1.0, ALU.mult, ALU.add))
                    chain.link(dve, nc.vector.tensor_scalar(mask_off[:], mask_off[:], -1.0e9, None, ALU.mult))
                batches(dve, body)
                if not causal:
                    sum_rows(B - 1, 1, NS - 1)
                widen_sums(B - 1, 1)
                normalise(B - 1, 1)
                if not rel:
                    add_output(B - 1, 1)


def load_block(core, name, loads):
    with Stage(core, name) as st:
        loaded = st.count("loaded")
        with core.nc.Block() as block:

            @block.sync
            def _(sp):
                for to, of in loads:
                    sp.dma_start(to, of).then_inc(loaded.sem, 16)
                sp.wait_ge(loaded.sem, loaded.at(16 * len(loads)))


def relative_attention(core, name, w):
    nc = core.nc
    W0, W1 = P, S
    W = W0 + W1
    scores0 = nc.dram_tensor("rel_scores0", (B, H, P * W0), F32).ap()
    scores1 = nc.dram_tensor("rel_scores1", (B, H, P * W1), F32).ap()
    Z0, Z1 = P, P - 1
    probs0 = nc.dram_tensor("rel_probs0", (B, H, Z0 + P * W0), F32).ap()
    probs1 = nc.dram_tensor("rel_probs1", (B, H, Z1 + P * W1), F32).ap()

    def dram_view(t, offset, pitch, rows, cols):
        flat = t.shape[2]
        return bass.AP(tensor=t.tensor, offset=offset, ap=[[H * flat, B], [pitch, rows], [flat, H], [1, cols]])

    rel = {
        "scores0_read": dram_view(scores0, P - 1, W0 - 1, P, W0),
        "scores1_read": dram_view(scores1, P - 1, W1 - 1, P, W1),
        "probs0_write": probs0[:, :, Z0:].rearrange("b h (t s) -> b h t s", t=P),
        "probs1_write": probs1[:, :, Z1:].rearrange("b h (t s) -> b h t s", t=P),
    }
    scores0_write = scores0.rearrange("b h (t u) -> b t h u", t=P)
    scores1_write = scores1.rearrange("b h (t u) -> b t h u", t=P)
    probs0_read = dram_view(probs0, 1, W0 + 1, P, W0)
    probs1_read = dram_view(probs1, 0, W1 + 1, P, W1)

    with Stage(core, name + "_rel") as keep:
        rel["y"] = core.xn[:].rearrange("p k (b s) -> p k b s", b=B)
        rel["sums"] = keep.buf("sums", [P, B, TB * H])
        relative_scores(core, name + "_scores", w, scores0_write, scores1_write, probs0[:, :, 0:Z0], probs1[:, :, 0:Z1])
        attention(core, name, w, rel=rel)
        relative_values(core, name + "_values", w, rel, probs0_read, probs1_read)


def relative_scores(core, name, w, scores0_write, scores1_write, zeros0, zeros1):
    nc = core.nc
    ps = core.psum
    with Stage(core, name) as st:
        wq = st.buf("wq", [P, KT, D])
        embk = st.buf("embk", [P, HB, S])
        q_sb = st.buf("q", [P, 2, QB, S])
        dist = st.buf("by_distance", [P, 2, H, P + S])
        zeros = st.buf("zeros", [P, P])
        loaded, projected, evacuated = st.count("loaded"), st.count("projected"), st.count("evacuated")
        scored, moved = st.count("scored"), [st.count(f"moved{parity}", 2) for parity in range(2)]
        stored = [st.count(f"stored{j}", 0) for j in range(2)]
        zeroed, cleared = st.count("zeroed"), st.count("cleared")
        xn = core.xn[:].rearrange("p k (b s) -> p k b s", b=B)
        Q_BANK, S_BANK = 0, 4
        TURNS = [(t, h, CH // ((t + 1) * P)) for blk in range(QB) for t in range(TB)
                 for h in range(blk * HB, (blk + 1) * HB, CH // ((t + 1) * P))]
        NU = len(TURNS)
        NEXT_AT = NU // 2

        def batches(engine, body):
            with engine.Fori(0, B // 2 - 1) as i:
                body(i, False)
            body(B // 2 - 1, True)

        def move(engine, copy, n, i, j, u):
            engine.wait_ge(scored.sem, scored.at(n * NU + u + 1))
            if u < 2:
                engine.wait_ge(stored[j].sem, stored[j].at(32 * i))
            t, h, heads = TURNS[u]
            to = dist[:, j, h:h + heads, P:P + S] if t else dist[:, j, h:h + heads, 0:P]
            copy(to, ps[:, S_BANK + u % 4, :].rearrange("p (h s) -> p h s", h=heads)).then_inc(moved[u % 2].sem, 1)

        with nc.Block() as block:

            @block.sync
            def _(sp):
                sp.dma_start(wq[:], w["wq"].rearrange("(k p) n -> p k n", p=P)).then_inc(loaded.sem, 16)
                sp.dma_start(embk[:], w["embkT"]).then_inc(loaded.sem, 16)
                sp.wait_ge(cleared.sem, cleared.at(1))
                sp.dma_start(zeros0.rearrange("b h z -> (b h) z"), zeros[:, 0:zeros0.shape[2]]).then_inc(zeroed.sem, 16)
                sp.dma_start(zeros1.rearrange("b h z -> (b h) z"), zeros[:, 0:zeros1.shape[2]]).then_inc(zeroed.sem, 16)
                for j in range(2):
                    sp.sem_inc(stored[j].sem, stored[j].credit)
                with sp.Fori(0, B // 2) as i:
                    for j in range(2):
                        n = i * 2 + j
                        for done in moved:
                            sp.wait_ge(done.sem, done.at((n + 1) * NU // 2))
                        sp.dma_start(scores0_write[n], dist[:, j, :, 0:P]).then_inc(stored[j].sem, 16)
                        sp.dma_start(scores1_write[n], dist[:, j, :, P:P + S]).then_inc(stored[j].sem, 16)
                for j in range(2):
                    sp.wait_ge(stored[j].sem, stored[j].at(32 * B // 2))
                sp.wait_ge(zeroed.sem, zeroed.at(32))

            @block.tensor
            def _(pe):
                def projection(n, j):
                    for m in range(QB):
                        for k in range(KT):
                            mm = nc.tensor.matmul(ps[:, Q_BANK + j, m * S:(m + 1) * S], wq[:, k, m * P:(m + 1) * P],
                                                  xn[:, k, n, :], start=(k == 0), stop=(k == KT - 1))
                    mm.then_inc(projected.sem, 1)

                def body(i, last):
                    for j in range(2):
                        n = i * 2 + j
                        pe.wait_ge(evacuated.sem, evacuated.at(n + 1))
                        for u, (t, h, heads) in enumerate(TURNS):
                            pe.wait_ge(moved[u % 2].sem, moved[u % 2].at(n * (NU // 2) + u // 2 - 1))
                            table = embk[:, h % HB:h % HB + heads, (0 if t else S - P):S]
                            nc.tensor.matmul(ps[:, S_BANK + u % 4, :], q_sb[:, j, h // HB, t * P:(t + 1) * P],
                                             table, start=True, stop=True).then_inc(scored.sem, 1)
                            if u == NEXT_AT and not (last and j == 1):
                                projection(n + 1, 1 - j)

                pe.wait_ge(loaded.sem, loaded.at(32))
                projection(0, 0)
                batches(pe, body)

            @block.scalar
            def _(act):
                def evacuate(n, j):
                    act.wait_ge(projected.sem, projected.at(n + 1))
                    nc.scalar.copy(q_sb[:, j], ps[:, Q_BANK + j, :].rearrange("p (m s) -> p m s", m=QB)).then_inc(evacuated.sem, 1)

                def body(i, last):
                    for j in range(2):
                        n = i * 2 + j
                        for u in range(1, NU, 2):
                            move(act, nc.scalar.copy, n, i, j, u)
                            if u == NEXT_AT + 1 and not (last and j == 1):
                                evacuate(n + 1, 1 - j)

                act.sem_inc(moved[1].sem, moved[1].credit)
                evacuate(0, 0)
                batches(act, body)

            @block.vector
            def _(dve):
                nc.vector.memset(zeros[:], 0.0).then_inc(cleared.sem, 1)
                dve.sem_inc(moved[0].sem, moved[0].credit)
                with dve.Fori(0, B // 2) as i:
                    for j in range(2):
                        for u in range(0, NU, 2):
                            move(dve, nc.vector.tensor_copy, i * 2 + j, i, j, u)


def relative_values(core, name, w, rel, probs0_read, probs1_read):
    nc = core.nc
    ps = core.psum
    T_BANK, Y_BANK, O_BANK = 0, 4, 6
    TILES = [P, 0, 2 * P]
    NT = len(TILES)
    with Stage(core, name) as st:
        wo = st.buf("wo", [P, KT, D])
        embv = st.buf("embv", [P, TB, HB, P])
        shifted = st.buf("by_distance", [P, 2, H, P + S])
        pT = st.buf("probsT", [P, 4, NT * P])
        rsum = st.buf("rsums", [P, 2, TB * H])
        rsum_wide = st.buf("rsums_by_channel", [P, 2, TB, D])
        y_sum = st.buf("y_sum", [P, 2, KT, S])
        yT = st.buf("yT", [P, 2, KT, S])
        loaded, shifted_in = st.count("loaded"), [st.count(f"shifted_in{j}") for j in range(2)]
        transposed, turned = st.count("transposed"), st.count("turned", 4)
        valued, normed = st.count("valued", 4), st.count("normed", 2)
        summed, recip, widened, spread = (st.count(k) for k in ("summed", "reciprocal", "widened", "spread"))
        out_done, added = st.count("out_done"), st.count("added", 2)
        SPREAD_AT, OUT_AT = 2, 7

        def batches(engine, body):
            body(0, True)
            with engine.Fori(1, B // 2) as i:
                body(i, False)

        x = core.x[:].rearrange("p k (b s) -> p k b s", b=B)
        with nc.Block() as block:

            @block.sync
            def _(sp):
                sp.dma_start(wo[:], w["wo"].rearrange("(k p) n -> p k n", p=P)).then_inc(loaded.sem, 16)
                sp.dma_start(embv[:], w["embv"]).then_inc(loaded.sem, 16)
                with sp.Fori(0, B // 2) as i:
                    for j in range(2):
                        n = i * 2 + j
                        sp.wait_ge(normed.sem, normed.at(n - 1))
                        sp.dma_start(shifted[:, j, :, 0:P], probs0_read[n]).then_inc(shifted_in[j].sem, 16)
                        sp.dma_start(shifted[:, j, :, P:P + S], probs1_read[n]).then_inc(shifted_in[j].sem, 16)
                sp.wait_ge(loaded.sem, loaded.at(32))

            @block.tensor
            def _(pe):
                def transposes(n, j, h):
                    pe.wait_ge(turned.sem, turned.at(n * H + h - 3))
                    for o in range(NT):
                        mm = nc.tensor.transpose(ps[:, T_BANK + h % 4, o * P:(o + 1) * P],
                                                 shifted[:, j, h, TILES[o]:TILES[o] + P], core.ident[:])
                    mm.then_inc(transposed.sem, 1)

                def values(n, j, h):
                    pe.wait_ge(turned.sem, turned.at(n * H + h + 1))
                    if h == 0:
                        pe.wait_ge(normed.sem, normed.at(n - 1))
                    blk, own = divmod(h, HB)
                    nc.tensor.matmul(ps[:, Y_BANK + j, blk * S:(blk + 1) * S], embv[:, 1, own, :],
                                     pT[:, h % 4, P:3 * P], start=(own == 0), stop=False)
                    mm = nc.tensor.matmul(ps[:, Y_BANK + j, blk * S + P:(blk + 1) * S], embv[:, 0, own, :],
                                          pT[:, h % 4, 0:P], start=False, stop=(own == HB - 1))
                    mm.then_inc(valued.sem, 1)

                def spread_sums(n, j):
                    pe.wait_ge(widened.sem, widened.at(n + 1))
                    pe.wait_ge(added.sem, added.at(n - 1))
                    for c in range(KT):
                        for t in range(TB):
                            mm = nc.tensor.matmul(ps[:, O_BANK + j, c * S + t * P:c * S + (t + 1) * P],
                                                  rsum_wide[:, j, t, c * P:(c + 1) * P], core.ident[:], start=True, stop=True)
                    mm.then_inc(spread.sem, 1)

                def output(n, j):
                    pe.wait_ge(normed.sem, normed.at(n + 1))
                    for m in range(KT):
                        for k in range(KT):
                            mm = nc.tensor.matmul(ps[:, O_BANK + j, m * S:(m + 1) * S], wo[:, k, m * P:(m + 1) * P],
                                                  yT[:, j, k, :], start=(k == 0), stop=(k == KT - 1))
                    mm.then_inc(out_done.sem, 1)

                def body(i, first):
                    for j in range(2):
                        n = i * 2 + j
                        pe.wait_ge(shifted_in[j].sem, shifted_in[j].at(32 * (i + 1)))
                        for step in range(H + 2):
                            if step < H:
                                transposes(n, j, step)
                            if step >= 2:
                                values(n, j, step - 2)
                            if not (first and j == 0):
                                if step == SPREAD_AT:
                                    spread_sums(n - 1, 1 - j)
                                if step == OUT_AT:
                                    output(n - 1, 1 - j)

                pe.sem_inc(valued.sem, valued.credit)
                pe.wait_ge(loaded.sem, loaded.at(32))
                batches(pe, body)
                spread_sums(B - 1, 1)
                output(B - 1, 1)

            @block.scalar
            def _(act):
                def body(i, first):
                    for j in range(2):
                        n = i * 2 + j
                        for h in range(H):
                            act.wait_ge(transposed.sem, transposed.at(n * H + h + 1))
                            act.wait_ge(valued.sem, valued.at(n * H + h - 3))
                            nc.scalar.copy(pT[:, h % 4, :], ps[:, T_BANK + h % 4, 0:NT * P]).then_inc(turned.sem, 1)

                act.sem_inc(turned.sem, turned.credit)
                with act.Fori(0, B // 2) as i:
                    body(i, False)

            @block.vector
            def _(dve):
                def widen_sums(n, j):
                    dve.wait_ge(normed.sem, normed.at(n - 1))
                    nc.vector.reciprocal(rsum[:, j], rel["sums"][:, n, :]).then_inc(recip.sem, 1)
                    dve.wait_ge(recip.sem, recip.at(n + 1))
                    nc.vector.tensor_copy(rsum_wide[:, j].rearrange("p t (h d) -> p (t h) d", d=HD),
                                          rsum[:, j].rearrange("p (a o) -> p a o", o=1).to_broadcast([P, TB * H, HD])
                                          ).then_inc(widened.sem, 1)

                def normalise(n, j):
                    dve.wait_ge(valued.sem, valued.at((n + 1) * H))
                    nc.vector.tensor_tensor(y_sum[:, j], rel["y"][:, :, n, :],
                                            ps[:, Y_BANK + j, :].rearrange("p (c s) -> p c s", c=KT),
                                            ALU.add).then_inc(summed.sem, 1)
                    dve.wait_ge(summed.sem, summed.at(n + 1))
                    dve.wait_ge(spread.sem, spread.at(n + 1))
                    nc.vector.tensor_tensor(yT[:, j], y_sum[:, j],
                                            ps[:, O_BANK + j, :].rearrange("p (c s) -> p c s", c=KT),
                                            ALU.mult).then_inc(normed.sem, 1)

                def add_output(n, j):
                    dve.wait_ge(out_done.sem, out_done.at(n + 1))
                    nc.vector.tensor_tensor(x[:, :, n, :], ps[:, O_BANK + j, :].rearrange("p (m s) -> p m s", m=KT),
                                            x[:, :, n, :], ALU.add).then_inc(added.sem, 1)

                dve.sem_inc(normed.sem, normed.credit)
                dve.sem_inc(added.sem, added.credit)
                with dve.Fori(0, B // 2) as i:
                    for j in range(2):
                        widen_sums(i * 2 + j, j)
                        normalise(i * 2 + j, j)
                        add_output(i * 2 + j, j)


def gate(core, name, src, rows, weight, bias, mode, gT, gate_dram, select_bias=None):
    nc = core.nc
    ps = core.psum
    NT = T // P
    kt = src.shape[1]
    eps = 1e-8 if mode == "top2_eps" else None
    with Stage(core, name) as st:
        wg = st.buf("wg", [P, kt, E])
        bg = st.buf("bg", [P, E])
        sb = st.buf("select_bias", [P, E])
        p = st.buf("p", [P, NT, E])
        key = st.buf("key", [P, NT, E])
        stat = st.buf("stat", [P, NT])
        pair = st.buf("pair", [P, NT, E, E])
        tie = st.buf("tie", [P, NT, E, E])
        rank = st.buf("rank", [P, NT, E])
        loaded, logits_done = st.count("loaded"), st.count("logits_done")
        shifted, exped = st.count("shifted"), st.count("exped")
        weighted, turned, moved, stored = st.count("weighted"), st.count("turned"), st.count("moved"), st.count("stored")
        chain = st.chain("chain")
        n_loads = 1 + (bias is not None) + (select_bias is not None)

        def over_experts(t):
            return t.rearrange("p (n o) -> p n o", o=1).to_broadcast([P, NT, E])

        def over_tiles(t):
            return t.rearrange("p (o e) -> p o e", o=1).to_broadcast([P, NT, E])

        with nc.Block() as block:

            @block.sync
            def _(sp):
                sp.dma_start(wg[0:rows], weight.rearrange("(k p) e -> p k e", p=rows)).then_inc(loaded.sem, 16)
                for dst, vec in ((bg, bias), (sb, select_bias)):
                    if vec is not None:
                        sp.dma_start(dst[:], vec.rearrange("(o e) -> o e", o=1).to_broadcast([P, E])).then_inc(loaded.sem, 16)
                sp.wait_ge(moved.sem, moved.at(4))
                sp.dma_start(gate_dram, gT[0:E, :]).then_inc(stored.sem, 16)
                sp.wait_ge(stored.sem, stored.at(16))
                sp.wait_ge(loaded.sem, loaded.at(16 * n_loads))

            @block.tensor
            def _(pe):
                pe.wait_ge(loaded.sem, loaded.at(16 * n_loads))
                for t in range(NT):
                    for k in range(kt):
                        mm = nc.tensor.matmul(ps[:, 0, t * E:(t + 1) * E], src[0:rows, k, t * P:(t + 1) * P],
                                              wg[0:rows, k, :], start=(k == 0), stop=(k == kt - 1))
                mm.then_inc(logits_done.sem, 1)
                pe.wait_ge(weighted.sem, weighted.at(1))
                for t in range(NT):
                    c, o = t * P // CH, t * P % CH
                    mm = nc.tensor.transpose(ps[0:E, 1 + c, o:o + P], p[:, t, :], core.ident[:])
                    if o + P == CH:
                        mm.then_inc(turned.sem, 1)

            @block.scalar
            def _(act):
                act.wait_ge(shifted.sem, shifted.at(1))
                nc.scalar.activation(p[:], p[:], ACT.Exp).then_inc(exped.sem, 1)
                for c in range(T // CH):
                    act.wait_ge(turned.sem, turned.at(c + 1))
                    nc.scalar.copy(gT[0:E, c * CH:(c + 1) * CH], ps[0:E, 1 + c, :]).then_inc(moved.sem, 1)

            @block.vector
            def _(dve):
                def do(ins):
                    chain.link(dve, ins)

                def tt(out, a, b, op):
                    do(nc.vector.tensor_tensor(out, a, b, op))

                dve.wait_ge(loaded.sem, loaded.at(16 * n_loads))
                dve.wait_ge(logits_done.sem, logits_done.at(1))
                logits = ps[:, 0, 0:NT * E].rearrange("p (n e) -> p n e", e=E)
                if bias is not None:
                    tt(p[:], logits, over_tiles(bg[:]), ALU.add)
                else:
                    do(nc.vector.tensor_copy(p[:], logits))
                do(nc.vector.tensor_reduce(stat[:], p[:], AX.X, ALU.max))
                nc.vector.tensor_tensor(p[:], p[:], over_experts(stat[:]), ALU.subtract).then_inc(shifted.sem, 1)
                dve.wait_ge(exped.sem, exped.at(1))
                do(nc.vector.tensor_reduce(stat[:], p[:], AX.X, ALU.add))
                do(nc.vector.reciprocal(stat[:], stat[:]))
                tt(p[:], p[:], over_experts(stat[:]), ALU.mult)
                if mode == "threshold":
                    do(nc.vector.tensor_scalar(rank[:], p[:], 0.1, None, ALU.is_ge))
                    tt(p[:], p[:], rank[:], ALU.mult)
                    do(nc.vector.tensor_reduce(stat[:], p[:], AX.X, ALU.add))
                    do(nc.vector.tensor_scalar(rank[:, :, 0], stat[:], 0.0, None, ALU.is_equal))
                    tt(stat[:], stat[:], rank[:, :, 0], ALU.add)
                    do(nc.vector.reciprocal(stat[:], stat[:]))
                else:
                    if select_bias is not None:
                        tt(key[:], p[:], over_tiles(sb[:]), ALU.add)
                    else:
                        do(nc.vector.tensor_copy(key[:], p[:]))
                    for t in range(NT):
                        mine = key[:, t, :].rearrange("p (e o) -> p e o", o=1).to_broadcast([P, E, E])
                        other = key[:, t, :].rearrange("p (o f) -> p o f", o=1).to_broadcast([P, E, E])
                        nc.vector.tensor_tensor(pair[:, t], other, mine, ALU.is_gt)
                        ins = nc.vector.tensor_tensor(tie[:, t], other, mine, ALU.is_equal)
                    do(ins)
                    tri = core.tri[:].rearrange("p (o e) f -> p o (e f)", o=1).to_broadcast([P, NT, E * E])
                    tt(tie[:].rearrange("p n e f -> p n (e f)"), tie[:].rearrange("p n e f -> p n (e f)"), tri, ALU.mult)
                    tt(pair[:], pair[:], tie[:], ALU.add)
                    do(nc.vector.tensor_reduce(rank[:], pair[:], AX.X, ALU.add))
                    do(nc.vector.tensor_scalar(rank[:], rank[:], 2.0, None, ALU.is_lt))
                    if mode == "top2_raw":
                        nc.vector.tensor_tensor(p[:], p[:], rank[:], ALU.mult).then_inc(weighted.sem, 1)
                        return
                    tt(p[:], p[:], rank[:], ALU.mult)
                    do(nc.vector.tensor_reduce(stat[:], p[:], AX.X, ALU.add))
                    if eps:
                        do(nc.vector.tensor_scalar(stat[:], stat[:], eps, None, ALU.add))
                    do(nc.vector.reciprocal(stat[:], stat[:]))
                nc.vector.tensor_tensor(p[:], p[:], over_experts(stat[:]), ALU.mult).then_inc(weighted.sem, 1)


def experts(core, name, kind, w, gT, gate_dram, src, parts=None, rows=P, hidden=0, out_rows=P, out_tiles=KT,
            act_fn=None, store=None):
    nc = core.nc
    ps = core.psum
    kt = src.shape[1]
    MT = kt if kind == "linear" else hidden // P
    NC = HALF // CH
    U = NC * MT
    NW1 = {"linear": 0, "mlp": 1, "swiglu": 2}[kind]
    W1 = kt * hidden
    WT = NW1 * W1 + MT * out_tiles * out_rows
    O2 = NW1 * W1
    LAG = 2
    R = 4
    H_RING = 4 // max(NW1, 1)
    with Stage(core, name) as st:
        raw = st.buf("raw", [P, WT])
        w_hi = st.buf("w_hi", [P, 2, WT], F32R)
        w_lo = st.buf("w_lo", [P, 2, WT], F32R)
        gates = st.buf("gates", [P, 2, HALF])
        zeros = st.buf("zeros", [P, CH], F32R)
        act_out = st.buf("act_out", [P, 2, CH])
        gated = st.buf("gated", [P, 2, CH])
        h_hi = st.buf("h_hi", [P, R, CH], F32R)
        h_lo = st.buf("h_lo", [P, R, CH], F32R)
        b1 = st.buf("b1", [P, E, max(MT, 1)])
        b2 = st.buf("b2", [E, out_tiles * out_rows])
        if kind == "swiglu":
            xs = st.buf("scaled_in", [P, kt, CH])
            xs_hi = st.buf("scaled_in_hi", [P, NC, kt, CH], F32R)
            xs_lo = st.buf("scaled_in_lo", [P, NC, kt, CH], F32R)
        loaded, zeroed = st.count("loaded"), st.count("zeroed")
        raw_in, w_split = st.count("raw_in"), st.count("w_split", 0)
        gates_in = [st.count(f"gates_in{j}") for j in range(2)]
        hidden_done, act_done = st.count("hidden_done", 2 * U), st.count("act_done", H_RING)
        gate_done, high_done, low_done = st.count("gate_done", U), st.count("high_done"), st.count("low_done", 2)
        product_done = st.count("product_done", max(R, U))
        in_split = st.count("in_split", NC)
        closed, emptied = st.count("closed"), st.count("emptied", 0)
        pool_chain = st.chain("pool_chain")
        step_on = st.count("step_on").sem
        has_b1, has_b2 = "b1" in w, "b2" in w
        n_loads = has_b1 + has_b2
        views = []
        if NW1:
            views.append((w["w1"].rearrange("e (k p) n -> e p k n", p=rows), 0, rows, kt))
        if NW1 == 2:
            views.append((w["w3"].rearrange("e (k p) n -> e p k n", p=rows), W1, rows, kt))
        views.append((w["w2"].rearrange("e (k p) n -> e p k n", p=P), O2, P, MT))
        RAWS = 16 * len(views)

        def w1_cols(which, k, m):
            o = which * W1 + k * hidden + m * P
            return slice(o, o + P)

        def w2_cols(m, mo):
            o = O2 + (m * out_tiles + mo) * out_rows
            return slice(o, o + out_rows)

        def tokens(half, c):
            return bass.ds(half * HALF + c * CH, CH)

        with nc.Block() as block:

            @block.sync
            def _(sp):
                if rows < P:
                    sp.wait_ge(zeroed.sem, zeroed.at(2))
                if has_b1:
                    sp.dma_start(b1[:], w["b1"]).then_inc(loaded.sem, 16)
                if has_b2:
                    sp.dma_start(b2[:], w["b2"]).then_inc(loaded.sem, 16)
                with sp.Fori(0, 2) as half:
                    with sp.Fori(0, E // 2) as pair:
                        for j in range(2):
                            turn = half * (E // 2) + pair
                            n = turn * 2 + j
                            sp.wait_ge(w_split.sem, w_split.at(n))
                            for view, o, r, tiles in views:
                                width = view.shape[3] * tiles
                                sp.dma_start(raw[0:r, o:o + width].rearrange("p (k n) -> p k n", k=tiles),
                                             view[pair * 2 + j]).then_inc(raw_in.sem, 16)
                            if kind == "swiglu":
                                sp.wait_ge(in_split.sem, in_split.at((n - 1) * NC))
                            else:
                                sp.wait_ge(gate_done.sem, gate_done.at((n - 1) * U))
                            sp.dma_start(gates[:, j, :], gate_dram[bass.ds(pair * 2 + j, 1), bass.ds(half * HALF, HALF)]
                                         .to_broadcast([P, HALF])).then_inc(gates_in[j].sem, 16)
                if n_loads:
                    sp.wait_ge(loaded.sem, loaded.at(16 * n_loads))

            @block.gpsimd
            def _(pool):
                pool.sem_inc(in_split.sem, in_split.credit)
                pool.sem_inc(w_split.sem, w_split.credit)
                nc.gpsimd.memset(zeros[:].bitcast(F32), 0.0).then_inc(zeroed.sem, 1)
                if rows < P:
                    nc.gpsimd.memset(raw[:], 0.0).then_inc(zeroed.sem, 1)
                with pool.Fori(0, 2) as half:
                    with pool.Fori(0, E // 2) as pair:
                        pool_chain.restart(pool)
                        for j in range(2):
                            turn = half * (E // 2) + pair
                            n = turn * 2 + j
                            pool.wait_ge(raw_in.sem, raw_in.at(RAWS * (n + 1)))
                            pool.wait_ge(product_done.sem, product_done.at((n - 1) * U))
                            pool.sem_inc(step_on, 1)
                            pool_chain.link(pool, nc.gpsimd.tensor_copy(w_hi[:, j, :], raw[:]))
                            nc.gpsimd.tensor_tensor(w_lo[:, j, :], raw[:], w_hi[:, j, :].bitcast(F32),
                                                    ALU.subtract).then_inc(w_split.sem, 1)
                            if kind == "swiglu":
                                pool.wait_ge(gates_in[j].sem, gates_in[j].at(16 * (turn + 1)))
                                for c in range(NC):
                                    pool.wait_ge(hidden_done.sem, hidden_done.at((n - 1) * U + (c + 1) * MT))
                                    pool.wait_ge(in_split.sem, in_split.at(n * NC + c))
                                    pool.sem_inc(step_on, 1)
                                    g = gates[:, j:j + 1, c * CH:(c + 1) * CH].to_broadcast([P, kt, CH])
                                    pool_chain.link(pool, nc.gpsimd.tensor_tensor(xs[:], src[:, :, tokens(half, c)], g, ALU.mult))
                                    pool_chain.link(pool, nc.gpsimd.tensor_copy(xs_hi[:, c], xs[:]))
                                    nc.gpsimd.tensor_tensor(xs_lo[:, c], xs[:], xs_hi[:, c].bitcast(F32),
                                                            ALU.subtract).then_inc(in_split.sem, 1)

            @block.tensor
            def _(pe):
                pe.sem_inc(hidden_done.sem, hidden_done.credit)
                pe.sem_inc(product_done.sem, product_done.credit)
                if n_loads:
                    pe.wait_ge(loaded.sem, loaded.at(16 * n_loads))
                pe.wait_ge(zeroed.sem, zeroed.at(1))

                def three(out, hi_w, lo_w, hi_x, lo_x, start, stop):
                    nc.tensor.matmul(out, hi_w, hi_x, start=start, stop=False, skip_group_check=True)
                    nc.tensor.matmul(out, hi_w, lo_x, start=False, stop=False, skip_group_check=True)
                    return nc.tensor.matmul(out, lo_w, hi_x, start=False, stop=stop, skip_group_check=True)

                def first_product(half, n, j, u):
                    c, m = divmod(u, MT)
                    if kind == "swiglu":
                        if m == 0:
                            pe.wait_ge(in_split.sem, in_split.at(n * NC + c + 1))
                        pe.wait_ge(gate_done.sem, gate_done.at(n * U + u + 1 - H_RING))
                        hi, lo = xs_hi[:, c], xs_lo[:, c]
                    else:
                        pe.wait_ge(act_done.sem, act_done.at(n * U + u + 1 - H_RING))
                        hi, lo = parts[0][0:rows, :, tokens(half, c)], parts[1][0:rows, :, tokens(half, c)]
                    for which in range(NW1):
                        bank = 4 + (u % H_RING) * NW1 + which
                        for k in range(kt):
                            cols = w1_cols(which, k, m)
                            mm = three(ps[:, bank, :], w_hi[0:rows, j, cols], w_lo[0:rows, j, cols], hi[:, k], lo[:, k],
                                       k == 0, k == kt - 1)
                    mm.then_inc(hidden_done.sem, 1)

                def last_product(n, j, u):
                    c, m = divmod(u, MT)
                    pe.wait_ge(low_done.sem, low_done.at(n * U + u + 1))
                    for mo in range(out_tiles):
                        mm = three(ps[0:out_rows, c * out_tiles + mo, :], w_hi[:, j, w2_cols(m, mo)],
                                   w_lo[:, j, w2_cols(m, mo)], h_hi[:, u % R, :], h_lo[:, u % R, :], False, False)
                    mm.then_inc(product_done.sem, 1)

                with pe.Fori(0, 2) as half:
                    pe.wait_ge(emptied.sem, emptied.at(half))
                    for c in range(NC):
                        for mo in range(out_tiles):
                            nc.tensor.matmul(ps[0:out_rows, c * out_tiles + mo, :], zeros[:, 0:out_rows], zeros[:],
                                             start=True, stop=False, skip_group_check=True)
                    with pe.Fori(0, E // 2) as pair:
                        for j in range(2):
                            n = (half * (E // 2) + pair) * 2 + j
                            pe.wait_ge(w_split.sem, w_split.at(n + 1))
                            for step in range(U + LAG):
                                if NW1 and step < U:
                                    first_product(half, n, j, step)
                                if step >= LAG:
                                    last_product(n, j, step - LAG)
                    for c in range(NC):
                        for mo in range(out_tiles):
                            out = ps[0:out_rows, c * out_tiles + mo, :]
                            if has_b2:
                                mm = nc.tensor.matmul(out, b2[:, mo * out_rows:(mo + 1) * out_rows], gT[0:E, tokens(half, c)],
                                                      start=False, stop=True, skip_group_check=True)
                            else:
                                mm = nc.tensor.matmul(out, zeros[:, 0:out_rows], zeros[:], start=False, stop=True,
                                                      skip_group_check=True)
                    mm.then_inc(closed.sem, 1)

            @block.scalar
            def _(act):
                act.sem_inc(act_done.sem, act_done.credit)
                if n_loads:
                    act.wait_ge(loaded.sem, loaded.at(16 * n_loads))
                with act.Fori(0, 2) as half:
                    with act.Fori(0, E // 2) as pair:
                        for j in range(2):
                            n = (half * (E // 2) + pair) * 2 + j
                            for step in range(U + 1):
                                if NW1 and step < U:
                                    u = step
                                    act.wait_ge(hidden_done.sem, hidden_done.at(n * U + u + 1))
                                    act.wait_ge(gate_done.sem, gate_done.at(n * U + u - 1))
                                    hidden_ps = ps[:, 4 + (u % H_RING) * NW1, :]
                                    if has_b1:
                                        act.sem_inc(step_on, 1)
                                        ins = nc.scalar.activation(act_out[:, u % 2, :], hidden_ps, act_fn,
                                                                   bias=b1[:, pair * 2 + j, u % MT:u % MT + 1])
                                    else:
                                        ins = nc.scalar.activation(act_out[:, u % 2, :], hidden_ps, act_fn)
                                    ins.then_inc(act_done.sem, 1)
                                if step >= 1:
                                    u = step - 1
                                    act.wait_ge(gate_done.sem, gate_done.at(n * U + u + 1))
                                    act.wait_ge(product_done.sem, product_done.at(n * U + u + 1 - R))
                                    nc.scalar.copy(h_hi[:, u % R, :], gated[:, u % 2, :]).then_inc(high_done.sem, 1)

            @block.vector
            def _(dve):
                dve.sem_inc(gate_done.sem, gate_done.credit)
                dve.sem_inc(low_done.sem, low_done.credit)
                dve.sem_inc(emptied.sem, emptied.credit)
                with dve.Fori(0, 2) as half:
                    with dve.Fori(0, E // 2) as pair:
                        for j in range(2):
                            turn = half * (E // 2) + pair
                            n = turn * 2 + j
                            dve.wait_ge(gates_in[j].sem, gates_in[j].at(16 * (turn + 1)))
                            for step in range(U + 1):
                                if step < U:
                                    u = step
                                    c, m = divmod(u, MT)
                                    dve.wait_ge(low_done.sem, low_done.at(n * U + u - 1))
                                    g = gates[:, j, c * CH:(c + 1) * CH]
                                    if kind == "linear":
                                        a, b = src[:, m, tokens(half, c)], g
                                    else:
                                        dve.wait_ge(act_done.sem, act_done.at(n * U + u + 1))
                                        a = act_out[:, u % 2, :]
                                        b = ps[:, 5 + (u % H_RING) * NW1, :] if kind == "swiglu" else g
                                    nc.vector.tensor_tensor(gated[:, u % 2, :], a, b, ALU.mult).then_inc(gate_done.sem, 1)
                                if step >= 1:
                                    u = step - 1
                                    dve.wait_ge(high_done.sem, high_done.at(n * U + u + 1))
                                    nc.vector.tensor_tensor(h_lo[:, u % R, :], gated[:, u % 2, :],
                                                            h_hi[:, u % R, :].bitcast(F32), ALU.subtract).then_inc(low_done.sem, 1)
                    dve.wait_ge(closed.sem, closed.at(half + 1))
                    for c in range(NC):
                        sums = ps[0:out_rows, c * out_tiles:(c + 1) * out_tiles, :]
                        if store is None:
                            dst = core.x[:, :, tokens(half, c)]
                            ins = nc.vector.tensor_tensor(dst, dst, sums, ALU.add)
                        else:
                            ins = nc.vector.tensor_copy(store[0:out_rows, :, tokens(half, c)], sums)
                    ins.then_inc(emptied.sem, 1)


def two_layers(core, name, w, src, rows, dst, out_rows, out_tiles, last_fn, parts=None, third=None):
    nc = core.nc
    ps = core.psum
    kt = src.shape[1]
    M1 = w["w1"].shape[1] // P
    with Stage(core, name) as st:
        w1 = st.buf("w1", [P, kt, M1 * P])
        w2 = st.buf("w2", [P, M1, out_tiles * out_rows])
        b1 = st.buf("b1", [P, M1])
        b2 = st.buf("b2", [P, out_tiles])
        w3 = st.buf("w3", [P, P])
        b3 = st.buf("b3", [P, 1])
        hid = st.buf("hidden", [P, 2, M1, CH])
        loaded, hidden_done, squashed = st.count("loaded"), st.count("hidden_done"), st.count("squashed", M1)
        out_done, moved = st.count("out_done", 2), st.count("moved", 2)
        third_done, third_moved = st.count("third_done"), st.count("third_moved", 2)
        split_high = st.count("split_high")
        loads = [(w1[0:rows], w["w1"].rearrange("(k p) n -> p k n", p=rows)), (w2[:], w["w2"].rearrange("(k p) n -> p k n", p=P)),
                 (b1[:], w["b1"]), (b2[0:out_rows], w["b2"])]
        if third:
            loads += [(w3[0:out_rows, 0:out_rows], third[0]), (b3[0:out_rows], third[1])]

        def tokens(q, j):
            return bass.ds((q * 2 + j) * CH, CH)

        with nc.Block() as block:

            @block.sync
            def _(sp):
                for to, of in loads:
                    sp.dma_start(to, of).then_inc(loaded.sem, 16)
                sp.wait_ge(loaded.sem, loaded.at(16 * len(loads)))

            @block.tensor
            def _(pe):
                pe.sem_inc(out_done.sem, out_done.credit)
                pe.wait_ge(loaded.sem, loaded.at(16 * len(loads)))
                with pe.Fori(0, NCH // 2) as q:
                    for j in range(2):
                        n = q * 2 + j
                        pe.wait_ge(out_done.sem, out_done.at(n - 1))
                        for m in range(M1):
                            pe.wait_ge(squashed.sem, squashed.at(n * M1 + m + 1 - M1))
                            for k in range(kt):
                                mm = nc.tensor.matmul(ps[:, m, :], w1[0:rows, k, m * P:(m + 1) * P],
                                                      src[0:rows, k, tokens(q, j)], start=(k == 0), stop=(k == kt - 1))
                            mm.then_inc(hidden_done.sem, 1)
                    for j in range(2):
                        n = q * 2 + j
                        pe.wait_ge(squashed.sem, squashed.at((n + 1) * M1))
                        before = third_moved if third else moved
                        pe.wait_ge(before.sem, before.at(n - 1))
                        for mo in range(out_tiles):
                            for m in range(M1):
                                mm = nc.tensor.matmul(ps[0:out_rows, 4 + j * 2 + mo, :],
                                                      w2[:, m, mo * out_rows:(mo + 1) * out_rows], hid[:, j, m, :],
                                                      start=(m == 0), stop=(m == M1 - 1))
                        mm.then_inc(out_done.sem, 1)
                        if third:
                            pe.wait_ge(moved.sem, moved.at(n + 1))
                            nc.tensor.matmul(ps[0:out_rows, 5 + j * 2, :], w3[0:out_rows, 0:out_rows],
                                             dst[0:out_rows, 0, tokens(q, j)], start=True, stop=True).then_inc(third_done.sem, 1)

            @block.scalar
            def _(act):
                act.sem_inc(squashed.sem, squashed.credit)
                act.sem_inc(moved.sem, moved.credit)
                act.sem_inc(third_moved.sem, third_moved.credit)
                act.wait_ge(loaded.sem, loaded.at(16 * len(loads)))
                with act.Fori(0, NCH // 2) as q:
                    for j in range(2):
                        n = q * 2 + j
                        act.wait_ge(out_done.sem, out_done.at(n - 1))
                        for m in range(M1):
                            act.wait_ge(hidden_done.sem, hidden_done.at(n * M1 + m + 1))
                            nc.scalar.activation(hid[:, j, m, :], ps[:, m, :], ACT.Sigmoid,
                                                 bias=b1[:, m:m + 1]).then_inc(squashed.sem, 1)
                    for j in range(2):
                        n = q * 2 + j
                        act.wait_ge(out_done.sem, out_done.at(n + 1))
                        for mo in range(out_tiles):
                            ins = nc.scalar.activation(dst[0:out_rows, mo, tokens(q, j)], ps[0:out_rows, 4 + j * 2 + mo, :],
                                                       last_fn, bias=b2[0:out_rows, mo:mo + 1])
                        ins.then_inc(moved.sem, 1)
                        if third:
                            act.wait_ge(third_done.sem, third_done.at(n + 1))
                            nc.scalar.activation(third[2][0:out_rows, 0, tokens(q, j)], ps[0:out_rows, 5 + j * 2, :],
                                                 ACT.Relu, bias=b3[0:out_rows, 0:1]).then_inc(third_moved.sem, 1)
                        if parts:
                            nc.scalar.copy(parts[0][0:out_rows, :, tokens(q, j)],
                                           dst[0:out_rows, :, tokens(q, j)]).then_inc(split_high.sem, 1)

            @block.vector
            def _(dve):
                if parts:
                    with dve.Fori(0, NCH // 2) as q:
                        for j in range(2):
                            dve.wait_ge(split_high.sem, split_high.at(q * 2 + j + 1))
                            nc.vector.tensor_tensor(parts[1][0:out_rows, :, tokens(q, j)], dst[0:out_rows, :, tokens(q, j)],
                                                    parts[0][0:out_rows, :, tokens(q, j)].bitcast(F32), ALU.subtract)


def mixture_buffers(core, name, stack):
    gT = core.sbuf(name + "_gateT", [E, T], stack=stack)
    return gT, core.nc.dram_tensor(name + "_gate_dram", (E, T), F32).ap()


def stage_L0_ffn(core, name, w, a):
    with ExitStack() as stack:
        gT, gate_dram = mixture_buffers(core, name, stack)
        layernorm(core, name + "_ln", core.x, core.xn)
        gate(core, name + "_gate", core.xn, P, w["gate_w"], w["gate_b"], "threshold", gT, gate_dram)
        experts(core, name, "linear", w, gT, gate_dram, core.xn)


def stage_L1_ffn(core, name, w, a):
    F = w["pre_w2"].shape[1]
    with ExitStack() as stack:
        gT, gate_dram = mixture_buffers(core, name, stack)
        cont = core.sbuf(name + "_cont", [P, 1, T], stack=stack)
        router = core.sbuf(name + "_router", [P, 1, T], stack=stack)
        parts = [core.sbuf(name + f"_cont_{p}", [P, 1, T], F32R, stack) for p in ("high", "low")]
        layernorm(core, name + "_ln", core.x, core.xn)
        two_layers(core, name + "_pre", {k[4:]: v for k, v in w.items() if k.startswith("pre_")}, core.xn, P, cont, F, 1,
                   ACT.Identity, parts, (w["r_w1"], w["r_b1"], router))
        gate(core, name + "_gate", router, F, w["r_w2"], w["r_b2"], "top2", gT, gate_dram)
        experts(core, name, "mlp", w, gT, gate_dram, cont, parts, rows=F, hidden=w["w1"].shape[2], out_rows=F, out_tiles=1,
                act_fn=ACT.Relu, store=cont)
        two_layers(core, name + "_post", {k[5:]: v for k, v in w.items() if k.startswith("post_")}, cont, F, core.xn, P, KT,
                   ACT.Sigmoid)
        layernorm(core, name + "_out", core.xn, core.x, affine=(w["ln_g"], w["ln_b"]))


def stage_L2_ffn(core, name, w, a):
    with ExitStack() as stack:
        gT, gate_dram = mixture_buffers(core, name, stack)
        layernorm(core, name + "_ln", core.x, core.xn)
        gate(core, name + "_gate", core.xn, P, w["gate_w"], None, "top2_raw", gT, gate_dram, w["expert_bias"])
        experts(core, name, "swiglu", w, gT, gate_dram, core.xn, hidden=w["w1"].shape[2], act_fn=ACT.Silu)


def stage_L3_ffn(core, name, w, a):
    with ExitStack() as stack:
        gT, gate_dram = mixture_buffers(core, name, stack)
        parts = [core.sbuf(name + f"_x_{p}", [P, KT, T], F32R, stack) for p in ("high", "low")]
        layernorm(core, name + "_ln", core.x, core.xn, parts=parts)
        gate(core, name + "_gate", core.xn, P, w["Wg"], w["bg"], "top2_eps", gT, gate_dram)
        experts(core, name, "mlp", w, gT, gate_dram, core.xn, parts, hidden=w["w1"].shape[2], act_fn=ACT.Gelu, store=core.xn)
        layernorm(core, name + "_out", core.xn, core.x, affine=(w["gamma"], w["beta"]))


def lay_out_mixtures(a, n):
    def hidden_bias(b):
        return b.reshape(E, -1, P).transpose(2, 0, 1)

    for k in ("gate_w", "gate_b"):
        a[f"L0_ffn_{k}"] = n[f"L0_ffn_{k}"]
    a["L0_ffn_w2"], a["L0_ffn_b2"] = n["L0_ffn_expert_w"], n["L0_ffn_expert_b"]

    p = "L1_ffn_"
    a[p + "pre_w1"], a[p + "pre_b1"] = n[p + "enc_w"], by_partition(n[p + "enc_b"])
    def filled(t, *axes):
        return np.pad(t, [(0, P - t.shape[i]) if i in axes else (0, 0) for i in range(t.ndim)])

    a[p + "pre_w2"], a[p + "pre_b2"] = filled(n[p + "s2c_w"], 1), filled(n[p + "s2c_b"], 0).reshape(-1, 1)
    a[p + "r_w1"], a[p + "r_b1"] = filled(n[p + "r_w1"], 0, 1), filled(n[p + "r_b1"], 0).reshape(-1, 1)
    a[p + "r_w2"], a[p + "r_b2"] = filled(n[p + "r_w2"], 0), n[p + "r_b2"]
    a[p + "w1"], a[p + "b1"] = filled(n[p + "e_w1"], 1), hidden_bias(n[p + "e_b1"])
    a[p + "w2"], a[p + "b2"] = filled(n[p + "e_w2"], 2), filled(n[p + "e_b2"], 1)
    a[p + "post_w1"], a[p + "post_b1"] = filled(n[p + "c2s_w"], 0), by_partition(n[p + "c2s_b"])
    a[p + "post_w2"], a[p + "post_b2"] = n[p + "dec_w"], by_partition(n[p + "dec_b"])
    a[p + "ln_g"], a[p + "ln_b"] = by_partition(n[p + "ln_g"]), by_partition(n[p + "ln_b"])

    p = "L2_ffn_"
    short = -n[p + "w1"].shape[2] % P
    a[p + "gate_w"], a[p + "expert_bias"] = n[p + "gate_w"].T, n[p + "expert_bias"]
    a[p + "w1"] = np.pad(n[p + "w1"], ((0, 0), (0, 0), (0, short)))
    a[p + "w3"] = np.pad(n[p + "w3"], ((0, 0), (0, 0), (0, short)))
    a[p + "w2"] = np.pad(n[p + "w2"], ((0, 0), (0, short), (0, 0)))

    p = "L3_ffn_"
    a[p + "Wg"], a[p + "bg"] = n[p + "Wg"], n[p + "bg"]
    a[p + "w1"], a[p + "b1"] = n[p + "W1"], hidden_bias(n[p + "b1"])
    a[p + "w2"], a[p + "b2"] = n[p + "W2"], n[p + "b2"]
    a[p + "gamma"], a[p + "beta"] = by_partition(n[p + "gamma"]), by_partition(n[p + "beta"])


def linear_attention(core, name, w):
    nc = core.nc
    ps = core.psum
    NG = H // 4
    F = 2 * HD
    VC = HD + 1
    BR = 2
    with Stage(core, name) as st:
        wt = {c: st.buf("w" + c, [P, KT, D]) for c in "qkvo"}
        bt = {c: st.buf("b" + c, [P, D]) for c in "qkv"}
        bo = st.buf("bo", [P, KT])
        angle = st.buf("sin_cos", [P, TB, 2])
        xb = st.buf("tokens", [P, 2, KT, S])
        qk = st.buf("qk", [P, 2, TB, 2 * D])
        mx = st.buf("max", [P, TB, 2 * H])
        total = st.buf("total", [P, TB, 2 * H])
        feat = st.buf("features", [P, TB, 2, BR, H, F])
        v = st.buf("v", [P, 2, TB, H, VC])
        kv = st.buf("kv", [P, BR * NG, 4, VC])
        qfT = st.buf("q_featuresT", [P, BR * NG, S])
        z = st.buf("z", [P, BR, TB, H])
        part = st.buf("branch", [P, BR, TB, D])
        y = st.buf("y", [P, TB, D])
        yT = st.buf("yT", [P, KT, S])
        loaded, copied, projected = st.count("loaded"), st.count("copied"), st.count("projected", 1)
        biased, step_on = st.count("biased", 0), st.count("step_on").sem
        shifted, exped, featured = (st.count(k) for k in ("shifted", "exped", "featured"))
        kv_done, kv_moved, qf_turned, qf_moved = (st.count(k) for k in ("kv_done", "kv_moved", "qf_turned", "qf_moved"))
        attended, summed, y_turned, y_moved = (st.count(k) for k in ("attended", "summed", "y_turned", "y_moved"))
        out_done, added = st.count("out_done"), st.count("added", 1)
        chain = st.chain("chain")
        xn = core.xn[:].rearrange("p k (b s) -> p k b s", b=B)
        x = core.x[:].rearrange("p k (s b) -> p k b s", b=B)
        loads = [(wt[c][:], w["W" + c].rearrange("(k p) n -> p k n", p=P)) for c in "qkvo"]
        loads += [(bt[c][:], w["b" + c].rearrange("(o n) -> o n", o=1).to_broadcast([P, D])) for c in "qkv"]
        loads += [(bo[:], w["bo"]), (angle[:], w["sin_cos"])]
        QK_BANK, V_BANK = 0, 2
        KV_BANK, QF_BANK, RES_BANK, Y_BANK, OUT_BANK = 5, (3, 5), ((7, 3), (4, 5)), 6, 7

        def batches(engine, body):
            with engine.Fori(0, B // 2 - 1) as i:
                body(i, False)
            body(B // 2 - 1, True)

        with nc.Block() as block:

            @block.sync
            def _(sp):
                for to, of in loads:
                    sp.dma_start(to, of).then_inc(loaded.sem, 16)
                sp.wait_ge(loaded.sem, loaded.at(16 * len(loads)))

            @block.tensor
            def _(pe):
                def projection(n, j):
                    pe.wait_ge(copied.sem, copied.at(n + 1))
                    pe.wait_ge(biased.sem, biased.at(n))
                    for t in range(TB):
                        for o, c in ((0, "q"), (D, "k")):
                            for k in range(KT):
                                nc.tensor.matmul(ps[:, QK_BANK + t, o:o + D], xb[:, j, k, t * P:(t + 1) * P],
                                                 wt[c][:, k, :], start=(k == 0), stop=(k == KT - 1))
                    for t in range(TB):
                        for k in range(KT):
                            mm = nc.tensor.matmul(ps[:, V_BANK, t * D:(t + 1) * D], xb[:, j, k, t * P:(t + 1) * P],
                                                  wt["v"][:, k, :], start=(k == 0), stop=(k == KT - 1))
                    mm.then_inc(projected.sem, 1)

                def back(n, j):
                    pe.wait_ge(featured.sem, featured.at(n + 1))
                    for br in range(BR):
                        for g in range(NG):
                            for t in range(TB):
                                mm = nc.tensor.matmul(ps[:, KV_BANK + br, g * 4 * VC:(g + 1) * 4 * VC],
                                                      feat[:, t, 1, br, g * 4:(g + 1) * 4, :].rearrange("p h f -> p (h f)"),
                                                      v[:, j, t, g * 4:(g + 1) * 4, :].rearrange("p h c -> p (h c)"),
                                                      start=(t == 0), stop=(t == TB - 1))
                    mm.then_inc(kv_done.sem, 1)
                    for br in range(BR):
                        if br == 1:
                            pe.wait_ge(kv_moved.sem, kv_moved.at(n + 1))
                        for g in range(NG):
                            for t in range(TB):
                                mm = nc.tensor.transpose(ps[:, QF_BANK[br] + g // 2, (g % 2) * S + t * P:(g % 2) * S + (t + 1) * P],
                                                         feat[:, t, 0, br, g * 4:(g + 1) * 4, :].rearrange("p h f -> p (h f)"),
                                                         core.ident[:])
                        mm.then_inc(qf_turned.sem, 1)
                    pe.wait_ge(added.sem, added.at(n))
                    pe.wait_ge(qf_moved.sem, qf_moved.at(2 * n + 2))
                    for br in range(BR):
                        for t in range(TB):
                            for g in range(NG):
                                mm = nc.tensor.matmul(ps[:, RES_BANK[br][t], g * 4 * VC:(g + 1) * 4 * VC],
                                                      qfT[:, br * NG + g, t * P:(t + 1) * P],
                                                      kv[:, br * NG + g].rearrange("p h c -> p (h c)"), start=True, stop=True)
                    mm.then_inc(attended.sem, 1)

                def output(n):
                    pe.wait_ge(summed.sem, summed.at(n + 1))
                    for c in range(KT):
                        for t in range(TB):
                            mm = nc.tensor.transpose(ps[:, Y_BANK, c * S + t * P:c * S + (t + 1) * P],
                                                     y[:, t, c * P:(c + 1) * P], core.ident[:])
                    mm.then_inc(y_turned.sem, 1)
                    pe.wait_ge(y_moved.sem, y_moved.at(n + 1))
                    for m in range(KT):
                        for k in range(KT):
                            mm = nc.tensor.matmul(ps[:, OUT_BANK, m * S:(m + 1) * S], wt["o"][:, k, m * P:(m + 1) * P],
                                                  yT[:, k, :], start=(k == 0), stop=(k == KT - 1))
                    mm.then_inc(out_done.sem, 1)

                def body(i, last):
                    for j in range(2):
                        n = i * 2 + j
                        if not (last and j == 1):
                            projection(n + 1, 1 - j)
                        back(n, j)
                        output(n)

                pe.sem_inc(projected.sem, projected.credit)
                pe.wait_ge(loaded.sem, loaded.at(16 * len(loads)))
                projection(0, 0)
                batches(pe, body)

            @block.scalar
            def _(act):
                def copy_tokens(n, j):
                    act.wait_ge(projected.sem, projected.at(n - 1))
                    act.sem_inc(step_on, 1)
                    nc.scalar.copy(xb[:, j], xn[:, :, n, :]).then_inc(copied.sem, 1)

                def exponentiate(n):
                    act.wait_ge(shifted.sem, shifted.at(n + 1))
                    nc.scalar.activation(qk[:, 0], qk[:, 0], ACT.Exp).then_inc(exped.sem, 1)

                def body(i, last):
                    for j in range(2):
                        n = i * 2 + j
                        if not last:
                            copy_tokens(n + 2, j)
                        if not (last and j == 1):
                            exponentiate(n + 1)
                        for br in range(BR):
                            act.wait_ge(qf_turned.sem, qf_turned.at(2 * n + br + 1))
                            nc.scalar.copy(qfT[:, br * NG:(br + 1) * NG].rearrange("p (a b) s -> p a (b s)", b=2),
                                           ps[:, QF_BANK[br]:QF_BANK[br] + 2, :]).then_inc(qf_moved.sem, 1)
                        act.wait_ge(y_turned.sem, y_turned.at(n + 1))
                        nc.scalar.copy(yT[:], ps[:, Y_BANK, :].rearrange("p (c s) -> p c s", c=KT)).then_inc(y_moved.sem, 1)

                copy_tokens(0, 0)
                copy_tokens(1, 1)
                exponentiate(0)
                batches(act, body)

            @block.vector
            def _(dve):
                def link(ins):
                    chain.link(dve, ins)

                rows = qk[:, 0].rearrange("p t (h d) -> p (t h) d", d=HD)

                def over_channels(s):
                    return s[:].rearrange("p t (h o) -> p (t h) o", o=1).to_broadcast([P, TB * 2 * H, HD])

                def take_projections(n, j):
                    dve.wait_ge(projected.sem, projected.at(n + 1))
                    for t in range(TB):
                        for o, c in ((0, "q"), (D, "k")):
                            nc.vector.tensor_tensor(qk[:, 0, t, o:o + D], ps[:, QK_BANK + t, o:o + D], bt[c][:], ALU.add)
                        ins = nc.vector.tensor_tensor(v[:, j, t, :, 0:HD],
                                                      ps[:, V_BANK, t * D:(t + 1) * D].rearrange("p (h d) -> p h d", d=HD),
                                                      bt["v"][:].rearrange("p (h d) -> p h d", d=HD), ALU.add)
                    ins.then_inc(biased.sem, 1)
                    dve.wait_ge(biased.sem, biased.at(n + 1))
                    link(nc.vector.tensor_reduce(mx[:].rearrange("p t h -> p (t h)"), rows, AX.X, ALU.max))
                    nc.vector.tensor_tensor(rows, rows, over_channels(mx), ALU.subtract).then_inc(shifted.sem, 1)

                def softmax(n):
                    dve.wait_ge(exped.sem, exped.at(n + 1))
                    link(nc.vector.tensor_reduce(total[:].rearrange("p t h -> p (t h)"), rows, AX.X, ALU.add))
                    link(nc.vector.reciprocal(total[:], total[:]))
                    link(nc.vector.tensor_tensor(rows, rows, over_channels(total), ALU.mult))
                    link(nc.vector.tensor_scalar(qk[:, 1], qk[:, 0], -1.0, 1.0, ALU.mult, ALU.add))

                def features(n):
                    for t in range(TB):
                        for which in range(2):
                            for br in range(BR):
                                src = qk[:, br, t, which * D:(which + 1) * D].rearrange("p (h d) -> p h d", d=HD)
                                for f in range(2):
                                    ins = nc.vector.tensor_scalar(feat[:, t, which, br, :, f * HD:(f + 1) * HD], src,
                                                                  angle[:, t, f:f + 1], None, ALU.mult)
                    ins.then_inc(featured.sem, 1)

                def move_kv(n):
                    dve.wait_ge(kv_done.sem, kv_done.at(n + 1))
                    for br in range(BR):
                        for hh in range(4):
                            r = slice(hh * F, (hh + 1) * F)
                            src = ps[r, KV_BANK + br, 0:NG * 4 * VC].rearrange("p (g h c) -> p g h c", g=NG, c=VC)[:, :, hh, :]
                            ins = nc.vector.tensor_copy(kv[r, br * NG:(br + 1) * NG, hh, :], src)
                    ins.then_inc(kv_moved.sem, 1)

                def divide(n):
                    dve.wait_ge(attended.sem, attended.at(n + 1))
                    for br in range(BR):
                        for t in range(TB):
                            res = ps[:, RES_BANK[br][t], 0:H * VC].rearrange("p (h c) -> p h c", c=VC)
                            ins = nc.vector.tensor_scalar(z[:, br, t, :], res[:, :, HD], 1e-6, None, ALU.max)
                    link(ins)
                    link(nc.vector.reciprocal(z[:], z[:]))
                    for br in range(BR):
                        for t in range(TB):
                            res = ps[:, RES_BANK[br][t], 0:H * VC].rearrange("p (h c) -> p h c", c=VC)
                            ins = nc.vector.tensor_tensor(part[:, br, t, :].rearrange("p (h d) -> p h d", d=HD),
                                                          res[:, :, 0:HD],
                                                          z[:, br, t, :].rearrange("p (h o) -> p h o", o=1).to_broadcast([P, H, HD]),
                                                          ALU.mult)
                    link(ins)
                    nc.vector.tensor_tensor(y[:], part[:, 0], part[:, 1], ALU.add).then_inc(summed.sem, 1)

                def add_output(n):
                    dve.wait_ge(out_done.sem, out_done.at(n + 1))
                    for m in range(KT):
                        ins = nc.vector.scalar_tensor_tensor(out=x[:, m, n, :], in0=ps[:, OUT_BANK, m * S:(m + 1) * S],
                                                             scalar=bo[:, m:m + 1], in1=x[:, m, n, :],
                                                             op0=ALU.add, op1=ALU.add)
                    ins.then_inc(added.sem, 1)

                def body(i, last):
                    chain.restart(dve)
                    for j in range(2):
                        n = i * 2 + j
                        more = not (last and j == 1)
                        if more:
                            dve.wait_ge(featured.sem, featured.at(n + 1))
                            take_projections(n + 1, 1 - j)
                        move_kv(n)
                        if more:
                            softmax(n + 1)
                        dve.wait_ge(added.sem, added.at(n))
                        divide(n)
                        if more:
                            features(n + 1)
                        add_output(n)

                dve.sem_inc(added.sem, added.credit)
                dve.sem_inc(biased.sem, biased.credit)
                link(nc.vector.memset(kv[:], 0.0))
                link(nc.vector.memset(v[:], 1.0))
                dve.wait_ge(loaded.sem, loaded.at(16 * len(loads)))
                take_projections(0, 0)
                softmax(0)
                features(0)
                batches(dve, body)


def memory_filter(core, name, w):
    nc = core.nc
    ps = core.psum
    PAD = TAPS - 1
    with Stage(core, name) as st:
        w1, w2 = st.buf("w1", [P, KT, D]), st.buf("w2", [P, KT, D])
        b1, b2 = st.buf("b1", [P, KT]), st.buf("b2", [P, KT])
        taps = st.buf("taps", [P, KT, TAPS + 1])
        tap_diff = st.buf("tap_diff", [P, KT, TAPS])
        p = st.buf("projected", [P, KT, B, PAD + S])
        acc = st.buf("filtered", [P, KT, B, S])
        total = st.buf("total", [P, KT, B])
        loaded, padded = st.count("loaded"), st.count("padded")
        proj_done, moved, filtered = st.count("proj_done"), st.count("moved", 4), st.count("filtered")
        out_done, added, chain = st.count("out_done"), st.count("added", 4), st.chain("chain")
        x = core.x
        loads = [(w1[:], w["W1"].rearrange("(k p) n -> p k n", p=P)), (w2[:], w["W2"].rearrange("(k p) n -> p k n", p=P)),
                 (b1[:], w["bias1"]), (b2[:], w["bias2"]), (taps[:], w["taps"])]
        with nc.Block() as block:

            @block.sync
            def _(sp):
                for to, of in loads:
                    sp.dma_start(to, of).then_inc(loaded.sem, 16)
                sp.wait_ge(loaded.sem, loaded.at(16 * len(loads)))

            @block.tensor
            def _(pe):
                pe.wait_ge(loaded.sem, loaded.at(16 * len(loads)))
                for m in range(KT):
                    for c in range(NCH):
                        n = m * NCH + c
                        if n >= 4:
                            pe.wait_ge(moved.sem, moved.at(n + 1 - 4))
                        for k in range(KT):
                            mm = nc.tensor.matmul(ps[:, n % 4, :], w1[:, k, m * P:(m + 1) * P], core.xn[:, k, c * CH:(c + 1) * CH],
                                                  start=(k == 0), stop=(k == KT - 1))
                        mm.then_inc(proj_done.sem, 1)
                pe.wait_ge(filtered.sem, filtered.at(1))
                for c in range(NCH):
                    for m in range(KT):
                        n = c * KT + m
                        if n >= 4:
                            pe.wait_ge(added.sem, added.at(n + 1 - 4))
                        for k in range(KT):
                            mm = nc.tensor.matmul(ps[:, 4 + n % 4, :], w2[:, k, m * P:(m + 1) * P],
                                                  acc[:, k].rearrange("p b s -> p (b s)")[:, c * CH:(c + 1) * CH],
                                                  start=(k == 0), stop=(k == KT - 1))
                        mm.then_inc(out_done.sem, 1)

            @block.scalar
            def _(act):
                act.sem_inc(moved.sem, moved.credit)
                act.wait_ge(loaded.sem, loaded.at(16 * len(loads)))
                for m in range(KT):
                    for c in range(NCH):
                        n = m * NCH + c
                        act.wait_ge(proj_done.sem, proj_done.at(n + 1))
                        bs = slice(c * CH // S, (c + 1) * CH // S)
                        nc.scalar.activation(p[:, m, bs, PAD:], ps[:, n % 4, :].rearrange("p (b s) -> p b s", s=S),
                                             ACT.Identity, bias=b1[:, m:m + 1]).then_inc(moved.sem, 1)

            @block.vector
            def _(dve):
                dve.sem_inc(added.sem, added.credit)
                for m in range(KT):
                    chain.link(dve, nc.vector.memset(p[:, m, :, 0:PAD], 0.0))
                dve.wait_ge(loaded.sem, loaded.at(16 * len(loads)))
                for m in range(KT):
                    chain.link(dve, nc.vector.tensor_scalar(tap_diff[:, m, :], taps[:, m, 1:], taps[:, m, 0:1], None, ALU.subtract))
                for m in range(KT):
                    dve.wait_ge(moved.sem, moved.at((m + 1) * NCH))
                    chain.link(dve, nc.vector.tensor_reduce(total[:, m, :], p[:, m, :, PAD:], AX.X, ALU.add))
                    chain.link(dve, nc.vector.tensor_scalar(total[:, m, :], total[:, m, :], taps[:, m, 0:1], None, ALU.mult))
                    chain.link(dve, nc.vector.scalar_tensor_tensor(
                        out=acc[:, m], in0=p[:, m, :, PAD:], scalar=tap_diff[:, m, 0:1],
                        in1=total[:, m, :].rearrange("p (b o) -> p b o", o=1).to_broadcast([P, B, S]),
                        op0=ALU.mult, op1=ALU.add))
                    for tap in range(1, TAPS):
                        ins = nc.vector.scalar_tensor_tensor(
                            out=acc[:, m], in0=p[:, m, :, PAD - tap:PAD - tap + S], scalar=tap_diff[:, m, tap:tap + 1],
                            in1=acc[:, m], op0=ALU.mult, op1=ALU.add)
                        if tap == TAPS - 1 and m == KT - 1:
                            ins.then_inc(filtered.sem, 1)
                        else:
                            chain.link(dve, ins)
                for c in range(NCH):
                    for m in range(KT):
                        n = c * KT + m
                        dve.wait_ge(out_done.sem, out_done.at(n + 1))
                        dst = x[:, m, c * CH:(c + 1) * CH]
                        nc.vector.scalar_tensor_tensor(out=dst, in0=ps[:, 4 + n % 4, :], scalar=b2[:, m:m + 1], in1=dst,
                                                       op0=ALU.add, op1=ALU.add).then_inc(added.sem, 1)


def stage_L1_attn(core, name, w, a):
    layernorm(core, name + "_ln", core.x, core.xn)
    linear_attention(core, name, w)


def stage_L2_attn(core, name, w, a):
    layernorm(core, name + "_ln", core.x, core.xn)
    memory_filter(core, name, w)


def lay_out_others(a, n):
    for c in "qkvo":
        a[f"L1_attn_W{c}"] = n[f"L1_attn_W{c}"]
    for c in "qkv":
        a[f"L1_attn_b{c}"] = n[f"L1_attn_b{c}"]
    a["L1_attn_bo"] = by_partition(n["L1_attn_bo"])
    index = np.float32(np.pi / 2) * np.arange(1, S + 1, dtype=np.float32) / np.float32(S)
    a["L1_attn_sin_cos"] = np.stack([np.sin(index), np.cos(index)], -1).astype(np.float32).reshape(TB, P, 2).transpose(1, 0, 2)
    p = "L2_attn_"
    a[p + "W1"], a[p + "W2"] = n[p + "W1"], n[p + "W2"]
    a[p + "bias1"], a[p + "bias2"] = by_partition(n[p + "bias1"]), by_partition(n[p + "bias2"])
    a[p + "taps"] = n[p + "memory_weights"].T.reshape(KT, P, TAPS + 1).transpose(1, 0, 2)


STAGES = ["L0_attn", "L0_xattn", "L0_ffn", "L1_attn", "L1_xattn", "L1_ffn",
          "L2_attn", "L2_xattn", "L2_ffn", "L3_attn", "L3_xattn", "L3_ffn"]


def build(nc, a, out, stages=STAGES):
    with ExitStack() as stack:
        core = Core(nc, stack)
        load_inputs(core, a)
        for name in stages:
            layer, part = name.split("_")
            w = {k[len(name) + 1:]: v for k, v in a.items() if k.startswith(name + "_")}
            STAGE[name](core, name, w, a)
        store_output(core, out)


def stage_L0_attn(core, name, w, a):
    layernorm(core, name + "_ln", core.x, core.xn)
    relative_attention(core, name, w)


def stage_L0_xattn(core, name, w, a):
    attention(core, name, w, kv="ctx")


def stage_L1_xattn(core, name, w, a):
    attention(core, name, w, kv="ctx", mask=a["mask_1x1xSxS2_if1"])


def stage_L2_xattn(core, name, w, a):
    attention(core, name, w, kv="ctx", project=False)


def stage_L3_attn(core, name, w, a):
    attention(core, name, w)


STAGE = {
    "L0_attn": stage_L0_attn, "L0_xattn": stage_L0_xattn,
    "L1_xattn": stage_L1_xattn, "L2_xattn": stage_L2_xattn,
    "L3_attn": stage_L3_attn, "L3_xattn": stage_L0_xattn,
    "L1_attn": stage_L1_attn, "L2_attn": stage_L2_attn,
    "L0_ffn": stage_L0_ffn, "L1_ffn": stage_L1_ffn, "L2_ffn": stage_L2_ffn, "L3_ffn": stage_L3_ffn,
}


def by_partition(v):
    return np.ascontiguousarray(v.reshape(-1, P).T)


def lay_out(x):
    a = {}
    n = {k: np.asarray(v) for k, v in x.items()}
    a["xT"] = n["x"].reshape(T, D).T
    a["ctxT"] = n["ctx_1024"].reshape(B * SC, D).T
    a["identity"] = np.eye(P, dtype=np.float32)
    own = np.arange(P)[:, None] // HD == np.arange(HB)
    a["key_scale"] = np.where(own, float(HD) ** -0.5, 0.0).astype(np.float32)
    a["earlier"] = np.tril(np.ones((E, E), np.float32), -1)
    a["mask_1x1xSxS2_if1"] = n["mask_1x1xSxS2_if1"]
    qkv = n["L0_attn_w_attn"]
    names = {
        "L0_attn": (qkv[:, :D], qkv[:, D:2 * D], qkv[:, 2 * D:], n["L0_attn_w_proj"], None),
        "L0_xattn": tuple(n[f"L0_xattn_w_{c}"].T for c in "qkvo") + (None,),
        "L1_xattn": tuple(n[f"L1_xattn_W_{c}"].T for c in "qkvo") + (None,),
        "L2_xattn": tuple(n[f"L2_xattn_W{c}"].T for c in "qkv") + (None, "L2_xattn_b"),
        "L3_attn": tuple(n[f"L3_attn_W{c}"] for c in "qkvo") + ("L3_attn_b",),
        "L3_xattn": tuple(n[f"L3_xattn_w{c}"].T for c in "qkvo") + ("L3_xattn_b",),
    }
    for name, (wq, wk, wv, wo, biases) in names.items():
        a[f"{name}_wq"], a[f"{name}_wk"], a[f"{name}_wv"] = wq, wk, wv
        if wo is not None:
            a[f"{name}_wo"] = wo
        if biases:
            a[f"{name}_bq"] = by_partition(n[f"{biases}q"])
            a[f"{name}_bk"] = by_partition(n[f"{biases}k"])
            a[f"{name}_bv"] = by_partition(n[f"{biases}v"])
            if wo is not None:
                a[f"{name}_bo"] = by_partition(n[f"{biases}o"])
    t, s = np.arange(P)[:, None], np.arange(S)[None, :]
    mask = np.concatenate([np.where(s[:, :P] <= t, 0.0, NEG), np.where(s <= t + P, 0.0, NEG)], 1)
    a["L0_attn_causal"] = mask.astype(np.float32)
    slopes = np.array([0.5 ** ((i + 1) * 8 / H) for i in range(H)])
    keys = np.concatenate([np.arange(P), np.arange(S)])
    alibi = -slopes[:, None] * (S - 1 - keys)[None, :]
    a["L3_attn_bias"] = (alibi[None] + mask[:, None, :]).astype(np.float32)
    embkT = n["L0_attn_embk"][::-1].T
    a["L0_attn_embkT"] = np.stack([np.pad(embkT, ((h * HD, P - (h + 1) * HD), (0, 0))) for h in range(HB)], 1)
    embv = n["L0_attn_embv"][::-1].reshape(TB, P, HD).transpose(1, 0, 2)
    a["L0_attn_embv"] = np.stack([np.pad(embv, ((0, 0), (0, 0), (h * HD, P - (h + 1) * HD))) for h in range(HB)], 2)
    lay_out_mixtures(a, n)
    lay_out_others(a, n)
    return {k: np.ascontiguousarray(v) for k, v in a.items()}


def kernel(**inputs):
    import concourse.bacc as _bacc
    from concourse.bass_utils import run_bass_kernel_spmd as _run

    nc = _bacc.Bacc("TRN2", target_bir_lowering=False, num_devices=1)
    arrays = lay_out(inputs)
    args = {k: nc.dram_tensor(f"in_{k}", v.shape, mybir.dt.from_np(v.dtype), kind="ExternalInput").ap()
            for k, v in arrays.items()}
    out = nc.dram_tensor("out_xT", (D, T), F32, kind="ExternalOutput").ap()
    build(nc, args, out)
    r = _run(nc, [{f"in_{k}": v for k, v in arrays.items()}], core_ids=[0])
    got = r.results[0]["out_xT"]
    return np.ascontiguousarray(got.T).reshape(B, S, D)
```

```python
from contextlib import ExitStack

import numpy as np
import concourse.bass as bass
from concourse import mybir

ALU = mybir.AluOpType
ACT = mybir.ActivationFunctionType
AX = mybir.AxisListType
F32 = mybir.dt.float32
F32R = mybir.dt.float32r
I32 = mybir.dt.int32

P = 128
B, S, D = 8, 256, 256
T = B * S
KT = D // P
H, HD = 16, 16
QB = D // P
HB = P // HD
VP = P + HD
TB = S // P
SC = 77
E = 8
CH = 512
NCH = T // CH
NEG = -1.0e30
LN_EPS = 1e-5
SEMAPHORES = 120
TAPS = 40


class Count:

    def __init__(self, core, name, credit=None):
        self.sem = core.semaphore(name)
        self.credit = credit + 1 if credit is not None else 0

    def at(self, events):
        return events + self.credit


class Chain:

    def __init__(self, core, name):
        self.sem = core.semaphore(name)
        self.n = 0

    def restart(self, engine):
        engine.sem_clear(self.sem)
        self.n = 0

    def link(self, engine, instruction):
        instruction.then_inc(self.sem, 1)
        self.n += 1
        engine.wait_ge(self.sem, self.n)

    def mark(self, instruction):
        instruction.then_inc(self.sem, 1)
        self.n += 1
        return self.n


class Core:

    def __init__(self, nc, stack):
        self.nc = nc
        self.stack = stack
        self.free_semaphores = sorted(nc.free_semaphores)[:SEMAPHORES]
        self.x = self.sbuf("x_residual", [P, KT, T])
        self.xn = self.sbuf("x_normed", [P, KT, T])
        self.ctx = self.sbuf("context", [P, KT, B * SC])
        self.ident = self.sbuf("identity", [P, P])
        self.mean_w = self.sbuf("mean_weights", [P, P])
        self.eps = self.sbuf("ln_eps", [P, 1])
        self.key_scale = self.sbuf("key_scale", [P, HB])
        self.tri = self.sbuf("earlier_expert", [P, E, E])
        self.psum = stack.enter_context(nc.psum_tensor("psum", [P, 8, CH], F32))

    def sbuf(self, name, shape, dtype=F32, stack=None):
        return (stack or self.stack).enter_context(self.nc.sbuf_tensor(name, shape, dtype))


class Stage:

    def __init__(self, core, name):
        self.nc, self.core, self.name = core.nc, core, name
        self.stack = ExitStack()
        self.semaphores = []

    def __enter__(self):
        return self

    def __exit__(self, *failure):
        self.nc.clear_and_free_semaphores(self.semaphores)
        self.core.free_semaphores.extend(s.num for s in self.semaphores)
        return self.stack.__exit__(*failure)

    def semaphore(self, name):
        self.semaphores.append(self.nc.alloc_semaphore(name, num=self.core.free_semaphores.pop(0)))
        return self.semaphores[-1]

    def buf(self, name, shape, dtype=F32):
        return self.stack.enter_context(self.nc.sbuf_tensor(f"{self.name}_{name}", shape, dtype))

    def count(self, name, credit=None):
        return Count(self, f"{self.name}_{name}", credit)

    def chain(self, name):
        return Chain(self, f"{self.name}_{name}")


def load_inputs(core, a):
    with Stage(core, "load") as st:
        nc = core.nc
        loaded = st.count("loaded")
        with nc.Block() as block:

            @block.sync
            def _(sp):
                sp.dma_start(core.x[:], a["xT"].rearrange("(k p) t -> p k t", p=P)).then_inc(loaded.sem, 16)
                sp.dma_start(core.ident[:], a["identity"]).then_inc(loaded.sem, 16)
                sp.dma_start(core.key_scale[:], a["key_scale"]).then_inc(loaded.sem, 16)
                sp.dma_start(core.tri[:], a["earlier"].rearrange("(o e) f -> o e f", o=1).to_broadcast([P, E, E])).then_inc(loaded.sem, 16)
                sp.dma_start(core.ctx[:], a["ctxT"].rearrange("(k p) t -> p k t", p=P)).then_inc(loaded.sem, 16)
                sp.wait_ge(loaded.sem, loaded.at(80))

            @block.vector
            def _(dve):
                nc.vector.memset(core.mean_w[:], 1.0 / D)
                nc.vector.memset(core.eps[:], LN_EPS)


def store_output(core, out):
    with Stage(core, "store") as st:
        stored = st.count("stored")
        with core.nc.Block() as block:

            @block.sync
            def _(sp):
                sp.dma_start(out.rearrange("(k p) t -> p k t", p=P), core.x[:]).then_inc(stored.sem, 16)
                sp.wait_ge(stored.sem, stored.at(16))


def layernorm(core, name, src, dst, affine=None, parts=None, preload=()):
    nc = core.nc
    CT = CH // P
    with Stage(core, name) as st:
        centred = st.buf("centred", [P, KT, T]) if affine is not None else dst
        square = st.buf("square", [P, NCH, KT, CH])
        pair = st.buf("channel_tiles_added", [P, NCH, CH])
        pair_square = st.buf("squares_added", [P, NCH, CH])
        std = st.buf("std", [P, NCH, CT])
        rstd = st.buf("rstd", [P, NCH, CT])
        gb = st.buf("gamma_beta", [P, 2, KT])
        pair_done, pair_square_done = st.count("pair_done"), st.count("pair_square_done")
        mean_done, var_done, spread = st.count("mean_done"), st.count("var_done"), st.count("spread")
        centre_done, square_done = st.count("centre_done"), st.count("square_done")
        std_done, rstd_done, normed = st.count("std_done"), st.count("rstd_done"), st.count("normed")
        split_high, loaded, chain = st.count("split_high"), st.count("loaded"), st.chain("dve_chain")
        preloaded = st.count("preloaded")
        ps = core.psum
        MEAN, VAR = 0, 4

        def tokens(c):
            return slice(c * CH, (c + 1) * CH)

        with nc.Block() as block:

            @block.sync
            def _(sp):
                if affine is not None:
                    for n, v in enumerate(affine):
                        sp.dma_start(gb[:, n, :], v).then_inc(loaded.sem, 16)
                    sp.wait_ge(loaded.sem, loaded.at(32))
                for to, of in preload:
                    sp.dma_start(to, of).then_inc(preloaded.sem, 16)
                if preload:
                    sp.wait_ge(preloaded.sem, preloaded.at(16 * len(preload)))

            @block.tensor
            def _(pe):
                for c in range(NCH):
                    pe.wait_ge(pair_done.sem, pair_done.at(c + 1))
                    nc.tensor.matmul(ps[:, MEAN + c, :], core.mean_w[:], pair[:, c, :],
                                     start=True, stop=True).then_inc(mean_done.sem, 1)
                for c in range(NCH):
                    pe.wait_ge(pair_square_done.sem, pair_square_done.at(c + 1))
                    for t in range(CT):
                        mm = nc.tensor.matmul(ps[:, VAR + c, t:t + 1], pair_square[:, c, t * P:(t + 1) * P],
                                              core.mean_w[:, 0:1], start=True, stop=True)
                    mm.then_inc(var_done.sem, 1)
                for c in range(NCH):
                    pe.wait_ge(centre_done.sem, centre_done.at(c + 1))
                    pe.wait_ge(rstd_done.sem, rstd_done.at(c + 1))
                    for t in range(CT):
                        mm = nc.tensor.transpose(ps[:, MEAN + c, t * P:(t + 1) * P],
                                                 rstd[:, c, t:t + 1].to_broadcast([P, P]), core.ident[:])
                    mm.then_inc(spread.sem, 1)

            @block.scalar
            def _(act):
                for c in range(NCH):
                    act.wait_ge(centre_done.sem, centre_done.at(c + 1))
                    nc.scalar.activation(square[:, c], centred[:, :, tokens(c)], ACT.Square).then_inc(square_done.sem, 1)
                for c in range(NCH):
                    act.wait_ge(var_done.sem, var_done.at(c + 1))
                    nc.scalar.activation(std[:, c], ps[:, VAR + c, 0:CT], ACT.Sqrt,
                                         bias=core.eps[:, 0:1]).then_inc(std_done.sem, 1)
                if parts is not None:
                    for c in range(NCH):
                        act.wait_ge(normed.sem, normed.at(c + 1))
                        nc.scalar.activation(parts[0][:, :, tokens(c)], dst[:, :, tokens(c)],
                                             ACT.Copy).then_inc(split_high.sem, 1)

            @block.gpsimd
            def _(pool):
                for c in range(NCH):
                    pool.wait_ge(square_done.sem, square_done.at(c + 1))
                    nc.gpsimd.tensor_tensor(pair_square[:, c], square[:, c, 0], square[:, c, 1],
                                            ALU.add).then_inc(pair_square_done.sem, 1)
                if parts is not None:
                    for c in range(NCH):
                        pool.wait_ge(split_high.sem, split_high.at(c + 1))
                        nc.gpsimd.tensor_tensor(parts[1][:, :, tokens(c)], dst[:, :, tokens(c)],
                                                parts[0][:, :, tokens(c)].bitcast(F32), ALU.subtract)

            @block.vector
            def _(dve):
                for c in range(NCH):
                    nc.vector.tensor_tensor(pair[:, c], src[:, 0, tokens(c)], src[:, 1, tokens(c)],
                                            ALU.add).then_inc(pair_done.sem, 1)
                for c in range(NCH):
                    dve.wait_ge(mean_done.sem, mean_done.at(c + 1))
                    nc.vector.tensor_tensor(centred[:, :, tokens(c)], src[:, :, tokens(c)],
                                            ps[:, MEAN + c:MEAN + c + 1, :].to_broadcast([P, KT, CH]),
                                            ALU.subtract).then_inc(centre_done.sem, 1)
                if affine is not None:
                    dve.wait_ge(loaded.sem, loaded.at(32))
                for c in range(NCH):
                    dve.wait_ge(std_done.sem, std_done.at(c + 1))
                    nc.vector.reciprocal(rstd[:, c], std[:, c]).then_inc(rstd_done.sem, 1)
                for c in range(NCH):
                    dve.wait_ge(spread.sem, spread.at(c + 1))
                    dve.wait_ge(square_done.sem, square_done.at(c + 1))
                    scale = ps[:, MEAN + c:MEAN + c + 1, :].to_broadcast([P, KT, CH])
                    scaled = nc.vector.tensor_tensor(centred[:, :, tokens(c)], centred[:, :, tokens(c)], scale, ALU.mult)
                    if affine is None:
                        scaled.then_inc(normed.sem, 1)
                        continue
                    chain.link(dve, scaled)
                    for k in range(KT):
                        ins = nc.vector.tensor_scalar(centred[:, k, tokens(c)], centred[:, k, tokens(c)],
                                                      gb[:, 0, k:k + 1], gb[:, 1, k:k + 1], ALU.mult, ALU.add)
                    chain.link(dve, ins)
                    nc.vector.tensor_tensor(dst[:, :, tokens(c)], dst[:, :, tokens(c)], centred[:, :, tokens(c)],
                                            ALU.add).then_inc(normed.sem, 1)


def attention(core, name, w, kv="self", mask=None, project=True, rel=None):
    nc = core.nc
    ps = core.psum
    causal = kv == "self"
    PH = 1 if causal else 2
    NS = H // PH
    NK = S if causal else SC
    SEG = [(0, P), (P, S)] if causal else [(0, PH * SC), (PH * SC, PH * SC)]
    W = SEG[1][0] + SEG[1][1]
    KP = P if causal else SC
    SB = NK // P if causal else 1
    if causal:
        TR = [[(0, 0, 0), (P, 0, 1), (2 * P, 1, 1)]]
    else:
        TR = [[(t * PH * SC + i * SC, 0, t) for t in range(TB)] for i in range(PH)]
    TW = len(TR[0]) * P
    T_LAG, COPY_LAG, Y_LAG = 2, 3, 4
    NPROJ = 3
    K_PER_STEP = 1 if causal else 4
    PROJ_AT = [0, 3, 4 + HB // K_PER_STEP]
    EVAC_AT = {1: (0, []), PROJ_AT[2] + 1: (2, [])}
    for k_step in range(HB // K_PER_STEP):
        EVAC_AT[4 + k_step] = (1, range(k_step * K_PER_STEP, (k_step + 1) * K_PER_STEP))
    RECIP_AT, SPREAD_AT, NORM_AT, BIAS_AT = 1, 2, Y_LAG, Y_LAG + 1
    OUT_AT, ADD_AT = (8, 10) if causal else (6, 7)
    MASK_HEADS = 2
    R = 4
    T_BANK, Y_BANK, P_BANK = 3, 5, 7
    PERIOD = 2 * NS
    S_BANK = [u % 3 for u in range(PERIOD)]
    if PERIOD % 3 == 1:
        S_BANK[-1] = 1
    S_AGO = [next(d for d in range(1, PERIOD) if S_BANK[(u - d) % PERIOD] == S_BANK[u]) for u in range(PERIOD)]

    with Stage(core, name) as st:
        wq = st.buf("wq", [P, KT, D])
        wk = st.buf("wk", [P, KT, D])
        wv = st.buf("wv", [P, KT, D])
        wo = st.buf("wo", [P, KT, D])
        bq = st.buf("bq", [P, QB])
        bk = st.buf("bk", [P, QB])
        bk_kept = st.buf("bk_kept", [P, HB, QB])
        bv = st.buf("bv", [P, KT])
        bo = st.buf("bo", [P, KT])
        xb = st.buf("tokens", [P, 2, KT, S])
        kvb = xb if causal else st.buf("ctx_tokens", [P, 2, KT, SC])
        q_sb = st.buf("q", [P, 2, QB, S])
        k_sb = st.buf("k", [P, 2, QB, HB, NK])
        v_sb = st.buf("v", [P, 2, SB, QB, HB * VP])
        s_sb = st.buf("scores", [P, R, W])
        top = st.buf("max", [P, R, PH * TB])
        p_sb = st.buf("probs", [P, R, W])
        pT = st.buf("probsT", [P, 2, PH * TW])
        sums = st.buf("sums", [P, 2, TB, H])
        rsum = st.buf("rsums", [P, TB, H])
        rsum_wide = st.buf("rsums_by_channel", [P, TB, D])
        divisor = st.buf("divisor", [P, KT, S])
        y_sb = st.buf("y", [P, 2, KT, S])
        yT = st.buf("yT", [P, 2, KT, S]) if "bv" in w else y_sb
        if causal:
            bias = st.buf("bias", [P, 2 if rel else 1, H, W])
            cmask = st.buf("causal", [P, W])
        if mask is not None:
            mask_i = st.buf("mask_int", [P, TB, SC], I32)
            mask_off = st.buf("mask_off", [P, TB, PH, SC])
            mask_on = st.buf("mask_on", [P, TB, PH, SC])
        copied, projected, evacuated = st.count("copied"), st.count("projected", 0), st.count("evacuated")
        scored = st.count("scored")
        taken = st.count("taken", PERIOD)
        ready = st.count("ready", PERIOD)
        exped, summed = st.count("exped", R), st.count("summed", R)
        transposed, turned = st.count("transposed", R), st.count("turned", 2)
        valued = st.count("valued", 2)
        widened, spread, spread_moved = st.count("widened", 1), st.count("spread"), st.count("spread_moved", 1)
        normed, y_biased, zeroed = st.count("normed"), st.count("y_biased"), st.count("v_zeroed")
        y_done = y_biased if "bv" in w else normed
        out_done, added = st.count("out_done"), st.count("added", 2)
        step_on = st.count("step_on").sem
        bias_in, bias_used = [st.count(f"bias_in{j}") for j in range(2)], st.count("bias_used", 2)
        bias_masked = st.count("bias_masked")
        p_out = [st.count(f"probs_out{r}", 32) for r in range(R)] if rel else []
        chain, act_chain = st.chain("chain"), st.chain("act_chain")
        bank_free = taken if causal or mask is not None else ready
        xn = core.xn[:].rearrange("p k (b s) -> p k b s", b=B)
        x = core.x[:].rearrange("p k (b s) -> p k b s", b=B)
        ctx = core.ctx[:].rearrange("p k (b s) -> p k b s", b=B)
        loads = [(wq[:], w["wq"].rearrange("(k p) n -> p k n", p=P)), (wk[:], w["wk"].rearrange("(k p) n -> p k n", p=P)),
                 (wv[:], w["wv"].rearrange("(k p) n -> p k n", p=P))]
        if project:
            loads.append((wo[:], w["wo"].rearrange("(k p) n -> p k n", p=P)))
        loads += [(t[:], w[key]) for t, key in [(bq, "bq"), (bk, "bk"), (bv, "bv"), (bo, "bo")] if key in w]
        if causal:
            loads.append((cmask[:], w["causal"]) if rel else (bias[:, 0], w["bias"]))
        if mask is not None:
            loads.append((mask_i[:], mask.rearrange("a b (t p) s -> p (a b t) s", p=P)))
        loaded = st.count("loaded")
        if not rel:
            layernorm(core, name + "_ln", core.x, core.xn, preload=loads)

        def batches(engine, body):
            body(0, True, False)
            with engine.Fori(1, B // 2 - 1) as i:
                body(i, False, False)
            body(B // 2 - 1, False, True)

        def is_first(n):
            return isinstance(n, int) and n == 0

        def bank_of(n, g):
            return (P_BANK, Y_BANK, Y_BANK + 1)[g] if is_first(n) else P_BANK

        def buffer_of(j, s):
            return (j * NS + s) % R

        with nc.Block() as block:

            @block.sync
            def _(sp):
                if not rel:
                    return

                def fetch_bias(n, i, j):
                    sp.wait_ge(bias_used.sem, bias_used.at(n - 1))
                    sp.dma_start(bias[:, j, :, 0:P], rel["scores0_read"][n]).then_inc(bias_in[j].sem, 16)
                    sp.dma_start(bias[:, j, :, P:W], rel["scores1_read"][n]).then_inc(bias_in[j].sem, 16)

                def body(i, first, last):
                    for j in range(2):
                        n = i * 2 + j
                        for s in range(NS):
                            if s == 4 and not (last and j == 1):
                                fetch_bias(n + 1, i + j, 1 - j)
                            r = buffer_of(j, s)
                            sp.wait_ge(exped.sem, exped.at(n * NS + s + 1))
                            sp.dma_start(rel["probs0_write"][n, s], p_sb[:, r, 0:P]).then_inc(p_out[r].sem, 16)
                            sp.dma_start(rel["probs1_write"][n, s], p_sb[:, r, P:W]).then_inc(p_out[r].sem, 16)

                for done in p_out:
                    sp.sem_inc(done.sem, done.credit)
                for to, of in loads:
                    sp.dma_start(to, of).then_inc(loaded.sem, 16)
                fetch_bias(0, 0, 0)
                batches(sp, body)
                sp.wait_ge(loaded.sem, loaded.at(16 * len(loads)))
                for done in p_out:
                    sp.wait_ge(done.sem, done.at(32 * B * H // R))

            @block.gpsimd
            def _(pool):
                def copy_tokens(n, j):
                    if not (isinstance(n, int) and n < 2):
                        pool.wait_ge(projected.sem, projected.at((n - 1) * NPROJ))
                    pool.sem_inc(step_on, 1)
                    if not causal:
                        nc.gpsimd.tensor_copy(kvb[:, j], ctx[:, :, n, :])
                    nc.gpsimd.tensor_copy(xb[:, j], xn[:, :, n, :]).then_inc(copied.sem, 1)

                def mask_scores(i, j):
                    pool.wait_ge(bias_in[j].sem, bias_in[j].at(32 * (i + 1)))
                    for h in range(0, H, MASK_HEADS):
                        nc.gpsimd.tensor_tensor(bias[:, j, h:h + MASK_HEADS], bias[:, j, h:h + MASK_HEADS],
                                                cmask[:].rearrange("p (o w) -> p o w", o=1).to_broadcast([P, MASK_HEADS, W]),
                                                ALU.add).then_inc(bias_masked.sem, 1)

                copy_tokens(1, 1)
                if rel:
                    pool.wait_ge(loaded.sem, loaded.at(16 * len(loads)))
                with pool.Fori(0, B // 2 - 1) as i:
                    for j in range(2):
                        if rel:
                            mask_scores(i, j)
                        copy_tokens(i * 2 + j + 2, j)
                if rel:
                    for j in range(2):
                        mask_scores(B // 2 - 1, j)

            @block.tensor
            def _(pe):
                def projection(n, j, g):
                    bank, queries, keys = bank_of(n, g), xb[:, j], kvb[:, j]
                    if is_first(n):
                        queries, keys = xn[:, :, 0, :], xn[:, :, 0, :] if causal else ctx[:, :, 0, :]
                    else:
                        pe.wait_ge(copied.sem, copied.at(n))
                    if not is_first(n):
                        pe.wait_ge(evacuated.sem, evacuated.at(n * NPROJ + g))
                    if g == 1 and not rel:
                        pe.wait_ge(spread_moved.sem, spread_moved.at(n - 1))
                    if g == NPROJ - 1:
                        for t in range(SB):
                            for k in range(KT):
                                mm = nc.tensor.matmul(ps[0:KP, bank, t * D:(t + 1) * D],
                                                      keys[:, k, t * P:t * P + KP], wv[:, k, :],
                                                      start=(k == 0), stop=(k == KT - 1))
                    else:
                        wt, src, n_cols = (wq, queries, S) if g == 0 else (wk, keys, NK)
                        for m in range(QB):
                            for k in range(KT):
                                mm = nc.tensor.matmul(ps[:, bank, m * S:m * S + n_cols],
                                                      wt[:, k, m * P:(m + 1) * P], src[:, k, :],
                                                      start=(k == 0), stop=(k == KT - 1))
                    mm.then_inc(projected.sem, 1)

                def scores(n, j, s):
                    u = j * NS + s
                    if s == 0:
                        pe.wait_ge(evacuated.sem, evacuated.at((n + 1) * NPROJ - 1))
                    pe.wait_ge(bank_free.sem, bank_free.at(n * NS + s + 1 - S_AGO[u]))
                    blk, h = s * PH // HB, s * PH % HB
                    for t, (c0, nk) in enumerate(SEG):
                        keys = k_sb[:, j, blk, h:h + PH, 0:nk // PH].rearrange("p h s -> p (h s)")
                        mm = nc.tensor.matmul(ps[:, S_BANK[u], c0:c0 + nk], q_sb[:, j, blk, t * P:(t + 1) * P],
                                              keys, start=True, stop=True)
                    mm.then_inc(scored.sem, 1)

                def transposes(n, j, s):
                    pe.wait_ge(exped.sem, exped.at(n * NS + s + 1))
                    pe.wait_ge(turned.sem, turned.at(n * NS + s - 1))
                    for i in range(PH):
                        for o, (c0, _, _) in enumerate(TR[i]):
                            mm = nc.tensor.transpose(ps[0:KP, T_BANK + s % 2, i * TW + o * P:i * TW + (o + 1) * P],
                                                     p_sb[:, buffer_of(j, s), c0:c0 + KP], core.ident[:])
                    mm.then_inc(transposed.sem, 1)

                def values(n, j, s):
                    pe.wait_ge(turned.sem, turned.at(n * NS + s + 1))
                    if s == 0:
                        pe.wait_ge(evacuated.sem, evacuated.at((n + 1) * NPROJ))
                        pe.wait_ge(added.sem, added.at(n - 1))
                    for i in range(PH):
                        blk, h = divmod(s * PH + i, HB)
                        for sb in range(SB):
                            o = sum(1 for _, b, _ in TR[i] if b < sb)
                            mm = nc.tensor.matmul(ps[:, Y_BANK + j, blk * S + sb * P:(blk + 1) * S],
                                                  v_sb[0:KP, j, sb, blk, h * P:(h + 1) * P],
                                                  pT[0:KP, s % 2, i * TW + o * P:i * TW + (o + TB - sb) * P],
                                                  start=(h == 0 and sb == 0), stop=(h == HB - 1 and sb == SB - 1))
                    mm.then_inc(valued.sem, 1)

                def spread_sums(n, behind):
                    pe.wait_ge(widened.sem, widened.at(n + 1))
                    if behind:
                        pe.wait_ge(evacuated.sem, evacuated.at((n + 2) * NPROJ + 1))
                    for c in range(KT):
                        for t in range(TB):
                            mm = nc.tensor.transpose(ps[:, P_BANK, c * S + t * P:c * S + (t + 1) * P],
                                                     rsum_wide[:, t, c * P:(c + 1) * P], core.ident[:])
                    mm.then_inc(spread.sem, 1)

                def output(n, j):
                    pe.wait_ge(y_done.sem, y_done.at(n + 1))
                    for m in range(KT):
                        for k in range(KT):
                            mm = nc.tensor.matmul(ps[:, Y_BANK + j, m * S:(m + 1) * S], wo[:, k, m * P:(m + 1) * P],
                                                  yT[:, j, k, :], start=(k == 0), stop=(k == KT - 1))
                    mm.then_inc(out_done.sem, 1)

                def late(work, lag, n, j, s, before):
                    if s >= lag:
                        if s - lag < NS:
                            work(n, j, s - lag)
                    elif before:
                        work(n - 1, 1 - j, NS + s - lag)

                def body(i, first, last):
                    for j in range(2):
                        n = i * 2 + j
                        before, behind = not (first and j == 0), not (last and j == 1)
                        for s in range(NS):
                            scores(n, j, s)
                            late(transposes, T_LAG, n, j, s, before)
                            late(values, Y_LAG, n, j, s, before)
                            if s in PROJ_AT and behind:
                                projection(n + 1, 1 - j, PROJ_AT.index(s))
                            if before and not rel:
                                if s == SPREAD_AT:
                                    spread_sums(n - 1, behind)
                                if s == OUT_AT and project:
                                    output(n - 1, 1 - j)

                pe.sem_inc(transposed.sem, transposed.credit)
                pe.sem_inc(valued.sem, valued.credit)
                pe.sem_inc(projected.sem, projected.credit)
                if rel:
                    pe.wait_ge(loaded.sem, loaded.at(16 * len(loads)))
                for g in range(NPROJ):
                    projection(0, 0, g)
                batches(pe, body)
                for s in range(NS, NS + Y_LAG):
                    late(transposes, T_LAG, B - 1, 1, s, True)
                    late(values, Y_LAG, B - 1, 1, s, True)
                if not rel:
                    spread_sums(B - 1, False)
                    if project:
                        output(B - 1, 1)

            @block.scalar
            def _(act):
                def evacuate(n, j, g, heads=range(HB)):
                    act.wait_ge(projected.sem, projected.at(n * NPROJ + g + 1))
                    bank = bank_of(n, g)
                    src = ps[:, bank, :].rearrange("p (m s) -> p m s", m=2)
                    if g == NPROJ - 1:
                        if isinstance(n, int) and n < 2:
                            act.wait_ge(zeroed.sem, zeroed.at(1))
                        else:
                            act.wait_ge(valued.sem, valued.at((n - 1) * NS))
                        for sb in range(SB):
                            heads = v_sb[0:KP, j, sb].rearrange("p b (h c) -> p b h c", c=VP)[:, :, :, 0:HD]
                            ins = nc.scalar.copy(heads, ps[0:KP, bank, sb * D:(sb + 1) * D]
                                                 .rearrange("p (b h d) -> p b h d", b=QB, d=HD))
                    elif g == 0:
                        if "bq" in w:
                            for m in range(QB):
                                ins = nc.scalar.activation(q_sb[:, j, m, :], src[:, m, :], ACT.Identity, bias=bq[:, m:m + 1])
                        else:
                            ins = nc.scalar.copy(q_sb[:, j], src)
                    elif "bk" in w:
                        for h in heads:
                            for m in range(QB):
                                ins = nc.scalar.activation(k_sb[:, j, m, h, :], src[:, m, 0:NK], ACT.Identity,
                                                           bias=bk_kept[:, h, m:m + 1],
                                                           scale=core.key_scale[:, h:h + 1])
                    else:
                        for h in heads:
                            ins = nc.scalar.mul(k_sb[:, j, :, h, :], src[:, :, 0:NK],
                                                core.key_scale[:, h:h + 1])
                    if g != 1 or heads[-1] == HB - 1:
                        ins.then_inc(evacuated.sem, 1)

                def exponentiate(n, j, s):
                    act.wait_ge(ready.sem, ready.at(n * NS + s + 1))
                    act.wait_ge(transposed.sem, transposed.at(n * NS + s + 1 - R))
                    r = buffer_of(j, s)
                    if rel:
                        act.wait_ge(p_out[r].sem, p_out[r].at(32 * (n * (NS // R) + s // R)))
                    if causal:
                        for t, (c0, nk) in enumerate(SEG):
                            ins = nc.scalar.activation(p_sb[:, r, c0:c0 + nk], s_sb[:, r, c0:c0 + nk], ACT.Exp,
                                                       bias=top[:, r, t:t + 1], accum_out=sums[:, j, t, s:s + 1])
                    else:
                        act.wait_ge(summed.sem, summed.at(n * NS + s + 1 - R))
                        ins = nc.scalar.activation(p_sb[:, r, :], s_sb[:, r, :], ACT.Exp)
                    ins.then_inc(exped.sem, 1)

                def turn(n, j, s):
                    act.wait_ge(transposed.sem, transposed.at(n * NS + s + 1))
                    act.wait_ge(valued.sem, valued.at(n * NS + s - 1))
                    nc.scalar.copy(pT[0:KP, s % 2, :], ps[0:KP, T_BANK + s % 2, 0:PH * TW]).then_inc(turned.sem, 1)

                def move_spread(n):
                    act.wait_ge(spread.sem, spread.at(n + 1))
                    act.wait_ge(normed.sem, normed.at(n))
                    nc.scalar.copy(divisor[:], ps[:, P_BANK, :].rearrange("p (c s) -> p c s", c=KT)).then_inc(spread_moved.sem, 1)

                def add_bias(n, j):
                    act.wait_ge(normed.sem, normed.at(n + 1))
                    for c in range(KT):
                        ins = nc.scalar.activation(yT[:, j, c, :], y_sb[:, j, c, :], ACT.Identity, bias=bv[:, c:c + 1])
                    ins.then_inc(y_biased.sem, 1)

                def body(i, first, last):
                    for j in range(2):
                        n = i * 2 + j
                        before, behind = not (first and j == 0), not (last and j == 1)
                        for s in range(NS):
                            if s >= COPY_LAG:
                                turn(n, j, s - COPY_LAG)
                            elif before:
                                turn(n - 1, 1 - j, NS + s - COPY_LAG)
                            if s in EVAC_AT and behind:
                                evacuate(n + 1, 1 - j, *EVAC_AT[s])
                            if s == SPREAD_AT and before and not rel:
                                move_spread(n - 1)
                            if s == BIAS_AT and before and "bv" in w:
                                add_bias(n - 1, 1 - j)
                            exponentiate(n, j, s)

                act.sem_inc(exped.sem, exped.credit)
                act.sem_inc(turned.sem, turned.credit)
                act.sem_inc(spread_moved.sem, spread_moved.credit)
                if "bk" in w:
                    for h in range(HB):
                        ins = nc.scalar.mul(bk_kept[:, h], bk[:], core.key_scale[:, h:h + 1])
                    act_chain.link(act, ins)
                for g in range(NPROJ):
                    evacuate(0, 0, g)
                batches(act, body)
                for s in range(NS - COPY_LAG, NS):
                    turn(B - 1, 1, s)
                if not rel:
                    move_spread(B - 1)
                if "bv" in w:
                    add_bias(B - 1, 1)

            @block.vector
            def _(dve):
                def prepare_scores(n, j, s):
                    if rel and s % MASK_HEADS == 0:
                        dve.wait_ge(bias_masked.sem, bias_masked.at(n * (NS // MASK_HEADS) + s // MASK_HEADS + 1))
                    r = buffer_of(j, s)
                    dve.wait_ge(scored.sem, scored.at(n * NS + s + 1))
                    dve.wait_ge(exped.sem, exped.at(n * NS + s + 1 - R))
                    tile = ps[:, S_BANK[j * NS + s], 0:W]
                    if causal:
                        nc.vector.tensor_tensor(s_sb[:, r, :], tile, bias[:, j if rel else 0, s, :],
                                                ALU.add).then_inc(taken.sem, 1)
                        dve.wait_ge(taken.sem, taken.at(n * NS + s + 1))
                        for t, (c0, nk) in enumerate(SEG):
                            ins = nc.vector.tensor_reduce(top[:, r, t:t + 1], s_sb[:, r, c0:c0 + nk], AX.X, ALU.max,
                                                          negate=True)
                        ins.then_inc(ready.sem, 1)
                        return
                    if mask is not None:
                        nc.vector.tensor_tensor(s_sb[:, r, :], tile, mask_on[:].rearrange("p t i s -> p (t i s)"),
                                                ALU.mult).then_inc(taken.sem, 1)
                        dve.wait_ge(taken.sem, taken.at(n * NS + s + 1))
                        tile = s_sb[:, r, :]
                        chain.link(dve, nc.vector.tensor_tensor(tile, tile, mask_off[:].rearrange("p t i s -> p (t i s)"), ALU.add))
                    rows = tile.rearrange("p (a s) -> p a s", s=SC)
                    chain.link(dve, nc.vector.tensor_reduce(top[:, r, :], rows, AX.X, ALU.max))
                    nc.vector.tensor_tensor(s_sb[:, r, :].rearrange("p (a s) -> p a s", s=SC), rows,
                                            top[:, r, :].rearrange("p (a o) -> p a o", o=1).to_broadcast([P, PH * TB, SC]),
                                            ALU.subtract).then_inc(ready.sem, 1)

                def sum_rows(n, j, s):
                    dve.wait_ge(exped.sem, exped.at(n * NS + s + 1))
                    nc.vector.tensor_reduce(sums[:, j, :, s * PH:(s + 1) * PH],
                                            p_sb[:, buffer_of(j, s), :].rearrange("p (t i s) -> p t i s", i=PH, s=SC),
                                            AX.X, ALU.add).then_inc(summed.sem, 1)

                def widen_sums(n, j):
                    if causal:
                        dve.wait_ge(exped.sem, exped.at((n + 1) * NS))
                    else:
                        dve.wait_ge(summed.sem, summed.at((n + 1) * NS))
                    if rel:
                        nc.vector.tensor_copy(rel["sums"][:, n, :],
                                              sums[:, j].rearrange("p t h -> p (t h)")).then_inc(bias_used.sem, 1)
                        return
                    dve.wait_ge(widened.sem, widened.at(n))
                    chain.link(dve, nc.vector.reciprocal(rsum[:], sums[:, j]))
                    if not (isinstance(n, int) and n == 0):
                        dve.wait_ge(spread.sem, spread.at(n))
                    nc.vector.tensor_copy(rsum_wide[:].rearrange("p t (h d) -> p t h d", d=HD),
                                          rsum[:].rearrange("p t (h o) -> p t h o", o=1).to_broadcast([P, TB, H, HD])
                                          ).then_inc(widened.sem, 1)

                def normalise(n, j):
                    dve.wait_ge(valued.sem, valued.at((n + 1) * NS))
                    y = ps[:, Y_BANK + j, :].rearrange("p (c s) -> p c s", c=KT)
                    if rel:
                        nc.vector.tensor_copy(rel["y"][:, :, n, :], y).then_inc(added.sem, 1)
                        return
                    dve.wait_ge(spread_moved.sem, spread_moved.at(n + 1))
                    nc.vector.tensor_tensor(y_sb[:, j], y, divisor[:], ALU.mult).then_inc(normed.sem, 1)

                def add_output(n, j):
                    done = out_done if project else y_done
                    dve.wait_ge(done.sem, done.at(n + 1))
                    for m in range(KT):
                        src = ps[:, Y_BANK + j, m * S:(m + 1) * S] if project else yT[:, j, m, :]
                        dst = x[:, m, n, :]
                        if "bo" in w:
                            ins = nc.vector.scalar_tensor_tensor(out=dst, in0=src, scalar=bo[:, m:m + 1], in1=dst,
                                                                 op0=ALU.add, op1=ALU.add)
                        else:
                            ins = nc.vector.tensor_tensor(dst, src, dst, ALU.add)
                    ins.then_inc(added.sem, 1)

                def body(i, first, last):
                    chain.restart(dve)
                    for j in range(2):
                        n = i * 2 + j
                        before = not (first and j == 0)
                        for s in range(NS):
                            if s == RECIP_AT and before:
                                widen_sums(n - 1, 1 - j)
                            if s == NORM_AT and before:
                                normalise(n - 1, 1 - j)
                            prepare_scores(n, j, s)
                            if not causal:
                                if s >= 1:
                                    sum_rows(n, j, s - 1)
                                elif before:
                                    sum_rows(n - 1, 1 - j, NS - 1)
                            if s == ADD_AT and before and not rel:
                                add_output(n - 1, 1 - j)

                nc.vector.memset(v_sb[:], 0.0).then_inc(zeroed.sem, 1)
                for c in (taken, ready, summed, added, bias_used, widened):
                    dve.sem_inc(c.sem, c.credit)
                if mask is not None:
                    for i in range(PH):
                        chain.link(dve, nc.vector.tensor_scalar(mask_off[:, :, i, :], mask_i[:], 0.0, None, ALU.is_equal))
                    chain.link(dve, nc.vector.tensor_scalar(mask_on[:], mask_off[:], -1.0, 1.0, ALU.mult, ALU.add))
                    chain.link(dve, nc.vector.tensor_scalar(mask_off[:], mask_off[:], -1.0e9, None, ALU.mult))
                batches(dve, body)
                if not causal:
                    sum_rows(B - 1, 1, NS - 1)
                widen_sums(B - 1, 1)
                normalise(B - 1, 1)
                if not rel:
                    add_output(B - 1, 1)


def relative_attention(core, name, w):
    nc = core.nc
    W0, W1 = P, S
    scores0 = nc.dram_tensor("rel_scores0", (B, H, P * W0), F32).ap()
    scores1 = nc.dram_tensor("rel_scores1", (B, H, P * W1), F32).ap()
    Z0, Z1 = P, P - 1
    probs0 = nc.dram_tensor("rel_probs0", (B, H, Z0 + P * W0), F32).ap()
    probs1 = nc.dram_tensor("rel_probs1", (B, H, Z1 + P * W1), F32).ap()

    def dram_view(t, offset, pitch, rows, cols):
        flat = t.shape[2]
        return bass.AP(tensor=t.tensor, offset=offset, ap=[[H * flat, B], [pitch, rows], [flat, H], [1, cols]])

    rel = {
        "scores0_read": dram_view(scores0, P - 1, W0 - 1, P, W0),
        "scores1_read": dram_view(scores1, P - 1, W1 - 1, P, W1),
        "probs0_write": probs0[:, :, Z0:].rearrange("b h (t s) -> b h t s", t=P),
        "probs1_write": probs1[:, :, Z1:].rearrange("b h (t s) -> b h t s", t=P),
    }
    scores0_write = scores0.rearrange("b h (t u) -> b t h u", t=P)
    scores1_write = scores1.rearrange("b h (t u) -> b t h u", t=P)
    probs0_read = dram_view(probs0, 1, W0 + 1, P, W0)
    probs1_read = dram_view(probs1, 0, W1 + 1, P, W1)

    with Stage(core, name + "_rel") as keep:
        rel["y"] = core.xn[:].rearrange("p k (b s) -> p k b s", b=B)
        rel["sums"] = keep.buf("sums", [P, B, TB * H])
        relative_scores(core, name + "_scores", w, scores0_write, scores1_write, probs0[:, :, 0:Z0], probs1[:, :, 0:Z1])
        attention(core, name, w, rel=rel)
        relative_values(core, name + "_values", w, rel, probs0_read, probs1_read)


def relative_scores(core, name, w, scores0_write, scores1_write, zeros0, zeros1):
    nc = core.nc
    ps = core.psum
    with Stage(core, name) as st:
        wq = st.buf("wq", [P, KT, D])
        embk = st.buf("embk", [P, HB, S])
        q_sb = st.buf("q", [P, 2, QB, S])
        dist = st.buf("by_distance", [P, 2, H, P + S])
        zeros = st.buf("zeros", [P, P])
        loaded, projected, evacuated = st.count("loaded"), st.count("projected"), st.count("evacuated")
        scored, moved = st.count("scored"), [st.count(f"moved{parity}", 2) for parity in range(2)]
        stored = [st.count(f"stored{j}", 0) for j in range(2)]
        zeroed, cleared = st.count("zeroed"), st.count("cleared")
        xn = core.xn[:].rearrange("p k (b s) -> p k b s", b=B)
        Q_BANK, S_BANK = 0, 4
        TURNS = [(t, h, CH // ((t + 1) * P)) for blk in range(QB) for t in range(TB)
                 for h in range(blk * HB, (blk + 1) * HB, CH // ((t + 1) * P))]
        NU = len(TURNS)
        NEXT_AT = NU // 2

        def batches(engine, body):
            with engine.Fori(0, B // 2 - 1) as i:
                body(i, False)
            body(B // 2 - 1, True)

        def move(engine, copy, n, i, j, u):
            engine.wait_ge(scored.sem, scored.at(n * NU + u + 1))
            if u < 2:
                engine.wait_ge(stored[j].sem, stored[j].at(32 * i))
            t, h, heads = TURNS[u]
            to = dist[:, j, h:h + heads, P:P + S] if t else dist[:, j, h:h + heads, 0:P]
            copy(to, ps[:, S_BANK + u % 4, :].rearrange("p (h s) -> p h s", h=heads)).then_inc(moved[u % 2].sem, 1)

        with nc.Block() as block:

            @block.sync
            def _(sp):
                sp.dma_start(wq[:], w["wq"].rearrange("(k p) n -> p k n", p=P)).then_inc(loaded.sem, 16)
                sp.dma_start(embk[:], w["embkT"]).then_inc(loaded.sem, 16)
                sp.wait_ge(cleared.sem, cleared.at(1))
                sp.dma_start(zeros0.rearrange("b h z -> (b h) z"), zeros[:, 0:zeros0.shape[2]]).then_inc(zeroed.sem, 16)
                sp.dma_start(zeros1.rearrange("b h z -> (b h) z"), zeros[:, 0:zeros1.shape[2]]).then_inc(zeroed.sem, 16)
                for j in range(2):
                    sp.sem_inc(stored[j].sem, stored[j].credit)
                with sp.Fori(0, B // 2) as i:
                    for j in range(2):
                        n = i * 2 + j
                        for done in moved:
                            sp.wait_ge(done.sem, done.at((n + 1) * NU // 2))
                        sp.dma_start(scores0_write[n], dist[:, j, :, 0:P]).then_inc(stored[j].sem, 16)
                        sp.dma_start(scores1_write[n], dist[:, j, :, P:P + S]).then_inc(stored[j].sem, 16)
                for j in range(2):
                    sp.wait_ge(stored[j].sem, stored[j].at(32 * B // 2))
                sp.wait_ge(zeroed.sem, zeroed.at(32))

            @block.tensor
            def _(pe):
                def projection(n, j):
                    for m in range(QB):
                        for k in range(KT):
                            mm = nc.tensor.matmul(ps[:, Q_BANK + j, m * S:(m + 1) * S], wq[:, k, m * P:(m + 1) * P],
                                                  xn[:, k, n, :], start=(k == 0), stop=(k == KT - 1))
                    mm.then_inc(projected.sem, 1)

                def body(i, last):
                    for j in range(2):
                        n = i * 2 + j
                        pe.wait_ge(evacuated.sem, evacuated.at(n + 1))
                        for u, (t, h, heads) in enumerate(TURNS):
                            pe.wait_ge(moved[u % 2].sem, moved[u % 2].at(n * (NU // 2) + u // 2 - 1))
                            table = embk[:, h % HB:h % HB + heads, (0 if t else S - P):S]
                            nc.tensor.matmul(ps[:, S_BANK + u % 4, :], q_sb[:, j, h // HB, t * P:(t + 1) * P],
                                             table, start=True, stop=True).then_inc(scored.sem, 1)
                            if u == NEXT_AT and not (last and j == 1):
                                projection(n + 1, 1 - j)

                pe.wait_ge(loaded.sem, loaded.at(32))
                projection(0, 0)
                batches(pe, body)

            @block.scalar
            def _(act):
                def evacuate(n, j):
                    act.wait_ge(projected.sem, projected.at(n + 1))
                    nc.scalar.copy(q_sb[:, j], ps[:, Q_BANK + j, :].rearrange("p (m s) -> p m s", m=QB)).then_inc(evacuated.sem, 1)

                def body(i, last):
                    for j in range(2):
                        n = i * 2 + j
                        for u in range(1, NU, 2):
                            move(act, nc.scalar.copy, n, i, j, u)
                            if u == NEXT_AT + 1 and not (last and j == 1):
                                evacuate(n + 1, 1 - j)

                act.sem_inc(moved[1].sem, moved[1].credit)
                evacuate(0, 0)
                batches(act, body)

            @block.vector
            def _(dve):
                nc.vector.memset(zeros[:], 0.0).then_inc(cleared.sem, 1)
                dve.sem_inc(moved[0].sem, moved[0].credit)
                with dve.Fori(0, B // 2) as i:
                    for j in range(2):
                        for u in range(0, NU, 2):
                            move(dve, nc.vector.tensor_copy, i * 2 + j, i, j, u)


def relative_values(core, name, w, rel, probs0_read, probs1_read):
    nc = core.nc
    ps = core.psum
    T_BANK, Y_BANK, O_BANK = 0, 4, 6
    TILES = [P, 0, 2 * P]
    NT = len(TILES)
    with Stage(core, name) as st:
        wo = st.buf("wo", [P, KT, D])
        embv = st.buf("embv", [P, TB, HB, P])
        shifted = st.buf("by_distance", [P, 2, H, P + S])
        pT = st.buf("probsT", [P, 4, NT * P])
        rsum = st.buf("rsums", [P, 2, TB * H])
        rsum_wide = st.buf("rsums_by_channel", [P, 2, TB, D])
        y_sum = st.buf("y_sum", [P, 2, KT, S])
        yT = st.buf("yT", [P, 2, KT, S])
        loaded, shifted_in = st.count("loaded"), [st.count(f"shifted_in{j}") for j in range(2)]
        transposed, turned = st.count("transposed"), st.count("turned", 4)
        valued, normed = st.count("valued", 4), st.count("normed", 2)
        summed, recip, widened, spread = (st.count(k) for k in ("summed", "reciprocal", "widened", "spread"))
        out_done, added = st.count("out_done"), st.count("added", 2)
        SPREAD_AT, OUT_AT = 2, 7

        def batches(engine, body):
            body(0, True)
            with engine.Fori(1, B // 2) as i:
                body(i, False)

        x = core.x[:].rearrange("p k (b s) -> p k b s", b=B)
        with nc.Block() as block:

            @block.sync
            def _(sp):
                sp.dma_start(wo[:], w["wo"].rearrange("(k p) n -> p k n", p=P)).then_inc(loaded.sem, 16)
                sp.dma_start(embv[:], w["embv"]).then_inc(loaded.sem, 16)
                with sp.Fori(0, B // 2) as i:
                    for j in range(2):
                        n = i * 2 + j
                        sp.wait_ge(normed.sem, normed.at(n - 1))
                        sp.dma_start(shifted[:, j, :, 0:P], probs0_read[n]).then_inc(shifted_in[j].sem, 16)
                        sp.dma_start(shifted[:, j, :, P:P + S], probs1_read[n]).then_inc(shifted_in[j].sem, 16)
                sp.wait_ge(loaded.sem, loaded.at(32))

            @block.tensor
            def _(pe):
                def transposes(n, j, h):
                    pe.wait_ge(turned.sem, turned.at(n * H + h - 3))
                    for o in range(NT):
                        mm = nc.tensor.transpose(ps[:, T_BANK + h % 4, o * P:(o + 1) * P],
                                                 shifted[:, j, h, TILES[o]:TILES[o] + P], core.ident[:])
                    mm.then_inc(transposed.sem, 1)

                def values(n, j, h):
                    pe.wait_ge(turned.sem, turned.at(n * H + h + 1))
                    if h == 0:
                        pe.wait_ge(normed.sem, normed.at(n - 1))
                    blk, own = divmod(h, HB)
                    nc.tensor.matmul(ps[:, Y_BANK + j, blk * S:(blk + 1) * S], embv[:, 1, own, :],
                                     pT[:, h % 4, P:3 * P], start=(own == 0), stop=False)
                    mm = nc.tensor.matmul(ps[:, Y_BANK + j, blk * S + P:(blk + 1) * S], embv[:, 0, own, :],
                                          pT[:, h % 4, 0:P], start=False, stop=(own == HB - 1))
                    mm.then_inc(valued.sem, 1)

                def spread_sums(n, j):
                    pe.wait_ge(widened.sem, widened.at(n + 1))
                    pe.wait_ge(added.sem, added.at(n - 1))
                    for c in range(KT):
                        for t in range(TB):
                            mm = nc.tensor.transpose(ps[:, O_BANK + j, c * S + t * P:c * S + (t + 1) * P],
                                                     rsum_wide[:, j, t, c * P:(c + 1) * P], core.ident[:])
                    mm.then_inc(spread.sem, 1)

                def output(n, j):
                    pe.wait_ge(normed.sem, normed.at(n + 1))
                    for m in range(KT):
                        for k in range(KT):
                            mm = nc.tensor.matmul(ps[:, O_BANK + j, m * S:(m + 1) * S], wo[:, k, m * P:(m + 1) * P],
                                                  yT[:, j, k, :], start=(k == 0), stop=(k == KT - 1))
                    mm.then_inc(out_done.sem, 1)

                def body(i, first):
                    for j in range(2):
                        n = i * 2 + j
                        pe.wait_ge(shifted_in[j].sem, shifted_in[j].at(32 * (i + 1)))
                        for step in range(H + 2):
                            if step < H:
                                transposes(n, j, step)
                            if step >= 2:
                                values(n, j, step - 2)
                            if not (first and j == 0):
                                if step == SPREAD_AT:
                                    spread_sums(n - 1, 1 - j)
                                if step == OUT_AT:
                                    output(n - 1, 1 - j)

                pe.sem_inc(valued.sem, valued.credit)
                pe.wait_ge(loaded.sem, loaded.at(32))
                batches(pe, body)
                spread_sums(B - 1, 1)
                output(B - 1, 1)

            @block.scalar
            def _(act):
                def body(i, first):
                    for j in range(2):
                        n = i * 2 + j
                        for h in range(H):
                            act.wait_ge(transposed.sem, transposed.at(n * H + h + 1))
                            act.wait_ge(valued.sem, valued.at(n * H + h - 3))
                            nc.scalar.copy(pT[:, h % 4, :], ps[:, T_BANK + h % 4, 0:NT * P]).then_inc(turned.sem, 1)

                act.sem_inc(turned.sem, turned.credit)
                with act.Fori(0, B // 2) as i:
                    body(i, False)

            @block.vector
            def _(dve):
                def widen_sums(n, j):
                    dve.wait_ge(normed.sem, normed.at(n - 1))
                    nc.vector.reciprocal(rsum[:, j], rel["sums"][:, n, :]).then_inc(recip.sem, 1)
                    dve.wait_ge(recip.sem, recip.at(n + 1))
                    nc.vector.tensor_copy(rsum_wide[:, j].rearrange("p t (h d) -> p (t h) d", d=HD),
                                          rsum[:, j].rearrange("p (a o) -> p a o", o=1).to_broadcast([P, TB * H, HD])
                                          ).then_inc(widened.sem, 1)

                def normalise(n, j):
                    dve.wait_ge(valued.sem, valued.at((n + 1) * H))
                    nc.vector.tensor_tensor(y_sum[:, j], rel["y"][:, :, n, :],
                                            ps[:, Y_BANK + j, :].rearrange("p (c s) -> p c s", c=KT),
                                            ALU.add).then_inc(summed.sem, 1)
                    dve.wait_ge(summed.sem, summed.at(n + 1))
                    dve.wait_ge(spread.sem, spread.at(n + 1))
                    nc.vector.tensor_tensor(yT[:, j], y_sum[:, j],
                                            ps[:, O_BANK + j, :].rearrange("p (c s) -> p c s", c=KT),
                                            ALU.mult).then_inc(normed.sem, 1)

                def add_output(n, j):
                    dve.wait_ge(out_done.sem, out_done.at(n + 1))
                    nc.vector.tensor_tensor(x[:, :, n, :], ps[:, O_BANK + j, :].rearrange("p (m s) -> p m s", m=KT),
                                            x[:, :, n, :], ALU.add).then_inc(added.sem, 1)

                dve.sem_inc(normed.sem, normed.credit)
                dve.sem_inc(added.sem, added.credit)
                with dve.Fori(0, B // 2) as i:
                    for j in range(2):
                        widen_sums(i * 2 + j, j)
                        normalise(i * 2 + j, j)
                        add_output(i * 2 + j, j)


def gate(core, name, src, rows, weight, bias, mode, gT, gate_dram, weights, select_bias=None):
    nc = core.nc
    ps = core.psum
    NT = T // P
    kt = src.shape[1]
    eps = 1e-8 if mode == "top2_eps" else None
    with Stage(core, name) as st:
        wg = st.buf("wg", [P, kt, E])
        bg = st.buf("bg", [P, E])
        sb = st.buf("select_bias", [P, E])
        p = st.buf("p", [P, NT, E])
        key = st.buf("key", [P, NT, E])
        stat = st.buf("stat", [P, NT])
        pair = st.buf("pair", [P, NT, E, E])
        tie = st.buf("tie", [P, NT, E, E])
        rank = st.buf("rank", [P, NT, E])
        loaded, logits_done = st.count("loaded"), st.count("logits_done")
        shifted, exped = st.count("shifted"), st.count("exped")
        weighted, turned, moved, stored = st.count("weighted"), st.count("turned"), st.count("moved"), st.count("stored")
        chain, pool_chain = st.chain("chain"), st.chain("pool_chain")
        n_loads = 1 + (bias is not None) + (select_bias is not None)

        def over_experts(t):
            return t.rearrange("p (n o) -> p n o", o=1).to_broadcast([P, NT, E])

        def over_tiles(t):
            return t.rearrange("p (o e) -> p o e", o=1).to_broadcast([P, NT, E])

        with nc.Block() as block:

            @block.sync
            def _(sp):
                sp.dma_start(wg[0:rows], weight.rearrange("(k p) e -> p k e", p=rows)).then_inc(loaded.sem, 16)
                for dst, vec in ((bg, bias), (sb, select_bias)):
                    if vec is not None:
                        sp.dma_start(dst[:], vec.rearrange("(o e) -> o e", o=1).to_broadcast([P, E])).then_inc(loaded.sem, 16)
                sp.wait_ge(moved.sem, moved.at(4))
                sp.dma_start(gate_dram, gT[0:E, :]).then_inc(stored.sem, 16)
                sp.wait_ge(stored.sem, stored.at(16))
                sp.wait_ge(loaded.sem, loaded.at(16 * n_loads))

            @block.gpsimd
            def _(pool):
                pool_chain.link(pool, nc.gpsimd.tensor_copy(weights.hi[:, 0, :], weights.raw[:]))
                nc.gpsimd.tensor_tensor(weights.lo[:, 0, :], weights.raw[:], weights.hi[:, 0, :].bitcast(F32), ALU.subtract)

            @block.tensor
            def _(pe):
                pe.wait_ge(loaded.sem, loaded.at(16 * n_loads))
                for t in range(NT):
                    for k in range(kt):
                        mm = nc.tensor.matmul(ps[:, 0, t * E:(t + 1) * E], src[0:rows, k, t * P:(t + 1) * P],
                                              wg[0:rows, k, :], start=(k == 0), stop=(k == kt - 1))
                mm.then_inc(logits_done.sem, 1)
                pe.wait_ge(weighted.sem, weighted.at(1))
                for t in range(NT):
                    c, o = t * P // CH, t * P % CH
                    mm = nc.tensor.transpose(ps[0:E, 1 + c, o:o + P], p[:, t, :], core.ident[:])
                    if o + P == CH:
                        mm.then_inc(turned.sem, 1)

            @block.scalar
            def _(act):
                act.wait_ge(shifted.sem, shifted.at(1))
                nc.scalar.activation(p[:], p[:], ACT.Exp).then_inc(exped.sem, 1)
                for c in range(T // CH):
                    act.wait_ge(turned.sem, turned.at(c + 1))
                    nc.scalar.copy(gT[0:E, c * CH:(c + 1) * CH], ps[0:E, 1 + c, :]).then_inc(moved.sem, 1)

            @block.vector
            def _(dve):
                def do(ins):
                    chain.link(dve, ins)

                def tt(out, a, b, op):
                    do(nc.vector.tensor_tensor(out, a, b, op))

                dve.wait_ge(loaded.sem, loaded.at(16 * n_loads))
                dve.wait_ge(logits_done.sem, logits_done.at(1))
                logits = ps[:, 0, 0:NT * E].rearrange("p (n e) -> p n e", e=E)
                if bias is not None:
                    tt(p[:], logits, over_tiles(bg[:]), ALU.add)
                else:
                    do(nc.vector.tensor_copy(p[:], logits))
                do(nc.vector.tensor_reduce(stat[:], p[:], AX.X, ALU.max))
                nc.vector.tensor_tensor(p[:], p[:], over_experts(stat[:]), ALU.subtract).then_inc(shifted.sem, 1)
                dve.wait_ge(exped.sem, exped.at(1))
                do(nc.vector.tensor_reduce(stat[:], p[:], AX.X, ALU.add))
                do(nc.vector.reciprocal(stat[:], stat[:]))
                tt(p[:], p[:], over_experts(stat[:]), ALU.mult)
                if mode == "threshold":
                    do(nc.vector.tensor_scalar(rank[:], p[:], 0.1, None, ALU.is_ge))
                    tt(p[:], p[:], rank[:], ALU.mult)
                    do(nc.vector.tensor_reduce(stat[:], p[:], AX.X, ALU.add))
                    do(nc.vector.tensor_scalar(rank[:, :, 0], stat[:], 0.0, None, ALU.is_equal))
                    tt(stat[:], stat[:], rank[:, :, 0], ALU.add)
                    do(nc.vector.reciprocal(stat[:], stat[:]))
                else:
                    if select_bias is not None:
                        tt(key[:], p[:], over_tiles(sb[:]), ALU.add)
                    else:
                        do(nc.vector.tensor_copy(key[:], p[:]))
                    mine = key[:].rearrange("p n (e o) -> p n e o", o=1).to_broadcast([P, NT, E, E])
                    other = key[:].rearrange("p n (o f) -> p n o f", o=1).to_broadcast([P, NT, E, E])
                    nc.vector.tensor_tensor(pair[:], other, mine, ALU.is_gt)
                    do(nc.vector.tensor_tensor(tie[:], other, mine, ALU.is_equal))
                    tri = core.tri[:].rearrange("p (o e) f -> p o (e f)", o=1).to_broadcast([P, NT, E * E])
                    tt(tie[:].rearrange("p n e f -> p n (e f)"), tie[:].rearrange("p n e f -> p n (e f)"), tri, ALU.mult)
                    tt(pair[:], pair[:], tie[:], ALU.add)
                    do(nc.vector.tensor_reduce(rank[:], pair[:], AX.X, ALU.add))
                    do(nc.vector.tensor_scalar(rank[:], rank[:], 2.0, None, ALU.is_lt))
                    if mode == "top2_raw":
                        nc.vector.tensor_tensor(p[:], p[:], rank[:], ALU.mult).then_inc(weighted.sem, 1)
                        return
                    tt(p[:], p[:], rank[:], ALU.mult)
                    do(nc.vector.tensor_reduce(stat[:], p[:], AX.X, ALU.add))
                    if eps:
                        do(nc.vector.tensor_scalar(stat[:], stat[:], eps, None, ALU.add))
                    do(nc.vector.reciprocal(stat[:], stat[:]))
                nc.vector.tensor_tensor(p[:], p[:], over_experts(stat[:]), ALU.mult).then_inc(weighted.sem, 1)


class ExpertWeights:

    def __init__(self, core, name, stack, kind, w, kt, rows, hidden, out_rows, out_tiles):
        self.products = {"linear": 0, "mlp": 1, "swiglu": 2}[kind]
        firsts = ["w1", "w3"][:self.products]
        self.last = sum(kt * w[key].shape[2] for key in firsts)
        last_tiles = w["w2"].shape[1] // P
        width = self.last + last_tiles * out_tiles * out_rows
        self.raw = core.sbuf(name + "_raw", [P, width], stack=stack)
        self.hi = core.sbuf(name + "_w_hi", [P, 2, width], F32R, stack)
        self.lo = core.sbuf(name + "_w_lo", [P, 2, width], F32R, stack)
        self.views = []
        for which, key in enumerate(firsts):
            self.views.append((w[key].rearrange("e (k p) n -> e p k n", p=rows), which * kt * hidden, rows, kt))
        self.views.append((w["w2"].rearrange("e (k p) n -> e p k n", p=P), self.last, P, last_tiles))

    def loads(self, e):
        return [(self.raw[0:r, o:o + view.shape[3] * tiles].rearrange("p (k n) -> p k n", k=tiles), view[e])
                for view, o, r, tiles in self.views]


def experts(core, name, weights, kind, w, gT, gate_dram, src, parts=None, rows=P, hidden=0, out_rows=P, out_tiles=KT,
            act_fn=None, store=None):
    nc = core.nc
    ps = core.psum
    kt = src.shape[1]
    MT = kt if kind == "linear" else hidden // P
    NW1 = {"linear": 0, "mlp": 1, "swiglu": 2}[kind]
    H_BANKS = 4 if NW1 else 0
    PARTS = max(1, NCH * out_tiles // (8 - H_BANKS))
    SPAN = T // PARTS
    NC = SPAN // CH
    U = NC * MT
    W1 = kt * hidden
    O2 = weights.last
    raw, w_hi, w_lo = weights.raw, weights.hi, weights.lo
    LAG = 3 if NW1 else 1
    R = 4
    H_RING = 4 // max(NW1, 1)
    with Stage(core, name) as st:
        gates = st.buf("gates", [P, 2, SPAN])
        zeros = st.buf("zeros", [P, CH], F32R)
        act_out = st.buf("act_out", [P, 2, CH])
        gated = st.buf("gated", [P, 2, CH])
        h_hi = st.buf("h_hi", [P, R, CH], F32R)
        h_lo = st.buf("h_lo", [P, R, CH], F32R)
        b1 = st.buf("b1", [P, E, max(MT, 1)])
        b2 = st.buf("b2", [E, out_tiles * out_rows])
        if kind == "swiglu":
            xs = st.buf("scaled_in", [P, kt, CH])
            xs_hi = st.buf("scaled_in_hi", [P, NC, kt, CH], F32R)
            xs_lo = st.buf("scaled_in_lo", [P, NC, kt, CH], F32R)
        loaded, zeroed = st.count("loaded"), st.count("zeroed")
        raw_in, w_split = st.count("raw_in"), st.count("w_split", 0)
        gates_in = [st.count(f"gates_in{j}") for j in range(2)]
        hidden_done, act_done = st.count("hidden_done", 2 * U), st.count("act_done", H_RING)
        gate_done, high_done, low_done = st.count("gate_done", U), st.count("high_done"), st.count("low_done", 2)
        product_done = st.count("product_done", max(R, U))
        in_split = st.count("in_split", NC)
        closed, emptied = st.count("closed"), st.count("emptied", 0)
        pool_chain = st.chain("pool_chain")
        step_on = st.count("step_on").sem
        has_b1, has_b2 = "b1" in w, "b2" in w
        n_loads = has_b1 + has_b2
        RAWS = 16 * len(weights.views)

        shared = kind == "swiglu" and w["w3"].shape[2] < hidden

        def is_shared(u):
            return shared and u % MT == MT - 1

        def channels(u):
            return slice(P // 2, P) if is_shared(u) else slice(0, P)

        def w1_cols(which, k, m):
            o = which * W1 + k * w[("w1", "w3")[which]].shape[2] + m * P
            return slice(o, o + P)

        def w2_cols(m, mo):
            o = O2 + (m * out_tiles + mo) * out_rows
            return slice(o, o + out_rows)

        def tokens(part, c):
            return bass.ds(part * SPAN + c * CH, CH)

        def turns(engine, body):
            body(0, 0, True)
            with engine.Fori(1, E // 2) as pair:
                body(0, pair, False)
            if PARTS == 2:
                with engine.Fori(0, E // 2) as pair:
                    body(1, pair, False)

        with nc.Block() as block:

            @block.sync
            def _(sp):
                def body(part, pair, first):
                    for j in range(2):
                        n = (part * (E // 2) + pair) * 2 + j
                        if not (first and j == 0):
                            sp.wait_ge(w_split.sem, w_split.at(n))
                            for to, of in weights.loads(pair * 2 + j):
                                sp.dma_start(to, of).then_inc(raw_in.sem, 16)
                        if kind == "swiglu":
                            sp.wait_ge(in_split.sem, in_split.at((n - 1) * NC))
                        else:
                            sp.wait_ge(gate_done.sem, gate_done.at((n - 1) * U))
                        sp.dma_start(gates[:, j, :], gate_dram[bass.ds(pair * 2 + j, 1), part * SPAN:(part + 1) * SPAN]
                                     .to_broadcast([P, SPAN])).then_inc(gates_in[j].sem, 16)

                if has_b1:
                    sp.dma_start(b1[:], w["b1"]).then_inc(loaded.sem, 16)
                if has_b2:
                    sp.dma_start(b2[:], w["b2"]).then_inc(loaded.sem, 16)
                turns(sp, body)
                if n_loads:
                    sp.wait_ge(loaded.sem, loaded.at(16 * n_loads))

            @block.gpsimd
            def _(pool):
                def split_weights(n, j):
                    pool.wait_ge(raw_in.sem, raw_in.at(RAWS * n))
                    pool.wait_ge(product_done.sem, product_done.at((n - 1) * U))
                    pool.sem_inc(step_on, 1)
                    pool_chain.link(pool, nc.gpsimd.tensor_copy(w_hi[:, j, :], raw[:]))
                    nc.gpsimd.tensor_tensor(w_lo[:, j, :], raw[:], w_hi[:, j, :].bitcast(F32),
                                            ALU.subtract).then_inc(w_split.sem, 1)

                def scale_input(part, turn, n, j):
                    pool.wait_ge(gates_in[j].sem, gates_in[j].at(16 * (turn + 1)))
                    for c in range(NC):
                        pool.wait_ge(hidden_done.sem, hidden_done.at((n - 1) * U + (c + 1) * MT))
                        pool.wait_ge(in_split.sem, in_split.at(n * NC + c))
                        pool.sem_inc(step_on, 1)
                        g = gates[:, j:j + 1, c * CH:(c + 1) * CH].to_broadcast([P, kt, CH])
                        tokens = slice(part * SPAN + c * CH, part * SPAN + (c + 1) * CH)
                        pool_chain.link(pool, nc.gpsimd.tensor_tensor(xs[:], src[:, :, tokens], g, ALU.mult))
                        pool_chain.link(pool, nc.gpsimd.tensor_copy(xs_hi[:, c], xs[:]))
                        nc.gpsimd.tensor_tensor(xs_lo[:, c], xs[:], xs_hi[:, c].bitcast(F32),
                                                ALU.subtract).then_inc(in_split.sem, 1)

                def body(part, pair, first):
                    pool_chain.restart(pool)
                    for j in range(2):
                        turn = part * (E // 2) + pair
                        n = turn * 2 + j
                        if not (first and j == 0):
                            split_weights(n, j)
                        if kind == "swiglu":
                            scale_input(part, turn, n, j)

                pool.sem_inc(in_split.sem, in_split.credit)
                pool.sem_inc(w_split.sem, w_split.credit + 1)
                nc.gpsimd.memset(zeros[:].bitcast(F32), 0.0).then_inc(zeroed.sem, 1)
                turns(pool, body)

            @block.tensor
            def _(pe):
                pe.sem_inc(hidden_done.sem, hidden_done.credit)
                pe.sem_inc(product_done.sem, product_done.credit)
                if n_loads:
                    pe.wait_ge(loaded.sem, loaded.at(16 * n_loads))
                pe.wait_ge(zeroed.sem, zeroed.at(1))

                def three(out, hi_w, lo_w, hi_x, lo_x, start, stop):
                    nc.tensor.matmul(out, hi_w, hi_x, start=start, stop=False, skip_group_check=True)
                    nc.tensor.matmul(out, hi_w, lo_x, start=False, stop=False, skip_group_check=True)
                    return nc.tensor.matmul(out, lo_w, hi_x, start=False, stop=stop, skip_group_check=True)

                def first_product(part, n, j, u):
                    c, m = divmod(u, MT)
                    if kind == "swiglu":
                        if m == 0:
                            pe.wait_ge(in_split.sem, in_split.at(n * NC + c + 1))
                        pe.wait_ge(gate_done.sem, gate_done.at(n * U + u + 1 - H_RING))
                        hi, lo = xs_hi[:, c], xs_lo[:, c]
                    else:
                        pe.wait_ge(act_done.sem, act_done.at(n * U + u + 1 - H_RING))
                        hi, lo = parts[0][0:rows, :, tokens(part, c)], parts[1][0:rows, :, tokens(part, c)]
                    for which in range(1 if is_shared(u) else NW1):
                        bank = 4 + (u % H_RING) * NW1 + which
                        for k in range(kt):
                            cols = w1_cols(which, k, m)
                            mm = three(ps[:, bank, :], w_hi[0:rows, j, cols], w_lo[0:rows, j, cols], hi[:, k], lo[:, k],
                                       k == 0, k == kt - 1)
                    mm.then_inc(hidden_done.sem, 1)

                def last_product(n, j, u):
                    c, m = divmod(u, MT)
                    pe.wait_ge(low_done.sem, low_done.at(n * U + u + 1))
                    for mo in range(out_tiles):
                        r = channels(u)
                        mm = three(ps[0:out_rows, c * out_tiles + mo, :], w_hi[r, j, w2_cols(m, mo)],
                                   w_lo[r, j, w2_cols(m, mo)], h_hi[r, u % R, :], h_lo[r, u % R, :], False, False)
                    mm.then_inc(product_done.sem, 1)

                def products(part, pair, first):
                    for j in range(2):
                        n = (part * (E // 2) + pair) * 2 + j
                        pe.wait_ge(w_split.sem, w_split.at(n + 1))
                        for step in range(U):
                            if NW1:
                                first_product(part, n, j, step)
                            if step >= LAG:
                                last_product(n, j, step - LAG)
                            elif not (first and j == 0):
                                last_product(n - 1, 1 - j, U + step - LAG)

                with pe.Fori(0, PARTS) as part:
                    pe.wait_ge(emptied.sem, emptied.at(part))
                    for c in range(NC):
                        for mo in range(out_tiles):
                            nc.tensor.matmul(ps[0:out_rows, c * out_tiles + mo, :], zeros[:, 0:out_rows], zeros[:],
                                             start=True, stop=False, skip_group_check=True)
                    products(part, 0, True)
                    with pe.Fori(1, E // 2) as pair:
                        products(part, pair, False)
                    for step in range(U - LAG, U):
                        last_product(part * E + E - 1, 1, step)
                    for c in range(NC):
                        for mo in range(out_tiles):
                            out = ps[0:out_rows, c * out_tiles + mo, :]
                            if has_b2:
                                mm = nc.tensor.matmul(out, b2[:, mo * out_rows:(mo + 1) * out_rows], gT[0:E, tokens(part, c)],
                                                      start=False, stop=True, skip_group_check=True)
                            else:
                                mm = nc.tensor.matmul(out, zeros[:, 0:out_rows], zeros[:], start=False, stop=True,
                                                      skip_group_check=True)
                    mm.then_inc(closed.sem, 1)

            @block.scalar
            def _(act):
                act.sem_inc(act_done.sem, act_done.credit)
                if n_loads:
                    act.wait_ge(loaded.sem, loaded.at(16 * n_loads))
                with act.Fori(0, PARTS) as part:
                    with act.Fori(0, E // 2) as pair:
                        for j in range(2):
                            n = (part * (E // 2) + pair) * 2 + j
                            for step in range(U + 1):
                                if NW1 and step < U:
                                    u = step
                                    act.wait_ge(hidden_done.sem, hidden_done.at(n * U + u + 1))
                                    act.wait_ge(gate_done.sem, gate_done.at(n * U + u - 1))
                                    r = slice(0, P // 2) if is_shared(u) else slice(0, P)
                                    hidden_ps = ps[r, 4 + (u % H_RING) * NW1, :]
                                    if has_b1:
                                        act.sem_inc(step_on, 1)
                                        ins = nc.scalar.activation(act_out[:, u % 2, :], hidden_ps, act_fn,
                                                                   bias=b1[:, pair * 2 + j, u % MT:u % MT + 1])
                                    else:
                                        ins = nc.scalar.activation(act_out[channels(u), u % 2, :], hidden_ps, act_fn)
                                    ins.then_inc(act_done.sem, 1)
                                if step >= 1:
                                    u = step - 1
                                    act.wait_ge(gate_done.sem, gate_done.at(n * U + u + 1))
                                    act.wait_ge(product_done.sem, product_done.at(n * U + u + 1 - R))
                                    r = channels(u)
                                    nc.scalar.copy(h_hi[r, u % R, :], gated[r, u % 2, :]).then_inc(high_done.sem, 1)

            @block.vector
            def _(dve):
                dve.sem_inc(gate_done.sem, gate_done.credit)
                dve.sem_inc(low_done.sem, low_done.credit)
                dve.sem_inc(emptied.sem, emptied.credit)
                with dve.Fori(0, PARTS) as part:
                    with dve.Fori(0, E // 2) as pair:
                        for j in range(2):
                            turn = part * (E // 2) + pair
                            n = turn * 2 + j
                            dve.wait_ge(gates_in[j].sem, gates_in[j].at(16 * (turn + 1)))
                            for step in range(U + 1):
                                if step < U:
                                    u = step
                                    c, m = divmod(u, MT)
                                    dve.wait_ge(low_done.sem, low_done.at(n * U + u - 1))
                                    g = gates[:, j, c * CH:(c + 1) * CH]
                                    if kind == "linear":
                                        a, b = src[:, m, tokens(part, c)], g
                                    else:
                                        dve.wait_ge(act_done.sem, act_done.at(n * U + u + 1))
                                        r = channels(u)
                                        a, b = act_out[r, u % 2, :], g
                                        if kind == "swiglu":
                                            b = ps[r, (4 if is_shared(u) else 5) + (u % H_RING) * NW1, :]
                                    nc.vector.tensor_tensor(gated[channels(u), u % 2, :], a, b, ALU.mult).then_inc(gate_done.sem, 1)
                                if step >= 1:
                                    u = step - 1
                                    dve.wait_ge(high_done.sem, high_done.at(n * U + u + 1))
                                    r = channels(u)
                                    nc.vector.tensor_tensor(h_lo[r, u % R, :], gated[r, u % 2, :],
                                                            h_hi[r, u % R, :].bitcast(F32), ALU.subtract).then_inc(low_done.sem, 1)
                    dve.wait_ge(closed.sem, closed.at(part + 1))
                    for c in range(NC):
                        sums = ps[0:out_rows, c * out_tiles:(c + 1) * out_tiles, :]
                        if store is None:
                            dst = core.x[:, :, tokens(part, c)]
                            ins = nc.vector.tensor_tensor(dst, dst, sums, ALU.add)
                        else:
                            ins = nc.vector.tensor_copy(store[0:out_rows, :, tokens(part, c)], sums)
                    ins.then_inc(emptied.sem, 1)


def two_layers(core, name, w, src, rows, dst, out_rows, out_tiles, last_fn, parts=None, third=None):
    nc = core.nc
    ps = core.psum
    kt = src.shape[1]
    M1 = w["w1"].shape[1] // P
    with Stage(core, name) as st:
        w1 = st.buf("w1", [P, kt, M1 * P])
        w2 = st.buf("w2", [P, M1, out_tiles * out_rows])
        b1 = st.buf("b1", [P, M1])
        b2 = st.buf("b2", [P, out_tiles])
        w3 = st.buf("w3", [P, P])
        b3 = st.buf("b3", [P, 1])
        hid = st.buf("hidden", [P, 2, M1, CH])
        loaded, hidden_done, squashed = st.count("loaded"), st.count("hidden_done"), st.count("squashed", M1)
        out_done, moved = st.count("out_done", 2), st.count("moved", 2)
        third_done, third_moved = st.count("third_done"), st.count("third_moved", 2)
        split_high = st.count("split_high")
        loads = [(w1[0:rows], w["w1"].rearrange("(k p) n -> p k n", p=rows)), (w2[:], w["w2"].rearrange("(k p) n -> p k n", p=P)),
                 (b1[:], w["b1"]), (b2[0:out_rows], w["b2"])]
        if third:
            loads += [(w3[0:out_rows, 0:out_rows], third[0]), (b3[0:out_rows], third[1])]

        def tokens(q, j):
            return bass.ds((q * 2 + j) * CH, CH)

        with nc.Block() as block:

            @block.sync
            def _(sp):
                for to, of in loads:
                    sp.dma_start(to, of).then_inc(loaded.sem, 16)
                sp.wait_ge(loaded.sem, loaded.at(16 * len(loads)))

            @block.tensor
            def _(pe):
                pe.sem_inc(out_done.sem, out_done.credit)
                pe.wait_ge(loaded.sem, loaded.at(16 * len(loads)))
                with pe.Fori(0, NCH // 2) as q:
                    for j in range(2):
                        n = q * 2 + j
                        pe.wait_ge(out_done.sem, out_done.at(n - 1))
                        for m in range(M1):
                            pe.wait_ge(squashed.sem, squashed.at(n * M1 + m + 1 - M1))
                            for k in range(kt):
                                mm = nc.tensor.matmul(ps[:, m, :], w1[0:rows, k, m * P:(m + 1) * P],
                                                      src[0:rows, k, tokens(q, j)], start=(k == 0), stop=(k == kt - 1))
                            mm.then_inc(hidden_done.sem, 1)
                    for j in range(2):
                        n = q * 2 + j
                        pe.wait_ge(squashed.sem, squashed.at((n + 1) * M1))
                        before = third_moved if third else moved
                        pe.wait_ge(before.sem, before.at(n - 1))
                        for mo in range(out_tiles):
                            for m in range(M1):
                                mm = nc.tensor.matmul(ps[0:out_rows, 4 + j * 2 + mo, :],
                                                      w2[:, m, mo * out_rows:(mo + 1) * out_rows], hid[:, j, m, :],
                                                      start=(m == 0), stop=(m == M1 - 1))
                        mm.then_inc(out_done.sem, 1)
                        if third:
                            pe.wait_ge(moved.sem, moved.at(n + 1))
                            nc.tensor.matmul(ps[0:out_rows, 5 + j * 2, :], w3[0:out_rows, 0:out_rows],
                                             dst[0:out_rows, 0, tokens(q, j)], start=True, stop=True).then_inc(third_done.sem, 1)

            @block.scalar
            def _(act):
                act.sem_inc(squashed.sem, squashed.credit)
                act.sem_inc(moved.sem, moved.credit)
                act.sem_inc(third_moved.sem, third_moved.credit)
                act.wait_ge(loaded.sem, loaded.at(16 * len(loads)))
                with act.Fori(0, NCH // 2) as q:
                    for j in range(2):
                        n = q * 2 + j
                        act.wait_ge(out_done.sem, out_done.at(n - 1))
                        for m in range(M1):
                            act.wait_ge(hidden_done.sem, hidden_done.at(n * M1 + m + 1))
                            nc.scalar.activation(hid[:, j, m, :], ps[:, m, :], ACT.Sigmoid,
                                                 bias=b1[:, m:m + 1]).then_inc(squashed.sem, 1)
                    for j in range(2):
                        n = q * 2 + j
                        act.wait_ge(out_done.sem, out_done.at(n + 1))
                        for mo in range(out_tiles):
                            ins = nc.scalar.activation(dst[0:out_rows, mo, tokens(q, j)], ps[0:out_rows, 4 + j * 2 + mo, :],
                                                       last_fn, bias=b2[0:out_rows, mo:mo + 1])
                        ins.then_inc(moved.sem, 1)
                        if third:
                            act.wait_ge(third_done.sem, third_done.at(n + 1))
                            nc.scalar.activation(third[2][0:out_rows, 0, tokens(q, j)], ps[0:out_rows, 5 + j * 2, :],
                                                 ACT.Relu, bias=b3[0:out_rows, 0:1]).then_inc(third_moved.sem, 1)
                        if parts:
                            nc.scalar.copy(parts[0][0:out_rows, :, tokens(q, j)],
                                           dst[0:out_rows, :, tokens(q, j)]).then_inc(split_high.sem, 1)

            @block.vector
            def _(dve):
                if parts:
                    with dve.Fori(0, NCH // 2) as q:
                        for j in range(2):
                            dve.wait_ge(split_high.sem, split_high.at(q * 2 + j + 1))
                            nc.vector.tensor_tensor(parts[1][0:out_rows, :, tokens(q, j)], dst[0:out_rows, :, tokens(q, j)],
                                                    parts[0][0:out_rows, :, tokens(q, j)].bitcast(F32), ALU.subtract)


def mixture_buffers(core, name, stack, kind, w, kt=KT, rows=P, hidden=0, out_rows=P, out_tiles=KT):
    gT = core.sbuf(name + "_gateT", [E, T], stack=stack)
    weights = ExpertWeights(core, name, stack, kind, w, kt, rows, hidden, out_rows, out_tiles)
    return gT, core.nc.dram_tensor(name + "_gate_dram", (E, T), F32).ap(), weights


def stage_L0_ffn(core, name, w, a):
    with ExitStack() as stack:
        gT, gate_dram, weights = mixture_buffers(core, name, stack, "linear", w)
        layernorm(core, name + "_ln", core.x, core.xn, preload=weights.loads(0))
        gate(core, name + "_gate", core.xn, P, w["gate_w"], w["gate_b"], "threshold", gT, gate_dram, weights)
        experts(core, name, weights, "linear", w, gT, gate_dram, core.xn)


def stage_L1_ffn(core, name, w, a):
    F, hidden = w["pre_w2"].shape[1], w["w1"].shape[2]
    with ExitStack() as stack:
        gT, gate_dram, weights = mixture_buffers(core, name, stack, "mlp", w, 1, F, hidden, F, 1)
        cont = core.sbuf(name + "_cont", [P, 1, T], stack=stack)
        router = core.sbuf(name + "_router", [P, 1, T], stack=stack)
        parts = [core.sbuf(name + f"_cont_{p}", [P, 1, T], F32R, stack) for p in ("high", "low")]
        layernorm(core, name + "_ln", core.x, core.xn, preload=weights.loads(0))
        two_layers(core, name + "_pre", {k[4:]: v for k, v in w.items() if k.startswith("pre_")}, core.xn, P, cont, F, 1,
                   ACT.Identity, parts, (w["r_w1"], w["r_b1"], router))
        gate(core, name + "_gate", router, F, w["r_w2"], w["r_b2"], "top2", gT, gate_dram, weights)
        experts(core, name, weights, "mlp", w, gT, gate_dram, cont, parts, rows=F, hidden=hidden, out_rows=F, out_tiles=1,
                act_fn=ACT.Relu, store=cont)
        two_layers(core, name + "_post", {k[5:]: v for k, v in w.items() if k.startswith("post_")}, cont, F, core.xn, P, KT,
                   ACT.Sigmoid)
        layernorm(core, name + "_out", core.xn, core.x, affine=(w["ln_g"], w["ln_b"]))


def stage_L2_ffn(core, name, w, a):
    hidden = w["w1"].shape[2]
    with ExitStack() as stack:
        gT, gate_dram, weights = mixture_buffers(core, name, stack, "swiglu", w, hidden=hidden)
        layernorm(core, name + "_ln", core.x, core.xn, preload=weights.loads(0))
        gate(core, name + "_gate", core.xn, P, w["gate_w"], None, "top2_raw", gT, gate_dram, weights, w["expert_bias"])
        experts(core, name, weights, "swiglu", w, gT, gate_dram, core.xn, hidden=hidden, act_fn=ACT.Silu)


def stage_L3_ffn(core, name, w, a):
    hidden = w["w1"].shape[2]
    with ExitStack() as stack:
        gT, gate_dram, weights = mixture_buffers(core, name, stack, "mlp", w, hidden=hidden)
        parts = [core.sbuf(name + f"_x_{p}", [P, KT, T], F32R, stack) for p in ("high", "low")]
        layernorm(core, name + "_ln", core.x, core.xn, parts=parts, preload=weights.loads(0))
        gate(core, name + "_gate", core.xn, P, w["Wg"], w["bg"], "top2_eps", gT, gate_dram, weights)
        experts(core, name, weights, "mlp", w, gT, gate_dram, core.xn, parts, hidden=hidden, act_fn=ACT.Gelu, store=core.xn)
    layernorm(core, name + "_out", core.xn, core.x, affine=(w["gamma"], w["beta"]))


def lay_out_mixtures(a, n):
    def hidden_bias(b):
        return b.reshape(E, -1, P).transpose(2, 0, 1)

    for k in ("gate_w", "gate_b"):
        a[f"L0_ffn_{k}"] = n[f"L0_ffn_{k}"]
    a["L0_ffn_w2"], a["L0_ffn_b2"] = n["L0_ffn_expert_w"], n["L0_ffn_expert_b"]

    p = "L1_ffn_"
    a[p + "pre_w1"], a[p + "pre_b1"] = n[p + "enc_w"], by_partition(n[p + "enc_b"])
    def filled(t, *axes):
        return np.pad(t, [(0, P - t.shape[i]) if i in axes else (0, 0) for i in range(t.ndim)])

    a[p + "pre_w2"], a[p + "pre_b2"] = filled(n[p + "s2c_w"], 1), filled(n[p + "s2c_b"], 0).reshape(-1, 1)
    a[p + "r_w1"], a[p + "r_b1"] = filled(n[p + "r_w1"], 0, 1), filled(n[p + "r_b1"], 0).reshape(-1, 1)
    a[p + "r_w2"], a[p + "r_b2"] = filled(n[p + "r_w2"], 0), n[p + "r_b2"]
    a[p + "w1"], a[p + "b1"] = filled(n[p + "e_w1"], 1), hidden_bias(n[p + "e_b1"])
    a[p + "w2"], a[p + "b2"] = filled(n[p + "e_w2"], 2), filled(n[p + "e_b2"], 1)
    a[p + "post_w1"], a[p + "post_b1"] = filled(n[p + "c2s_w"], 0), by_partition(n[p + "c2s_b"])
    a[p + "post_w2"], a[p + "post_b2"] = n[p + "dec_w"], by_partition(n[p + "dec_b"])
    a[p + "ln_g"], a[p + "ln_b"] = by_partition(n[p + "ln_g"]), by_partition(n[p + "ln_b"])

    p = "L2_ffn_"
    a[p + "gate_w"], a[p + "expert_bias"] = n[p + "gate_w"].T, n[p + "expert_bias"]
    w1, w2, w3 = n[p + "w1"], n[p + "w2"], n[p + "w3"]
    whole = w1.shape[2] // P * P
    if w1.shape[2] - whole == P // 2:
        a[p + "w1"], a[p + "w3"] = np.concatenate([w1, w3[:, :, whole:]], 2), w3[:, :, :whole]
        a[p + "w2"] = np.concatenate([w2[:, :whole], np.zeros_like(w2[:, :P // 2]), w2[:, whole:]], 1)
    else:
        short = -w1.shape[2] % P
        a[p + "w1"], a[p + "w3"] = (np.pad(v, ((0, 0), (0, 0), (0, short))) for v in (w1, w3))
        a[p + "w2"] = np.pad(w2, ((0, 0), (0, short), (0, 0)))

    p = "L3_ffn_"
    a[p + "Wg"], a[p + "bg"] = n[p + "Wg"], n[p + "bg"]
    a[p + "w1"], a[p + "b1"] = n[p + "W1"], hidden_bias(n[p + "b1"])
    a[p + "w2"], a[p + "b2"] = n[p + "W2"], n[p + "b2"]
    a[p + "gamma"], a[p + "beta"] = by_partition(n[p + "gamma"]), by_partition(n[p + "beta"])


def linear_attention(core, name, w):
    nc = core.nc
    ps = core.psum
    NG = H // 4
    F = 2 * HD
    VC = HD + 1
    BR = 2
    with Stage(core, name) as st:
        wt = {c: st.buf("w" + c, [P, KT, D]) for c in "qkvo"}
        bt = {c: st.buf("b" + c, [P, D]) for c in "qkv"}
        bo = st.buf("bo", [P, KT])
        angle = st.buf("sin_cos", [P, TB, 2])
        xb = st.buf("tokens", [P, 2, KT, S])
        qk = st.buf("qk", [P, 2, TB, 2 * D])
        mx = st.buf("max", [P, TB, 2 * H])
        total = st.buf("total", [P, TB, 2 * H])
        feat = st.buf("features", [P, TB, 2, BR, H, F])
        v = st.buf("v", [P, 2, TB, H, VC])
        kv = st.buf("kv", [P, BR * NG, 4, VC])
        qfT = st.buf("q_featuresT", [P, BR * NG, S])
        z = st.buf("z", [P, BR, TB, H])
        part = st.buf("branch", [P, BR, TB, D])
        y = st.buf("y", [P, TB, D])
        yT = st.buf("yT", [P, KT, S])
        copied, projected = st.count("copied"), st.count("projected", 1)
        biased, step_on = st.count("biased", 0), st.count("step_on").sem
        shifted, exped, softmaxed = (st.count(k) for k in ("shifted", "exped", "softmaxed"))
        featured, q_featured = st.count("k_featured"), st.count("q_featured")
        kv_done, kv_moved, qf_turned, qf_moved = (st.count(k) for k in ("kv_done", "kv_moved", "qf_turned", "qf_moved"))
        attended, summed, y_turned, y_moved = (st.count(k) for k in ("attended", "summed", "y_turned", "y_moved"))
        out_done, added = st.count("out_done"), st.count("added", 1)
        chain = st.chain("chain")
        xn = core.xn[:].rearrange("p k (b s) -> p k b s", b=B)
        x = core.x[:].rearrange("p k (s b) -> p k b s", b=B)
        loads = [(wt[c][:], w["W" + c].rearrange("(k p) n -> p k n", p=P)) for c in "qkvo"]
        loads += [(bt[c][:], w["b" + c].rearrange("(o n) -> o n", o=1).to_broadcast([P, D])) for c in "qkv"]
        loads += [(bo[:], w["bo"]), (angle[:], w["sin_cos"])]
        QK_BANK, V_BANK = 0, 2
        KV_BANK, QF_BANK, RES_BANK, Y_BANK, OUT_BANK = 5, (3, 5), ((7, 3), (4, 5)), 6, 7

        layernorm(core, name + "_ln", core.x, core.xn, preload=loads)

        def batches(engine, body):
            body(0, True, False)
            with engine.Fori(1, B // 2 - 1) as i:
                body(i, False, False)
            body(B // 2 - 1, False, True)

        with nc.Block() as block:

            @block.tensor
            def _(pe):
                def projection(n, j):
                    pe.wait_ge(copied.sem, copied.at(n + 1))
                    pe.wait_ge(biased.sem, biased.at(n))
                    for t in range(TB):
                        for o, c in ((0, "q"), (D, "k")):
                            for k in range(KT):
                                nc.tensor.matmul(ps[:, QK_BANK + t, o:o + D], xb[:, j, k, t * P:(t + 1) * P],
                                                 wt[c][:, k, :], start=(k == 0), stop=(k == KT - 1))
                    for t in range(TB):
                        for k in range(KT):
                            mm = nc.tensor.matmul(ps[:, V_BANK, t * D:(t + 1) * D], xb[:, j, k, t * P:(t + 1) * P],
                                                  wt["v"][:, k, :], start=(k == 0), stop=(k == KT - 1))
                    mm.then_inc(projected.sem, 1)

                def back(n, j):
                    pe.wait_ge(featured.sem, featured.at(n + 1))
                    for br in range(BR):
                        for g in range(NG):
                            for t in range(TB):
                                mm = nc.tensor.matmul(ps[:, KV_BANK + br, g * 4 * VC:(g + 1) * 4 * VC],
                                                      feat[:, t, 1, br, g * 4:(g + 1) * 4, :].rearrange("p h f -> p (h f)"),
                                                      v[:, j, t, g * 4:(g + 1) * 4, :].rearrange("p h c -> p (h c)"),
                                                      start=(t == 0), stop=(t == TB - 1))
                    mm.then_inc(kv_done.sem, 1)
                    pe.wait_ge(q_featured.sem, q_featured.at(n + 1))
                    for br in range(BR):
                        if br == 1:
                            pe.wait_ge(kv_moved.sem, kv_moved.at(n + 1))
                        for g in range(NG):
                            for t in range(TB):
                                mm = nc.tensor.transpose(ps[:, QF_BANK[br] + g // 2, (g % 2) * S + t * P:(g % 2) * S + (t + 1) * P],
                                                         feat[:, t, 0, br, g * 4:(g + 1) * 4, :].rearrange("p h f -> p (h f)"),
                                                         core.ident[:])
                        mm.then_inc(qf_turned.sem, 1)
                    pe.wait_ge(added.sem, added.at(n))
                    pe.wait_ge(qf_moved.sem, qf_moved.at(2 * n + 2))
                    for br in range(BR):
                        for t in range(TB):
                            for g in range(NG):
                                mm = nc.tensor.matmul(ps[:, RES_BANK[br][t], g * 4 * VC:(g + 1) * 4 * VC],
                                                      qfT[:, br * NG + g, t * P:(t + 1) * P],
                                                      kv[:, br * NG + g].rearrange("p h c -> p (h c)"), start=True, stop=True)
                    mm.then_inc(attended.sem, 1)

                def output(n):
                    pe.wait_ge(summed.sem, summed.at(n + 1))
                    for c in range(KT):
                        for t in range(TB):
                            mm = nc.tensor.transpose(ps[:, Y_BANK, c * S + t * P:c * S + (t + 1) * P],
                                                     y[:, t, c * P:(c + 1) * P], core.ident[:])
                    mm.then_inc(y_turned.sem, 1)
                    pe.wait_ge(y_moved.sem, y_moved.at(n + 1))
                    for m in range(KT):
                        for k in range(KT):
                            mm = nc.tensor.matmul(ps[:, OUT_BANK, m * S:(m + 1) * S], wt["o"][:, k, m * P:(m + 1) * P],
                                                  yT[:, k, :], start=(k == 0), stop=(k == KT - 1))
                    mm.then_inc(out_done.sem, 1)

                def body(i, first, last):
                    for j in range(2):
                        n = i * 2 + j
                        back(n, j)
                        if not last:
                            projection(n + 2, j)
                        output(n)

                pe.sem_inc(projected.sem, projected.credit)
                projection(0, 0)
                projection(1, 1)
                batches(pe, body)

            @block.scalar
            def _(act):
                def copy_tokens(n, j):
                    act.wait_ge(projected.sem, projected.at(n - 1))
                    act.sem_inc(step_on, 1)
                    nc.scalar.copy(xb[:, j], xn[:, :, n, :]).then_inc(copied.sem, 1)

                def exponentiate(n):
                    act.wait_ge(shifted.sem, shifted.at(n + 1))
                    nc.scalar.activation(qk[:, 0], qk[:, 0], ACT.Exp).then_inc(exped.sem, 1)

                def q_features(n):
                    act.wait_ge(softmaxed.sem, softmaxed.at(n + 1))
                    for t in range(TB):
                        for br in range(BR):
                            src = qk[:, br, t, 0:D].rearrange("p (h d) -> p h d", d=HD)
                            for f in range(2):
                                ins = nc.scalar.mul(feat[:, t, 0, br, :, f * HD:(f + 1) * HD], src, angle[:, t, f:f + 1])
                    ins.then_inc(q_featured.sem, 1)

                def body(i, first, last):
                    for j in range(2):
                        n = i * 2 + j
                        if not last:
                            copy_tokens(n + 2, j)
                        if not (last and j == 1):
                            exponentiate(n + 1)
                        for br in range(BR):
                            act.wait_ge(qf_turned.sem, qf_turned.at(2 * n + br + 1))
                            nc.scalar.copy(qfT[:, br * NG:(br + 1) * NG].rearrange("p (a b) s -> p a (b s)", b=2),
                                           ps[:, QF_BANK[br]:QF_BANK[br] + 2, :]).then_inc(qf_moved.sem, 1)
                        if not (last and j == 1):
                            q_features(n + 1)
                        act.wait_ge(y_turned.sem, y_turned.at(n + 1))
                        nc.scalar.copy(yT[:], ps[:, Y_BANK, :].rearrange("p (c s) -> p c s", c=KT)).then_inc(y_moved.sem, 1)

                copy_tokens(0, 0)
                copy_tokens(1, 1)
                exponentiate(0)
                q_features(0)
                batches(act, body)

            @block.vector
            def _(dve):
                def link(ins):
                    chain.link(dve, ins)

                rows = qk[:, 0].rearrange("p t (h d) -> p (t h) d", d=HD)

                def over_channels(s):
                    return s[:].rearrange("p t (h o) -> p (t h) o", o=1).to_broadcast([P, TB * 2 * H, HD])

                def take_projections(n, j):
                    dve.wait_ge(projected.sem, projected.at(n + 1))
                    for t in range(TB):
                        for o, c in ((0, "q"), (D, "k")):
                            nc.vector.tensor_tensor(qk[:, 0, t, o:o + D], ps[:, QK_BANK + t, o:o + D], bt[c][:], ALU.add)
                        ins = nc.vector.tensor_tensor(v[:, j, t, :, 0:HD],
                                                      ps[:, V_BANK, t * D:(t + 1) * D].rearrange("p (h d) -> p h d", d=HD),
                                                      bt["v"][:].rearrange("p (h d) -> p h d", d=HD), ALU.add)
                    ins.then_inc(biased.sem, 1)
                    dve.wait_ge(biased.sem, biased.at(n + 1))
                    link(nc.vector.tensor_reduce(mx[:].rearrange("p t h -> p (t h)"), rows, AX.X, ALU.max))
                    nc.vector.tensor_tensor(rows, rows, over_channels(mx), ALU.subtract).then_inc(shifted.sem, 1)

                def softmax(n):
                    dve.wait_ge(exped.sem, exped.at(n + 1))
                    link(nc.vector.tensor_reduce(total[:].rearrange("p t h -> p (t h)"), rows, AX.X, ALU.add))
                    link(nc.vector.reciprocal(total[:], total[:]))
                    link(nc.vector.tensor_tensor(rows, rows, over_channels(total), ALU.mult))
                    nc.vector.tensor_scalar(qk[:, 1], qk[:, 0], -1.0, 1.0, ALU.mult, ALU.add).then_inc(softmaxed.sem, 1)
                    dve.wait_ge(softmaxed.sem, softmaxed.at(n + 1))

                def k_features(n):
                    for t in range(TB):
                        for br in range(BR):
                            src = qk[:, br, t, D:2 * D].rearrange("p (h d) -> p h d", d=HD)
                            for f in range(2):
                                ins = nc.vector.tensor_scalar(feat[:, t, 1, br, :, f * HD:(f + 1) * HD], src,
                                                              angle[:, t, f:f + 1], None, ALU.mult)
                    ins.then_inc(featured.sem, 1)

                def move_kv(n):
                    dve.wait_ge(kv_done.sem, kv_done.at(n + 1))
                    for br in range(BR):
                        for hh in range(4):
                            r = slice(hh * F, (hh + 1) * F)
                            src = ps[r, KV_BANK + br, 0:NG * 4 * VC].rearrange("p (g h c) -> p g h c", g=NG, c=VC)[:, :, hh, :]
                            ins = nc.vector.tensor_copy(kv[r, br * NG:(br + 1) * NG, hh, :], src)
                    ins.then_inc(kv_moved.sem, 1)

                def divide(n):
                    dve.wait_ge(attended.sem, attended.at(n + 1))
                    for br in range(BR):
                        for t in range(TB):
                            res = ps[:, RES_BANK[br][t], 0:H * VC].rearrange("p (h c) -> p h c", c=VC)
                            ins = nc.vector.tensor_scalar(z[:, br, t, :], res[:, :, HD], 1e-6, None, ALU.max)
                    link(ins)
                    link(nc.vector.reciprocal(z[:], z[:]))
                    for br in range(BR):
                        for t in range(TB):
                            res = ps[:, RES_BANK[br][t], 0:H * VC].rearrange("p (h c) -> p h c", c=VC)
                            ins = nc.vector.tensor_tensor(part[:, br, t, :].rearrange("p (h d) -> p h d", d=HD),
                                                          res[:, :, 0:HD],
                                                          z[:, br, t, :].rearrange("p (h o) -> p h o", o=1).to_broadcast([P, H, HD]),
                                                          ALU.mult)
                    link(ins)
                    nc.vector.tensor_tensor(y[:], part[:, 0], part[:, 1], ALU.add).then_inc(summed.sem, 1)

                def add_output(n):
                    dve.wait_ge(out_done.sem, out_done.at(n + 1))
                    for m in range(KT):
                        ins = nc.vector.scalar_tensor_tensor(out=x[:, m, n, :], in0=ps[:, OUT_BANK, m * S:(m + 1) * S],
                                                             scalar=bo[:, m:m + 1], in1=x[:, m, n, :],
                                                             op0=ALU.add, op1=ALU.add)
                    ins.then_inc(added.sem, 1)

                def body(i, first, last):
                    chain.restart(dve)
                    for j in range(2):
                        n = i * 2 + j
                        more = not (last and j == 1)
                        if more:
                            dve.wait_ge(featured.sem, featured.at(n + 1))
                            dve.wait_ge(q_featured.sem, q_featured.at(n + 1))
                            take_projections(n + 1, 1 - j)
                        if not (first and j == 0):
                            add_output(n - 1)
                        move_kv(n)
                        if more:
                            softmax(n + 1)
                        dve.wait_ge(added.sem, added.at(n))
                        divide(n)
                        if more:
                            k_features(n + 1)

                dve.sem_inc(added.sem, added.credit)
                dve.sem_inc(biased.sem, biased.credit)
                link(nc.vector.memset(kv[:], 0.0))
                link(nc.vector.memset(v[:], 1.0))
                take_projections(0, 0)
                softmax(0)
                k_features(0)
                batches(dve, body)
                add_output(B - 1)


def memory_filter(core, name, w):
    nc = core.nc
    ps = core.psum
    PAD = TAPS - 1
    PE_TAPS = 16
    DVE_TAPS = TAPS - PE_TAPS
    with Stage(core, name) as st:
        w1, w2 = st.buf("w1", [P, KT, D]), st.buf("w2", [P, KT, D])
        b1, b2 = st.buf("b1", [P, KT]), st.buf("b2", [P, KT])
        taps = st.buf("taps", [P, KT, TAPS + 1])
        tap_diff = st.buf("tap_diff", [P, KT, TAPS])
        p = st.buf("projected", [P, KT, B, PAD + S])
        acc = st.buf("filtered", [P, KT, B, S])
        total = st.buf("total", [P, KT, B])
        diagonal = st.buf("diagonal", [P, KT, PE_TAPS, P])
        diff_done, diagonals, padded = st.count("diff_done"), st.count("diagonals"), st.count("padded")
        proj_done, moved, filtered = st.count("proj_done"), st.count("moved"), st.count("filtered")
        pe_filtered = st.count("pe_filtered")
        out_done, chain = st.count("out_done"), st.chain("chain")
        x = core.x
        loads = [(w1[:], w["W1"].rearrange("(k p) n -> p k n", p=P)), (w2[:], w["W2"].rearrange("(k p) n -> p k n", p=P)),
                 (b1[:], w["bias1"]), (b2[:], w["bias2"]), (taps[:], w["taps"])]
        layernorm(core, name + "_ln", core.x, core.xn, preload=loads)

        def filter_bank(m, c):
            return (4 if m == 0 else 0) + c

        with nc.Block() as block:

            @block.gpsimd
            def _(pool):
                pool.wait_ge(diff_done.sem, diff_done.at(1))
                for m in range(KT):
                    nc.gpsimd.tensor_tensor(diagonal[:, m], core.ident[:].rearrange("p (o c) -> p o c", o=1).to_broadcast([P, PE_TAPS, P]),
                                            tap_diff[:, m, DVE_TAPS:].rearrange("p (t o) -> p t o", o=1).to_broadcast([P, PE_TAPS, P]),
                                            ALU.mult).then_inc(diagonals.sem, 1)

            @block.tensor
            def _(pe):
                for m in range(KT):
                    for c in range(NCH):
                        n = m * NCH + c
                        if n >= 4:
                            pe.wait_ge(moved.sem, moved.at(n + 1 - 4))
                        for k in range(KT):
                            mm = nc.tensor.matmul(ps[:, n % 4, :], w1[:, k, m * P:(m + 1) * P], core.xn[:, k, c * CH:(c + 1) * CH],
                                                  start=(k == 0), stop=(k == KT - 1))
                        mm.then_inc(proj_done.sem, 1)
                pe.wait_ge(padded.sem, padded.at(KT))
                for m in range(KT):
                    pe.wait_ge(diagonals.sem, diagonals.at(m + 1))
                    pe.wait_ge(moved.sem, moved.at((m + 1) * NCH))
                    for t in range(PE_TAPS):
                        start = PAD - DVE_TAPS - t
                        for c in range(NCH):
                            mm = nc.tensor.matmul(ps[:, filter_bank(m, c), :], diagonal[:, m, t, :],
                                                  p[:, m, c * CH // S:(c + 1) * CH // S, start:start + S],
                                                  start=(t == 0), stop=(t == PE_TAPS - 1))
                    mm.then_inc(pe_filtered.sem, 1)
                for c in range(NCH):
                    pe.wait_ge(filtered.sem, filtered.at(c + 1))
                    for m in range(KT):
                        for k in range(KT):
                            mm = nc.tensor.matmul(ps[:, filter_bank(m, c), :], w2[:, k, m * P:(m + 1) * P],
                                                  acc[:, k].rearrange("p b s -> p (b s)")[:, c * CH:(c + 1) * CH],
                                                  start=(k == 0), stop=(k == KT - 1))
                        mm.then_inc(out_done.sem, 1)

            @block.scalar
            def _(act):
                for m in range(KT):
                    for c in range(NCH):
                        n = m * NCH + c
                        act.wait_ge(proj_done.sem, proj_done.at(n + 1))
                        bs = slice(c * CH // S, (c + 1) * CH // S)
                        nc.scalar.activation(p[:, m, bs, PAD:], ps[:, n % 4, :].rearrange("p (b s) -> p b s", s=S),
                                             ACT.Identity, bias=b1[:, m:m + 1]).then_inc(moved.sem, 1)

            @block.vector
            def _(dve):
                for m in range(KT):
                    nc.vector.memset(p[:, m, :, 0:PAD], 0.0).then_inc(padded.sem, 1)
                dve.wait_ge(padded.sem, padded.at(KT))
                for m in range(KT):
                    ins = nc.vector.tensor_scalar(tap_diff[:, m, :], taps[:, m, 1:], taps[:, m, 0:1], None, ALU.subtract)
                ins.then_inc(diff_done.sem, 1)
                dve.wait_ge(diff_done.sem, diff_done.at(1))
                for m in range(KT):
                    dve.wait_ge(moved.sem, moved.at((m + 1) * NCH))
                    chain.link(dve, nc.vector.tensor_reduce(total[:, m, :], p[:, m, :, PAD:], AX.X, ALU.add))
                    chain.link(dve, nc.vector.tensor_scalar(total[:, m, :], total[:, m, :], taps[:, m, 0:1], None, ALU.mult))
                    chain.link(dve, nc.vector.scalar_tensor_tensor(
                        out=acc[:, m], in0=p[:, m, :, PAD:], scalar=tap_diff[:, m, 0:1],
                        in1=total[:, m, :].rearrange("p (b o) -> p b o", o=1).to_broadcast([P, B, S]),
                        op0=ALU.mult, op1=ALU.add))
                    for tap in range(1, DVE_TAPS):
                        chain.link(dve, nc.vector.scalar_tensor_tensor(
                            out=acc[:, m], in0=p[:, m, :, PAD - tap:PAD - tap + S], scalar=tap_diff[:, m, tap:tap + 1],
                            in1=acc[:, m], op0=ALU.mult, op1=ALU.add))
                dve.wait_ge(pe_filtered.sem, pe_filtered.at(KT))
                for c in range(NCH):
                    for m in range(KT):
                        part = acc[:, m].rearrange("p b s -> p (b s)")[:, c * CH:(c + 1) * CH]
                        ins = nc.vector.tensor_tensor(part, part, ps[:, filter_bank(m, c), :], ALU.add)
                    ins.then_inc(filtered.sem, 1)
                for c in range(NCH):
                    for m in range(KT):
                        dve.wait_ge(out_done.sem, out_done.at(c * KT + m + 1))
                        dst = x[:, m, c * CH:(c + 1) * CH]
                        nc.vector.scalar_tensor_tensor(out=dst, in0=ps[:, filter_bank(m, c), :], scalar=b2[:, m:m + 1], in1=dst,
                                                       op0=ALU.add, op1=ALU.add)


def stage_L1_attn(core, name, w, a):
    linear_attention(core, name, w)


def stage_L2_attn(core, name, w, a):
    memory_filter(core, name, w)


def lay_out_others(a, n):
    for c in "qkvo":
        a[f"L1_attn_W{c}"] = n[f"L1_attn_W{c}"]
    for c in "qkv":
        a[f"L1_attn_b{c}"] = n[f"L1_attn_b{c}"]
    a["L1_attn_bo"] = by_partition(n["L1_attn_bo"])
    index = np.float32(np.pi / 2) * np.arange(1, S + 1, dtype=np.float32) / np.float32(S)
    a["L1_attn_sin_cos"] = np.stack([np.sin(index), np.cos(index)], -1).astype(np.float32).reshape(TB, P, 2).transpose(1, 0, 2)
    p = "L2_attn_"
    a[p + "W1"], a[p + "W2"] = n[p + "W1"], n[p + "W2"]
    a[p + "bias1"], a[p + "bias2"] = by_partition(n[p + "bias1"]), by_partition(n[p + "bias2"])
    a[p + "taps"] = n[p + "memory_weights"].T.reshape(KT, P, TAPS + 1).transpose(1, 0, 2)


STAGES = ["L0_attn", "L0_xattn", "L0_ffn", "L1_attn", "L1_xattn", "L1_ffn",
          "L2_attn", "L2_xattn", "L2_ffn", "L3_attn", "L3_xattn", "L3_ffn"]


def build(nc, a, out, stages=STAGES):
    with ExitStack() as stack:
        core = Core(nc, stack)
        load_inputs(core, a)
        for name in stages:
            w = {k[len(name) + 1:]: v for k, v in a.items() if k.startswith(name + "_")}
            STAGE[name](core, name, w, a)
        store_output(core, out)


def stage_L0_attn(core, name, w, a):
    layernorm(core, name + "_ln", core.x, core.xn)
    relative_attention(core, name, w)


def stage_L0_xattn(core, name, w, a):
    attention(core, name, w, kv="ctx")


def stage_L1_xattn(core, name, w, a):
    attention(core, name, w, kv="ctx", mask=a["mask_1x1xSxS2_if1"])


def stage_L2_xattn(core, name, w, a):
    attention(core, name, w, kv="ctx", project=False)


def stage_L3_attn(core, name, w, a):
    attention(core, name, w)


STAGE = {
    "L0_attn": stage_L0_attn, "L0_xattn": stage_L0_xattn,
    "L1_xattn": stage_L1_xattn, "L2_xattn": stage_L2_xattn,
    "L3_attn": stage_L3_attn, "L3_xattn": stage_L0_xattn,
    "L1_attn": stage_L1_attn, "L2_attn": stage_L2_attn,
    "L0_ffn": stage_L0_ffn, "L1_ffn": stage_L1_ffn, "L2_ffn": stage_L2_ffn, "L3_ffn": stage_L3_ffn,
}


def by_partition(v):
    return np.ascontiguousarray(v.reshape(-1, P).T)


def lay_out(x):
    a = {}
    n = {k: np.asarray(v) for k, v in x.items()}
    a["xT"] = n["x"].reshape(T, D).T
    a["ctxT"] = n["ctx_1024"].reshape(B * SC, D).T
    a["identity"] = np.eye(P, dtype=np.float32)
    own = np.arange(P)[:, None] // HD == np.arange(HB)
    a["key_scale"] = np.where(own, float(HD) ** -0.5, 0.0).astype(np.float32)
    a["earlier"] = np.tril(np.ones((E, E), np.float32), -1)
    a["mask_1x1xSxS2_if1"] = n["mask_1x1xSxS2_if1"]
    qkv = n["L0_attn_w_attn"]
    names = {
        "L0_attn": (qkv[:, :D], qkv[:, D:2 * D], qkv[:, 2 * D:], n["L0_attn_w_proj"], None),
        "L0_xattn": tuple(n[f"L0_xattn_w_{c}"].T for c in "qkvo") + (None,),
        "L1_xattn": tuple(n[f"L1_xattn_W_{c}"].T for c in "qkvo") + (None,),
        "L2_xattn": tuple(n[f"L2_xattn_W{c}"].T for c in "qkv") + (None, "L2_xattn_b"),
        "L3_attn": tuple(n[f"L3_attn_W{c}"] for c in "qkvo") + ("L3_attn_b",),
        "L3_xattn": tuple(n[f"L3_xattn_w{c}"].T for c in "qkvo") + ("L3_xattn_b",),
    }
    for name, (wq, wk, wv, wo, biases) in names.items():
        a[f"{name}_wq"], a[f"{name}_wk"], a[f"{name}_wv"] = wq, wk, wv
        if wo is not None:
            a[f"{name}_wo"] = wo
        if biases:
            a[f"{name}_bq"] = by_partition(n[f"{biases}q"])
            a[f"{name}_bk"] = by_partition(n[f"{biases}k"])
            a[f"{name}_bv"] = by_partition(n[f"{biases}v"])
            if wo is not None:
                a[f"{name}_bo"] = by_partition(n[f"{biases}o"])
    t, s = np.arange(P)[:, None], np.arange(S)[None, :]
    mask = np.concatenate([np.where(s[:, :P] <= t, 0.0, NEG), np.where(s <= t + P, 0.0, NEG)], 1)
    a["L0_attn_causal"] = mask.astype(np.float32)
    slopes = np.array([0.5 ** ((i + 1) * 8 / H) for i in range(H)])
    keys = np.concatenate([np.arange(P), np.arange(S)])
    alibi = -slopes[:, None] * (S - 1 - keys)[None, :]
    a["L3_attn_bias"] = (alibi[None] + mask[:, None, :]).astype(np.float32)
    embkT = n["L0_attn_embk"][::-1].T
    a["L0_attn_embkT"] = np.stack([np.pad(embkT, ((h * HD, P - (h + 1) * HD), (0, 0))) for h in range(HB)], 1)
    embv = n["L0_attn_embv"][::-1].reshape(TB, P, HD).transpose(1, 0, 2)
    a["L0_attn_embv"] = np.stack([np.pad(embv, ((0, 0), (0, 0), (h * HD, P - (h + 1) * HD))) for h in range(HB)], 2)
    lay_out_mixtures(a, n)
    lay_out_others(a, n)
    return {k: np.ascontiguousarray(v) for k, v in a.items()}


def kernel(**inputs):
    import concourse.bacc as _bacc
    from concourse.bass_utils import run_bass_kernel_spmd as _run

    nc = _bacc.Bacc("TRN2", target_bir_lowering=False, num_devices=1)
    arrays = lay_out(inputs)
    args = {k: nc.dram_tensor(f"in_{k}", v.shape, mybir.dt.from_np(v.dtype), kind="ExternalInput").ap()
            for k, v in arrays.items()}
    out = nc.dram_tensor("out_xT", (D, T), F32, kind="ExternalOutput").ap()
    build(nc, args, out)
    r = _run(nc, [{f"in_{k}": v for k, v in arrays.items()}], core_ids=[0])
    got = r.results[0]["out_xT"]
    return np.ascontiguousarray(got.T).reshape(B, S, D)
```
